# Optimizing a Trainium2 kernel written in Bass

```python
import numpy as np
import jax
import jax.numpy as jnp

def _softmax(x, axis=-1):
    return jax.nn.softmax(x, axis=axis)

def _gelu(x):
    return jax.nn.gelu(x, approximate=True)

def _silu(x):
    return jax.nn.silu(x)

def _sigmoid(x):
    return jax.nn.sigmoid(x)

def _layernorm(x, axis=-1, eps=1e-05):
    m = jnp.mean(x, axis=axis, keepdims=True)
    v = jnp.var(x, axis=axis, keepdims=True)
    return (x - m) / jnp.sqrt(v + eps)

def _scatter_add(tgt, idx, src, axis=0):
    return tgt.at[idx].add(src)

def _segment_sum(src, seg, n):
    return jax.ops.segment_sum(src, seg, n)
kernel_name = 'mk_conv_seq_d4_conv_nchw256_r2_f13dc5'

def setup_inputs(seed: int=0):
    np.random.seed(seed)
    _w = jnp.asarray

    def _rec_inputs():
        import jax
        import jax.numpy as jnp
        _gk = jax.random.key(seed)
        x = 7.22e-05 + 1 * jax.random.normal(jax.random.fold_in(_gk, 1), (8, 128, 32, 32), jnp.float32)
        return x
    x = _rec_inputs()

    def _L0_conv_setup():
        import jax, jax.numpy as jnp
        import numpy as np
        B, C, CK, CV, W, H = (8, 128, 128, 128, 32, 32)
        EPS = 1e-06
        key = jax.random.key(seed)
        ks = jax.random.split(key, 13)

        def wmat(k, shape, fan_in):
            return jax.random.normal(k, shape, jnp.float32) / np.float32(np.sqrt(fan_in))
        return {'x': jax.random.normal(ks[0], (B, C, W, H), jnp.float32), 'qw': wmat(ks[1], (CK, C), C), 'qb': jnp.zeros((CK,), jnp.float32), 'kw': wmat(ks[2], (CK, C), C), 'kb': jnp.zeros((CK,), jnp.float32), 'vw': wmat(ks[3], (CV, C), C), 'vb': jnp.zeros((CV,), jnp.float32), 'rw': wmat(ks[4], (C, CV), CV), 'rb': jnp.zeros((C,), jnp.float32), 'c1w': wmat(ks[5], (C, C, 3, 3), C * 9), 'c1b': jnp.zeros((C,), jnp.float32), 'c2w': wmat(ks[6], (C, C, 3, 3), C * 9), 'c2b': jnp.zeros((C,), jnp.float32)}
    _L0_conv_all = _L0_conv_setup()
    _L0_conv_in = {k: v for k, v in _L0_conv_all.items() if k in ('qw', 'qb', 'kw', 'kb', 'vw', 'vb', 'rw', 'rb', 'c1w', 'c1b', 'c2w', 'c2b')}
    del _L0_conv_all

    def _L1_conv_setup():
        import jax, jax.numpy as jnp
        import numpy as np
        from jax import lax
        DN = ('NCHW', 'OIHW', 'NCHW')

        def dsconv(x, dw_w, dw_b, pw_w, pw_b, dilation):
            C = x.shape[1]
            y = lax.conv_general_dilated(x, dw_w, window_strides=(1, 1), padding=[(dilation, dilation), (dilation, dilation)], rhs_dilation=(dilation, dilation), dimension_numbers=DN, feature_group_count=C)
            y = y + dw_b[None, :, None, None]
            y = lax.conv_general_dilated(y, pw_w, window_strides=(1, 1), padding='VALID', dimension_numbers=DN)
            return y + pw_b[None, :, None, None]
        key = jax.random.key(seed)
        ks = jax.random.split(key, 16)
        B, C, H, W = (4, 128, 32, 32)
        R = C // 8
        s = 0.05
        inp = {'x': jax.random.normal(ks[0], (B, C, H, W), dtype=jnp.float32), 'c1_dw_w': jax.random.normal(ks[1], (C, 1, 3, 3), dtype=jnp.float32) * s, 'c1_dw_b': jax.random.normal(ks[2], (C,), dtype=jnp.float32) * s, 'c1_pw_w': jax.random.normal(ks[3], (R, C, 1, 1), dtype=jnp.float32) * s, 'c1_pw_b': jax.random.normal(ks[4], (R,), dtype=jnp.float32) * s, 'c2_dw_w': jax.random.normal(ks[5], (C, 1, 3, 3), dtype=jnp.float32) * s, 'c2_dw_b': jax.random.normal(ks[6], (C,), dtype=jnp.float32) * s, 'c2_pw_w': jax.random.normal(ks[7], (R, C, 1, 1), dtype=jnp.float32) * s, 'c2_pw_b': jax.random.normal(ks[8], (R,), dtype=jnp.float32) * s, 'c3_dw_w': jax.random.normal(ks[9], (C, 1, 3, 3), dtype=jnp.float32) * s, 'c3_dw_b': jax.random.normal(ks[10], (C,), dtype=jnp.float32) * s, 'c3_pw_w': jax.random.normal(ks[11], (R, C, 1, 1), dtype=jnp.float32) * s, 'c3_pw_b': jax.random.normal(ks[12], (R,), dtype=jnp.float32) * s, 'co_w': jax.random.normal(ks[13], (C, R, 1, 1), dtype=jnp.float32) * s, 'co_b': jax.random.normal(ks[14], (C,), dtype=jnp.float32) * s}
        return inp
    _L1_conv_all = _L1_conv_setup()
    _L1_conv_in = {k: v for k, v in _L1_conv_all.items() if k in ('c1_dw_w', 'c1_dw_b', 'c1_pw_w', 'c1_pw_b', 'c2_dw_w', 'c2_dw_b', 'c2_pw_w', 'c2_pw_b', 'c3_dw_w', 'c3_dw_b', 'c3_pw_w', 'c3_pw_b', 'co_w', 'co_b')}
    del _L1_conv_all

    def _L2_conv_setup():
        import jax, jax.numpy as jnp
        from jax import lax
        import numpy as np
        DIM = 128
        INNER = 64
        DS = 2
        K = 3
        EPS = 1e-05

        def _sss(seq, wd, bd, wv, bv):
            delta = jax.nn.sigmoid(jnp.einsum('nlc,dc->nld', seq, wd) + bd)
            value = jnp.einsum('nlc,dc->nld', seq, wv) + bv
            init = jnp.zeros((seq.shape[0], seq.shape[2]), seq.dtype)

            def step(state, dv):
                d, v = dv
                s = (1.0 - d) * state + d * v
                return (s, s)
            _, ys = lax.scan(step, init, (jnp.moveaxis(delta, 1, 0), jnp.moveaxis(value, 1, 0)))
            return jnp.moveaxis(ys, 0, 1)

        def _bidir(seq, wd, bd, wv, bv):
            fwd = _sss(seq, wd, bd, wv, bv)
            bwd = jnp.flip(_sss(jnp.flip(seq, axis=1), wd, bd, wv, bv), axis=1)
            return 0.5 * (fwd + bwd)
        key = jax.random.key(seed)
        ks = jax.random.split(key, 16)
        s = lambda *sh: 0.05
        inp = {'x': jax.random.normal(ks[0], (4, DIM, 100, 100), jnp.float32), 'gn_w': jnp.ones((DIM,), jnp.float32), 'gn_b': jnp.zeros((DIM,), jnp.float32), 'w_in': jax.random.normal(ks[1], (2 * INNER, DIM), jnp.float32) * 0.05, 'w_dw': jax.random.normal(ks[2], (INNER, 1, K, K), jnp.float32) * 0.1, 'row_wd': jax.random.normal(ks[3], (INNER, INNER), jnp.float32) * 0.05, 'row_bd': jax.random.normal(ks[4], (INNER,), jnp.float32) * 0.05, 'row_wv': jax.random.normal(ks[5], (INNER, INNER), jnp.float32) * 0.05, 'row_bv': jax.random.normal(ks[6], (INNER,), jnp.float32) * 0.05, 'col_wd': jax.random.normal(ks[7], (INNER, INNER), jnp.float32) * 0.05, 'col_bd': jax.random.normal(ks[8], (INNER,), jnp.float32) * 0.05, 'col_wv': jax.random.normal(ks[9], (INNER, INNER), jnp.float32) * 0.05, 'col_bv': jax.random.normal(ks[10], (INNER,), jnp.float32) * 0.05, 'w_out': jax.random.normal(ks[11], (DIM, INNER), jnp.float32) * 0.05}
        return inp
    _L2_conv_all = _L2_conv_setup()
    _L2_conv_in = {k: v for k, v in _L2_conv_all.items() if k in ('gn_w', 'gn_b', 'w_in', 'w_dw', 'row_wd', 'row_bd', 'row_wv', 'row_bv', 'col_wd', 'col_bd', 'col_wv', 'col_bv', 'w_out')}
    del _L2_conv_all

    def _L3_conv_setup():
        import jax, jax.numpy as jnp
        import numpy as np
        EPS = 1e-05

        def _bn(x, g, b, m, v):
            s = g / jnp.sqrt(v + EPS)
            return x * s[None, :, None, None] + (b - m * s)[None, :, None, None]

        def _conv1x1(x, w):
            return jnp.einsum('bchw,oc->bohw', x, w)

        def _bilinear(img, y, x):
            B, C, Hi, Wi = img.shape
            y0 = jnp.floor(y)
            x0 = jnp.floor(x)
            wy1 = y - y0
            wx1 = x - x0
            wy0 = 1.0 - wy1
            wx0 = 1.0 - wx1
            imgf = img.reshape(B, C, Hi * Wi)

            def gather(yi, xi):
                valid = (yi >= 0) & (yi < Hi) & (xi >= 0) & (xi < Wi)
                yc = jnp.clip(yi, 0, Hi - 1).astype(jnp.int32)
                xc = jnp.clip(xi, 0, Wi - 1).astype(jnp.int32)
                flat = yc * Wi + xc

                def per_b(imgb, flatb):
                    return imgb[:, flatb.reshape(-1)].reshape(C, *flatb.shape)
                out = jax.vmap(per_b)(imgf, flat)
                return out * valid[:, None].astype(img.dtype)
            return gather(y0, x0) * (wy0 * wx0)[:, None] + gather(y0, x0 + 1) * (wy0 * wx1)[:, None] + gather(y0 + 1, x0) * (wy1 * wx0)[:, None] + gather(y0 + 1, x0 + 1) * (wy1 * wx1)[:, None]

        def _dcn(h, woff, boff, w2, b2):
            B, C, H, W = h.shape
            off = jax.lax.conv_general_dilated(h, woff, (1, 1), [(1, 1), (1, 1)], dimension_numbers=('NCHW', 'OIHW', 'NCHW')) + boff[None, :, None, None]
            o = off[:, :18].reshape(B, 9, 2, H, W)
            mask = jax.nn.sigmoid(off[:, 18:])
            ky, kx = jnp.meshgrid(jnp.arange(3), jnp.arange(3), indexing='ij')
            base_y = (jnp.arange(H)[None, :, None] - 1 + ky.reshape(9)[:, None, None]).astype(h.dtype)
            base_x = (jnp.arange(W)[None, None, :] - 1 + kx.reshape(9)[:, None, None]).astype(h.dtype)
            y = o[:, :, 0] + base_y[None]
            x = o[:, :, 1] + base_x[None]
            samp = _bilinear(h, y, x) * mask[:, None]
            out = jnp.einsum('bckhw,ock->bohw', samp, w2.reshape(w2.shape[0], w2.shape[1], 9))
            return out + b2[None, :, None, None]
        key = jax.random.key(seed)
        ks = jax.random.split(key, 20)
        B, Cin, Cb, H, W = (4, 128, 32, 56, 56)
        d = {'x': jax.random.normal(ks[0], (B, Cin, H, W), jnp.float32), 'w1': jax.random.normal(ks[1], (Cb, Cin), jnp.float32) * 0.05, 'bn1_g': jax.random.uniform(ks[2], (Cb,), jnp.float32, 0.5, 1.5), 'bn1_b': jax.random.normal(ks[3], (Cb,), jnp.float32) * 0.1, 'bn1_m': jax.random.normal(ks[4], (Cb,), jnp.float32) * 0.1, 'bn1_v': jax.random.uniform(ks[5], (Cb,), jnp.float32, 0.5, 1.5), 'woff': jax.random.normal(ks[6], (27, Cb, 3, 3), jnp.float32) * 0.01, 'boff': jax.random.normal(ks[7], (27,), jnp.float32) * 0.1, 'w2': jax.random.normal(ks[8], (Cb, Cb, 3, 3), jnp.float32) * 0.05, 'dcn_b': jax.random.normal(ks[9], (Cb,), jnp.float32) * 0.1, 'bn2_g': jax.random.uniform(ks[10], (Cb,), jnp.float32, 0.5, 1.5), 'bn2_b': jax.random.normal(ks[11], (Cb,), jnp.float32) * 0.1, 'bn2_m': jax.random.normal(ks[12], (Cb,), jnp.float32) * 0.1, 'bn2_v': jax.random.uniform(ks[13], (Cb,), jnp.float32, 0.5, 1.5), 'w3': jax.random.normal(ks[14], (Cin, Cb), jnp.float32) * 0.05, 'bn3_g': jax.random.uniform(ks[15], (Cin,), jnp.float32, 0.5, 1.5), 'bn3_b': jax.random.normal(ks[16], (Cin,), jnp.float32) * 0.1, 'bn3_m': jax.random.normal(ks[17], (Cin,), jnp.float32) * 0.1, 'bn3_v': jax.random.uniform(ks[18], (Cin,), jnp.float32, 0.5, 1.5)}
        return d
    _L3_conv_all = _L3_conv_setup()
    _L3_conv_in = {k: v for k, v in _L3_conv_all.items() if k in ('w1', 'bn1_g', 'bn1_b', 'bn1_m', 'bn1_v', 'woff', 'boff', 'w2', 'dcn_b', 'bn2_g', 'bn2_b', 'bn2_m', 'bn2_v', 'w3', 'bn3_g', 'bn3_b', 'bn3_m', 'bn3_v')}
    del _L3_conv_all
    return {'x': x, 'L0_conv_qw': _L0_conv_in['qw'], 'L0_conv_qb': _L0_conv_in['qb'], 'L0_conv_kw': _L0_conv_in['kw'], 'L0_conv_kb': _L0_conv_in['kb'], 'L0_conv_vw': _L0_conv_in['vw'], 'L0_conv_vb': _L0_conv_in['vb'], 'L0_conv_rw': _L0_conv_in['rw'], 'L0_conv_rb': _L0_conv_in['rb'], 'L0_conv_c1w': _L0_conv_in['c1w'], 'L0_conv_c1b': _L0_conv_in['c1b'], 'L0_conv_c2w': _L0_conv_in['c2w'], 'L0_conv_c2b': _L0_conv_in['c2b'], 'L1_conv_c1_dw_w': _L1_conv_in['c1_dw_w'], 'L1_conv_c1_dw_b': _L1_conv_in['c1_dw_b'], 'L1_conv_c1_pw_w': _L1_conv_in['c1_pw_w'], 'L1_conv_c1_pw_b': _L1_conv_in['c1_pw_b'], 'L1_conv_c2_dw_w': _L1_conv_in['c2_dw_w'], 'L1_conv_c2_dw_b': _L1_conv_in['c2_dw_b'], 'L1_conv_c2_pw_w': _L1_conv_in['c2_pw_w'], 'L1_conv_c2_pw_b': _L1_conv_in['c2_pw_b'], 'L1_conv_c3_dw_w': _L1_conv_in['c3_dw_w'], 'L1_conv_c3_dw_b': _L1_conv_in['c3_dw_b'], 'L1_conv_c3_pw_w': _L1_conv_in['c3_pw_w'], 'L1_conv_c3_pw_b': _L1_conv_in['c3_pw_b'], 'L1_conv_co_w': _L1_conv_in['co_w'], 'L1_conv_co_b': _L1_conv_in['co_b'], 'L2_conv_gn_w': _L2_conv_in['gn_w'], 'L2_conv_gn_b': _L2_conv_in['gn_b'], 'L2_conv_w_in': _L2_conv_in['w_in'], 'L2_conv_w_dw': _L2_conv_in['w_dw'], 'L2_conv_row_wd': _L2_conv_in['row_wd'], 'L2_conv_row_bd': _L2_conv_in['row_bd'], 'L2_conv_row_wv': _L2_conv_in['row_wv'], 'L2_conv_row_bv': _L2_conv_in['row_bv'], 'L2_conv_col_wd': _L2_conv_in['col_wd'], 'L2_conv_col_bd': _L2_conv_in['col_bd'], 'L2_conv_col_wv': _L2_conv_in['col_wv'], 'L2_conv_col_bv': _L2_conv_in['col_bv'], 'L2_conv_w_out': _L2_conv_in['w_out'], 'L3_conv_w1': _L3_conv_in['w1'], 'L3_conv_bn1_g': _L3_conv_in['bn1_g'], 'L3_conv_bn1_b': _L3_conv_in['bn1_b'], 'L3_conv_bn1_m': _L3_conv_in['bn1_m'], 'L3_conv_bn1_v': _L3_conv_in['bn1_v'], 'L3_conv_woff': _L3_conv_in['woff'], 'L3_conv_boff': _L3_conv_in['boff'], 'L3_conv_w2': _L3_conv_in['w2'], 'L3_conv_dcn_b': _L3_conv_in['dcn_b'], 'L3_conv_bn2_g': _L3_conv_in['bn2_g'], 'L3_conv_bn2_b': _L3_conv_in['bn2_b'], 'L3_conv_bn2_m': _L3_conv_in['bn2_m'], 'L3_conv_bn2_v': _L3_conv_in['bn2_v'], 'L3_conv_w3': _L3_conv_in['w3'], 'L3_conv_bn3_g': _L3_conv_in['bn3_g'], 'L3_conv_bn3_b': _L3_conv_in['bn3_b'], 'L3_conv_bn3_m': _L3_conv_in['bn3_m'], 'L3_conv_bn3_v': _L3_conv_in['bn3_v']}

def reference(x, L0_conv_qw, L0_conv_qb, L0_conv_kw, L0_conv_kb, L0_conv_vw, L0_conv_vb, L0_conv_rw, L0_conv_rb, L0_conv_c1w, L0_conv_c1b, L0_conv_c2w, L0_conv_c2b, L1_conv_c1_dw_w, L1_conv_c1_dw_b, L1_conv_c1_pw_w, L1_conv_c1_pw_b, L1_conv_c2_dw_w, L1_conv_c2_dw_b, L1_conv_c2_pw_w, L1_conv_c2_pw_b, L1_conv_c3_dw_w, L1_conv_c3_dw_b, L1_conv_c3_pw_w, L1_conv_c3_pw_b, L1_conv_co_w, L1_conv_co_b, L2_conv_gn_w, L2_conv_gn_b, L2_conv_w_in, L2_conv_w_dw, L2_conv_row_wd, L2_conv_row_bd, L2_conv_row_wv, L2_conv_row_bv, L2_conv_col_wd, L2_conv_col_bd, L2_conv_col_wv, L2_conv_col_bv, L2_conv_w_out, L3_conv_w1, L3_conv_bn1_g, L3_conv_bn1_b, L3_conv_bn1_m, L3_conv_bn1_v, L3_conv_woff, L3_conv_boff, L3_conv_w2, L3_conv_dcn_b, L3_conv_bn2_g, L3_conv_bn2_b, L3_conv_bn2_m, L3_conv_bn2_v, L3_conv_w3, L3_conv_bn3_g, L3_conv_bn3_b, L3_conv_bn3_m, L3_conv_bn3_v):
    import jax
    import jax.numpy as jnp

    def _L0_conv_ref(x, qw, qb, kw, kb, vw, vb, rw, rb, c1w, c1b, c2w, c2b):
        import jax, jax.numpy as jnp
        import numpy as np
        B, C, CK, CV, W, H = (8, 128, 128, 128, 32, 32)
        EPS = 1e-06
        Bz, Cc, Wd, Hd = x.shape
        n = Wd * Hd
        xf = x.reshape(Bz, Cc, n)
        Q = jnp.einsum('oc,bcn->bon', qw, xf) + qb[None, :, None]
        K = jnp.einsum('oc,bcn->bon', kw, xf) + kb[None, :, None]
        V = jnp.einsum('oc,bcn->bon', vw, xf) + vb[None, :, None]
        Qn = Q / jnp.linalg.norm(Q, axis=1, keepdims=True)
        Kn = K / jnp.linalg.norm(K, axis=1, keepdims=True)
        Qt = jnp.transpose(Qn, (0, 2, 1))
        agg_dom = jnp.einsum('bnk,bk->bn', Qt, Kn.sum(-1))
        denom = 1.0 / (n + agg_dom + EPS)
        vsum = V.sum(-1)
        kv = jnp.einsum('bkn,bcn->bkc', Kn, V)
        qkv = jnp.einsum('bnk,bkc->bcn', Qt, kv)
        wv = (vsum[:, :, None] + qkv) * denom[:, None, :]
        wv = wv.reshape(Bz, -1, Hd, Wd)
        attn = jnp.einsum('oc,bchw->bohw', rw, wv) + rb[None, :, None, None]
        dn = ('NCHW', 'OIHW', 'NCHW')
        h = jax.lax.conv_general_dilated(attn, c1w, (1, 1), 'SAME', dimension_numbers=dn) + c1b[None, :, None, None]
        h = jax.lax.conv_general_dilated(h, c2w, (1, 1), 'SAME', dimension_numbers=dn) + c2b[None, :, None, None]
        return h * x + x

    def _L1_conv_ref(x, c1_dw_w, c1_dw_b, c1_pw_w, c1_pw_b, c2_dw_w, c2_dw_b, c2_pw_w, c2_pw_b, c3_dw_w, c3_dw_b, c3_pw_w, c3_pw_b, co_w, co_b):
        import jax, jax.numpy as jnp
        import numpy as np
        from jax import lax
        DN = ('NCHW', 'OIHW', 'NCHW')

        def dsconv(x, dw_w, dw_b, pw_w, pw_b, dilation):
            C = x.shape[1]
            y = lax.conv_general_dilated(x, dw_w, window_strides=(1, 1), padding=[(dilation, dilation), (dilation, dilation)], rhs_dilation=(dilation, dilation), dimension_numbers=DN, feature_group_count=C)
            y = y + dw_b[None, :, None, None]
            y = lax.conv_general_dilated(y, pw_w, window_strides=(1, 1), padding='VALID', dimension_numbers=DN)
            return y + pw_b[None, :, None, None]
        B, C, H, W = x.shape
        R = C // 8
        N = H * W
        Fp1 = dsconv(x, c1_dw_w, c1_dw_b, c1_pw_w, c1_pw_b, 1).reshape(B, R, N)
        Fp2 = dsconv(x, c2_dw_w, c2_dw_b, c2_pw_w, c2_pw_b, 3).reshape(B, R, N)
        Fp3 = dsconv(x, c3_dw_w, c3_dw_b, c3_pw_w, c3_pw_b, 5).reshape(B, R, N)
        Mpam = jax.nn.softmax(jnp.einsum('bci,bcj->bij', Fp2, Fp3), axis=-1)
        Fpmap = jnp.einsum('bcj,bij->bci', Fp1, Mpam).reshape(B, R, H, W)
        Fpmap = lax.conv_general_dilated(Fpmap, co_w, (1, 1), 'VALID', dimension_numbers=DN) + co_b[None, :, None, None]
        return x + Fpmap

    def _L2_conv_ref(x, gn_w, gn_b, w_in, w_dw, row_wd, row_bd, row_wv, row_bv, col_wd, col_bd, col_wv, col_bv, w_out):
        import jax, jax.numpy as jnp
        from jax import lax
        import numpy as np
        DIM = 128
        INNER = 64
        DS = 2
        K = 3
        EPS = 1e-05

        def _sss(seq, wd, bd, wv, bv):
            delta = jax.nn.sigmoid(jnp.einsum('nlc,dc->nld', seq, wd) + bd)
            value = jnp.einsum('nlc,dc->nld', seq, wv) + bv
            init = jnp.zeros((seq.shape[0], seq.shape[2]), seq.dtype)

            def step(state, dv):
                d, v = dv
                s = (1.0 - d) * state + d * v
                return (s, s)
            _, ys = lax.scan(step, init, (jnp.moveaxis(delta, 1, 0), jnp.moveaxis(value, 1, 0)))
            return jnp.moveaxis(ys, 0, 1)

        def _bidir(seq, wd, bd, wv, bv):
            fwd = _sss(seq, wd, bd, wv, bv)
            bwd = jnp.flip(_sss(jnp.flip(seq, axis=1), wd, bd, wv, bv), axis=1)
            return 0.5 * (fwd + bwd)
        B, C, H, W = x.shape
        residual = x
        mu = jnp.mean(x, axis=(1, 2, 3), keepdims=True)
        var = jnp.var(x, axis=(1, 2, 3), keepdims=True)
        y = (x - mu) * lax.rsqrt(var + EPS)
        y = y * gn_w[None, :, None, None] + gn_b[None, :, None, None]
        h, w = (H // DS, W // DS)
        y = y.reshape(B, C, h, DS, w, DS).mean(axis=(3, 5))
        y = jnp.einsum('oc,bchw->bohw', w_in, y)
        y, gate = (y[:, :INNER], y[:, INNER:])
        y = lax.conv_general_dilated(y, w_dw, (1, 1), 'SAME', feature_group_count=INNER, dimension_numbers=('NCHW', 'OIHW', 'NCHW'))
        y = jax.nn.silu(y)
        seq_r = y.transpose(0, 2, 3, 1).reshape(B * h, w, INNER)
        rows = _bidir(seq_r, row_wd, row_bd, row_wv, row_bv)
        rows = rows.reshape(B, h, w, INNER).transpose(0, 3, 1, 2)
        seq_c = y.transpose(0, 3, 2, 1).reshape(B * w, h, INNER)
        cols = _bidir(seq_c, col_wd, col_bd, col_wv, col_bv)
        cols = cols.reshape(B, w, h, INNER).transpose(0, 3, 2, 1)
        y = 0.5 * (rows + cols)
        y = y * jax.nn.sigmoid(gate)
        y = jnp.einsum('oc,bchw->bohw', w_out, y)
        y = jax.image.resize(y, (B, C, H, W), method='bilinear')
        return residual + y

    def _L3_conv_ref(x, w1, bn1_g, bn1_b, bn1_m, bn1_v, woff, boff, w2, dcn_b, bn2_g, bn2_b, bn2_m, bn2_v, w3, bn3_g, bn3_b, bn3_m, bn3_v):
        import jax, jax.numpy as jnp
        import numpy as np
        EPS = 1e-05

        def _bn(x, g, b, m, v):
            s = g / jnp.sqrt(v + EPS)
            return x * s[None, :, None, None] + (b - m * s)[None, :, None, None]

        def _conv1x1(x, w):
            return jnp.einsum('bchw,oc->bohw', x, w)

        def _bilinear(img, y, x):
            B, C, Hi, Wi = img.shape
            y0 = jnp.floor(y)
            x0 = jnp.floor(x)
            wy1 = y - y0
            wx1 = x - x0
            wy0 = 1.0 - wy1
            wx0 = 1.0 - wx1
            imgf = img.reshape(B, C, Hi * Wi)

            def gather(yi, xi):
                valid = (yi >= 0) & (yi < Hi) & (xi >= 0) & (xi < Wi)
                yc = jnp.clip(yi, 0, Hi - 1).astype(jnp.int32)
                xc = jnp.clip(xi, 0, Wi - 1).astype(jnp.int32)
                flat = yc * Wi + xc

                def per_b(imgb, flatb):
                    return imgb[:, flatb.reshape(-1)].reshape(C, *flatb.shape)
                out = jax.vmap(per_b)(imgf, flat)
                return out * valid[:, None].astype(img.dtype)
            return gather(y0, x0) * (wy0 * wx0)[:, None] + gather(y0, x0 + 1) * (wy0 * wx1)[:, None] + gather(y0 + 1, x0) * (wy1 * wx0)[:, None] + gather(y0 + 1, x0 + 1) * (wy1 * wx1)[:, None]

        def _dcn(h, woff, boff, w2, b2):
            B, C, H, W = h.shape
            off = jax.lax.conv_general_dilated(h, woff, (1, 1), [(1, 1), (1, 1)], dimension_numbers=('NCHW', 'OIHW', 'NCHW')) + boff[None, :, None, None]
            o = off[:, :18].reshape(B, 9, 2, H, W)
            mask = jax.nn.sigmoid(off[:, 18:])
            ky, kx = jnp.meshgrid(jnp.arange(3), jnp.arange(3), indexing='ij')
            base_y = (jnp.arange(H)[None, :, None] - 1 + ky.reshape(9)[:, None, None]).astype(h.dtype)
            base_x = (jnp.arange(W)[None, None, :] - 1 + kx.reshape(9)[:, None, None]).astype(h.dtype)
            y = o[:, :, 0] + base_y[None]
            x = o[:, :, 1] + base_x[None]
            samp = _bilinear(h, y, x) * mask[:, None]
            out = jnp.einsum('bckhw,ock->bohw', samp, w2.reshape(w2.shape[0], w2.shape[1], 9))
            return out + b2[None, :, None, None]
        h = jax.nn.relu(_bn(_conv1x1(x, w1), bn1_g, bn1_b, bn1_m, bn1_v))
        h = _dcn(h, woff, boff, w2, dcn_b)
        h = jax.nn.relu(_bn(h, bn2_g, bn2_b, bn2_m, bn2_v))
        h = _bn(_conv1x1(h, w3), bn3_g, bn3_b, bn3_m, bn3_v)
        return jax.nn.relu(h + x)

    def _gn(v, G=32, eps=1e-05):
        B_, C_, H_, W_ = v.shape
        g = v.reshape(B_, G, C_ // G, H_, W_)
        m = jnp.mean(g, axis=(2, 3, 4), keepdims=True)
        s = jnp.var(g, axis=(2, 3, 4), keepdims=True)
        return ((g - m) / jnp.sqrt(s + eps)).reshape(v.shape)

    def _ln_c(v, eps=1e-06):
        m = jnp.mean(v, axis=1, keepdims=True)
        s = jnp.var(v, axis=1, keepdims=True)
        return (v - m) / jnp.sqrt(s + eps)

    def _ln_t(v, eps=1e-05):
        m = jnp.mean(v, axis=-1, keepdims=True)
        s = jnp.var(v, axis=-1, keepdims=True)
        return (v - m) / jnp.sqrt(s + eps)

    def _to_tokens(v):
        B_, C_, H_, W_ = v.shape
        return v.reshape(B_, C_, H_ * W_).transpose(0, 2, 1)

    def _from_tokens(t, like):
        B_, C_, H_, W_ = like.shape
        return t.transpose(0, 2, 1).reshape(B_, C_, H_, W_)
    x = _L0_conv_ref(x, L0_conv_qw, L0_conv_qb, L0_conv_kw, L0_conv_kb, L0_conv_vw, L0_conv_vb, L0_conv_rw, L0_conv_rb, L0_conv_c1w, L0_conv_c1b, L0_conv_c2w, L0_conv_c2b)
    x = _L1_conv_ref(x, L1_conv_c1_dw_w, L1_conv_c1_dw_b, L1_conv_c1_pw_w, L1_conv_c1_pw_b, L1_conv_c2_dw_w, L1_conv_c2_dw_b, L1_conv_c2_pw_w, L1_conv_c2_pw_b, L1_conv_c3_dw_w, L1_conv_c3_dw_b, L1_conv_c3_pw_w, L1_conv_c3_pw_b, L1_conv_co_w, L1_conv_co_b)
    x = _L2_conv_ref(x, L2_conv_gn_w, L2_conv_gn_b, L2_conv_w_in, L2_conv_w_dw, L2_conv_row_wd, L2_conv_row_bd, L2_conv_row_wv, L2_conv_row_bv, L2_conv_col_wd, L2_conv_col_bd, L2_conv_col_wv, L2_conv_col_bv, L2_conv_w_out)
    x = _L3_conv_ref(x, L3_conv_w1, L3_conv_bn1_g, L3_conv_bn1_b, L3_conv_bn1_m, L3_conv_bn1_v, L3_conv_woff, L3_conv_boff, L3_conv_w2, L3_conv_dcn_b, L3_conv_bn2_g, L3_conv_bn2_b, L3_conv_bn2_m, L3_conv_bn2_v, L3_conv_w3, L3_conv_bn3_g, L3_conv_bn3_b, L3_conv_bn3_m, L3_conv_bn3_v)
    return x

_drawn_inputs = setup_inputs


def setup_inputs(seed=0):
    import zlib

    import numpy as np

    out = dict(_drawn_inputs(seed))
    spreads = {'L0_conv_qb': (0.0, 2.0),
     'L0_conv_kb': (0.0, 2.0),
     'L0_conv_vb': (0.0, 0.1),
     'L0_conv_rb': (0.0, 0.1),
     'L0_conv_c1b': (0.0, 0.1),
     'L0_conv_c2b': (0.0, 0.1),
     'L2_conv_gn_w': (1.0, 0.6),
     'L2_conv_gn_b': (0.0, 0.8)}
    factors = {'L0_conv_qw': 7.334,
     'L0_conv_kw': 7.15,
     'L1_conv_c1_dw_w': 8.0,
     'L1_conv_c1_dw_b': 8.0,
     'L1_conv_c1_pw_w': 8.0,
     'L1_conv_c1_pw_b': 5.868,
     'L1_conv_c2_dw_w': 8.0,
     'L1_conv_c2_dw_b': 8.0,
     'L1_conv_c2_pw_w': 8.0,
     'L1_conv_c2_pw_b': 8.0,
     'L1_conv_c3_dw_w': 8.0,
     'L1_conv_c3_dw_b': 200.0,
     'L1_conv_c3_pw_w': 8.0,
     'L1_conv_c3_pw_b': 200.0,
     'L1_conv_co_w': 5.114,
     'L2_conv_w_in': 8.0,
     'L2_conv_w_dw': 8.0,
     'L2_conv_row_wd': 8.0,
     'L2_conv_row_bd': 44.042,
     'L2_conv_row_wv': 8.0,
     'L2_conv_row_bv': 39.905,
     'L2_conv_col_wd': 8.0,
     'L2_conv_col_bd': 28.918,
     'L2_conv_col_wv': 8.0,
     'L2_conv_col_bv': 48.356,
     'L2_conv_w_out': 7.91,
     'L3_conv_bn1_g': 18.958,
     'L3_conv_bn1_b': 64.0,
     'L3_conv_bn1_m': 48.017,
     'L3_conv_bn1_v': 27.678,
     'L3_conv_woff': 8.0,
     'L3_conv_boff': 61.427,
     'L3_conv_bn2_g': 22.264,
     'L3_conv_bn2_b': 72.401,
     'L3_conv_bn2_m': 23.008,
     'L3_conv_bn2_v': 56.24,
     'L3_conv_bn3_v': 27.648,
     'L1_conv_co_b': 2.889,
     'L3_conv_w1': 2.995,
     'L3_conv_w2': 2.975,
     'L3_conv_dcn_b': 8.0,
     'L3_conv_bn3_g': 8.0,
     'L3_conv_bn3_b': 24.185,
     'L3_conv_bn3_m': 8.0}
    for name, (base, spread) in spreads.items():
        noise = np.random.default_rng([zlib.crc32(name.encode()), seed]).standard_normal(out[name].shape)
        drawn = base * np.exp(spread * noise) if base else spread * noise
        out[name] = jnp.asarray(drawn.astype(out[name].dtype))
    for name, factor in factors.items():
        out[name] = (out[name] * factor).astype(out[name].dtype)
    return out
```

```python
from contextlib import ExitStack

import concourse.bass as bass
from concourse import mybir

F32 = mybir.dt.float32
U32 = mybir.dt.uint32
ALU = mybir.AluOpType
ACT = mybir.ActivationFunctionType
AX_X = mybir.AxisListType.X

B, C, H, W = 8, 128, 32, 32
N = H * W
HALF = N // 2
HR = H // 2
T = N // 128
R = C // 8
RS = R + 1
DIL = (1, 3, 5)
PADD = max(DIL)
CB = 32
NT = 9
QS = W + 2
QT = 11
QP = (H + 1) * QS // QT
INNER = 64
h2, w2 = H // 2, W // 2
NP = h2 * w2
EPS_L0, EPS_GN, EPS_BN = 1e-6, 1e-5, 1e-5
ROUND = float(2 ** 23)

FIELDS = [("wkv", 2 * C), ("kvb", 2 * C), ("qwT", C), ("rwT", C), ("c1T", 9 * C), ("ident", C), ("c2T", 9 * C),
          ("pwT", 3 * RS), ("dww", 27), ("dwb", 3), ("pwb", 3), ("coT", C), ("densel", C),
          ("winY", C), ("winG", C), ("dwk", 9), ("wd", C), ("wv", C), ("wout", C),
          ("w1T", C), ("woff", 4 * 27), ("w2T", 3 * CB), ("w3T", C), ("base", T * 18),
          ("qb", 1), ("rb", 1), ("c1b", 1), ("c2b", 1), ("gnw", 1), ("gnb", 1), ("bd", 1), ("bv", 1), ("boff", 1),
          ("bn1", 4), ("bn2", 5), ("bn3", 4)]
AT = {}
_n = 0
for _name, _len in FIELDS:
    AT[_name] = (_n, _len)
    _n += _len
WCOLS = _n
FIRST = AT["c1T"][0]


def build(nc, x, weights, table, out):
    with ExitStack() as ctx:
        def sb(name, shape, dt=F32):
            return ctx.enter_context(nc.sbuf_tensor(name, shape, dt))

        def sem(name):
            return ctx.enter_context(nc.semaphore(name))

        wt = sb("wt", [128, WCOLS])

        def w(name):
            a, n = AT[name]
            return wt[:, a:a + n]

        PA = ctx.enter_context(nc.psum_tensor("PA", [128, N], F32))
        PB = ctx.enter_context(nc.psum_tensor("PB", [128, N], F32))
        PC = ctx.enter_context(nc.psum_tensor("PC", [128, N], F32))
        PD = ctx.enter_context(nc.psum_tensor("PD", [128, N], F32))
        PAB = (PA, PB)

        ones = sb("ones", [128, 128])
        mean = sb("mean", [128, 128])
        wf = sb("wf", [128, 3, 9, RS])
        fbias = sb("fbias", [128, 3])
        bns = sb("bns", [128, 3])
        bnb = sb("bnb", [128, 3])
        bnt = sb("bnt", [128, 3])
        bnr = sb("bnr", [128, 3])
        xin = sb("xin", [128, N])
        kvt = sb("kvt", [128, T, 2 * C])
        ksqj = sb("ksqj", [128, C])
        kss = sb("kss", [128, T])
        krn = sb("krn", [128, T])
        kn = sb("kn", [128, T, C + 1])
        q = sb("q", [128, N])
        qsq = sb("qsq", [128, N])
        kv = sb("kv", [128, C + 1])
        ksr = sb("ksr", [128, 128])
        m2 = sb("m2", [128, C])
        rv = sb("rv", [128, 1])
        nq = sb("nq", [128, N])
        den = sb("den", [128, N])
        num = sb("num", [128, N])
        attn = sb("attn", [128, H + 2, W + 2])
        h1 = sb("h1", [128, H + 2, W + 2])
        hx = qsq[:].rearrange("p (a b) -> p a b", b=W)
        x1 = sb("x1", [128, H + 2 * PADD, W + 2 * PADD])
        four = sb("four", [128, N])
        f1, U, off, h3 = four[0:RS], four[32:32 + RS], four[64:91], four[96:128]
        f2 = sb("f2", [RS, N])
        f3 = sb("f3", [RS, N])
        f1T = sb("f1T", [128, T, RS])
        mx = sb("mx", [128, T])
        nm = sb("nm", [128, T])
        E = sb("E", [128, 2, N])
        rden = sb("rden", [128, N])
        x2 = sb("x2", [128, H, W])
        st = sb("st", [128, 2, 6])
        mv = sb("mv", [128, 2])
        gs = sb("gs", [128, 8])
        p1 = sb("p1", [128, h2, W])
        p2 = sb("p2", [128, h2, w2])
        y0 = sb("y0", [128, NP])
        ypad = sb("ypad", [128, h2 + 2, w2 + 2])
        y1 = sb("y1", [128, h2, w2])
        y2 = sb("y2", [128, NP])
        es = sb("es", [128, NP])
        gate = sb("gate", [128, h2, w2])
        dl = sb("dl", [128, h2, w2])
        af = sb("af", [128, h2, w2])
        ab = sb("ab", [128, h2, w2])
        bb = sb("bb", [128, NP])
        sf = sb("sf", [128, NP])
        sr = sb("sr", [128, NP])
        ss = sb("ss", [128, h2, w2])
        yg = sb("yg", [128, h2, w2])
        zp = sb("zp", [128, h2, w2 + 2])
        up = sb("up", [128, h2 + 2, W])
        rs = sb("rs", [128, h2, 2, W])
        x3 = sb("x3", [128, H, W])
        S4 = sb("S4", [128, H + 2, W + 2])
        offT = sb("offT", [128, T, 27])
        quads = sb("quads", [QP, QT, 128])
        uu = sb("uu", [128, T, 18])
        rr = sb("rr", [128, T, 18])
        gg = sb("gg", [128, T, 18])
        u0 = sb("u0", [128, T, 18])
        w1_ = sb("w1_", [128, T, 18])
        w0_ = sb("w0_", [128, T, 18])
        ixf = sb("ixf", [128, T, 9])
        ix = sb("ix", [128, T * 9], U32)
        em = sb("em", [128, T, 9])
        ay = sb("ay", [128, 2, T, 9])
        wq = sb("wq", [128, T, 9, 4])
        G = sb("G", [128, T, 9, 128])
        Gw = sb("Gw", [128, 9, 128])
        G2 = sb("G2", [128, 9, 64])
        sm = sb("sm", [128, 2, 9 * CB])
        sT = sb("sT", [96, 3, HALF])
        o = den
        ob = sb("ob", [128, N])

        names = ("w_in x_in zeroed consts bnv_sb bnr_sb kss_rt gnv_sb gn_rt bias_mm init_v kvt_ps kvt_sb ksq_sb krn_sb kn_sb q_ps q_sb qsq_sb nq_ps kv_ps kv_sb ksr_sb "
                 "m2_ps m2_sb kq_ps m2q_ps nq_sb den_sb rden_sb num_sb attn_raw attn_sb c1_ps h1_sb c2_ps hx_sb x1_sb "
                 "f_ps f_sb f1T_ps f1T_sb s_ps mx_sb nm_sb nmrow_ps nmrow_sb st_ps e_sb pv_ps U_sb co_ps rd_sb av_sb x2_sb "
                 "stat_sb mu_ps dev_sb var_ps gn_sb pool_sb y0_sb yw_ps ypad_sb eg_sb gate_sb y1_sb es_sb y2_sb dv_ps "
                 "ed_sb scan_in scan_sb ss_sb yg_sb z_ps zp_sb up_sb upe_sb rs_sb x3_sb "
                 "w1_ps s4_sb off_ps off_sb offT_ps offT_sb tab_ps quads_sb table_in ixs em_sb ix_sb wq_sb "
                 "wq3_sb gw_sb g2_sb sm_sb tr_ps sT_sb dcn_ps h3_sb w3_ps o_sb ob_sb stored").split()
        S = {n: sem("s_" + n) for n in names}
        gathered = [sem(f"s_gathered{t}") for t in range(T)]
        IX_STEPS = 9

        def vec(name, i=0, p=128):
            a, n = AT[name]
            return wt[0:p, a + i:a + i + 1]

        def rows(ap, half):
            return ap[:, half * HALF:(half + 1) * HALF]

        block = ctx.enter_context(nc.Block())

        @block.sync
        def _(sp):
            sp.dma_start(wt[:, 0:FIRST], weights[:, 0:FIRST]).then_inc(S["w_in"], 16)
            sp.dma_start(xin[:], x[0]).then_inc(S["x_in"], 16)
            sp.wait_ge(S["w_in"], 16)
            sp.dma_start(wt[:, FIRST:WCOLS], weights[:, FIRST:WCOLS]).then_inc(S["w_in"], 16)

            def store_table(b):
                sp.wait_ge(S["quads_sb"], 3 * b + 3)
                if b:
                    for t in range(T):
                        sp.wait_ge(gathered[t], 144 * b)
                sp.dma_start(table.rearrange("(t p) c -> p t c", p=QP), quads[:]).then_inc(S["table_in"], 16)

            def store_out(b):
                sp.wait_ge(S["ob_sb"], b + 1)
                sp.dma_start(out[b], ob[:]).then_inc(S["stored"], 16)

            def load_next(b):
                sp.wait_ge(S["x1_sb"], 2 * b)
                sp.dma_start(xin[:], x[b]).then_inc(S["x_in"], 16)

            load_next(1)
            store_table(0)
            for b in range(1, B - 1):
                load_next(b + 1)
                store_out(b - 1)
                store_table(b)
            store_out(B - 2)
            store_table(B - 1)
            store_out(B - 1)
            sp.wait_ge(S["stored"], 16 * B)

        @block.gpsimd
        def _(pool):
            for buf in (attn, h1, x1, ypad, S4, af, ab):
                nc.gpsimd.memset(buf[:], 0.0).then_inc(S["zeroed"], 1)
            nc.gpsimd.memset(ones[:], 1.0).then_inc(S["zeroed"], 1)
            nc.gpsimd.memset(mean[:], 1.0 / C).then_inc(S["zeroed"], 1)
            nc.gpsimd.memset(kn[:], 1.0).then_inc(S["zeroed"], 1)

            def gathers(b):
                pool.wait_ge(S["table_in"], 16 * b + 16)
                pool.wait_ge(S["ix_sb"], b + 1)
                pool.wait_ge(S["wq_sb"], 5 * b + 5)
                nc.gpsimd.tensor_tensor(wq[:, :, :, 3], ay[:, 1], w1_[:, :, 1:18:2], ALU.mult).then_inc(S["wq3_sb"], 1)
                for t in range(T):
                    for k in range(NT):
                        pool.indirect_dma_start(G[:, t, k, :], None, table, bass.IndirectOffsetOnAxis(
                            ap=ix[:, NT * t + k:NT * t + k + 1], axis=0)).then_inc(gathered[t], 16)

            gathers(0)
            with pool.Fori(1, B) as b:
                pool.wait_ge(S["gw_sb"], T * b)
                gathers(b)

        @block.tensor
        def _(pe):
            mm = nc.tensor.matmul
            ident = w("ident")

            pe.wait_ge(S["zeroed"], 10)
            pe.wait_ge(S["w_in"], 32)
            for i in range(3):
                m = mm(PA[0:RS, i:i + 1], w("pwT")[:, i * RS:(i + 1) * RS], w("dwb")[:, i:i + 1], start=True, stop=True)
            m.then_inc(S["bias_mm"], 1)
            pe.wait_ge(S["init_v"], 1)

            def conv3(ps, wname, src, half):
                for tap in range(9):
                    dy, dx = divmod(tap, 3)
                    m = mm(rows(ps, half), w(wname)[:, tap * C:(tap + 1) * C],
                           src[:, dy + HR * half:dy + HR * half + HR, dx:dx + W], start=tap == 0, stop=tap == 8)
                return m

            def linear_attention(b):
                pe.wait_ge(S["x_in"], 16 * b + 16)
                for t in range(T):
                    bank = PAB[t // 4]
                    m = mm(bank[:, (t % 4) * 256:(t % 4 + 1) * 256], xin[:, 128 * t:128 * (t + 1)], w("wkv"),
                           start=True, stop=True)
                    if t % 2:
                        m.then_inc(S["kvt_ps"], 1)
                pe.wait_ge(S["quads_sb"], 3 * b)
                pe.wait_ge(S["offT_sb"], b)
                for half in range(2):
                    m = mm(rows(PC, half), w("qwT"), rows(xin, half), start=True, stop=True)
                m.then_inc(S["q_ps"], 1)
                pe.wait_ge(S["qsq_sb"], b + 1)
                for half in range(2):
                    m = mm(rows(PD, half), ones[:], rows(qsq, half), start=True, stop=True)
                m.then_inc(S["nq_ps"], 1)
                pe.wait_ge(S["kn_sb"], b + 1)
                for t in range(T):
                    mm(PA[:, 0:C + 1], kvt[:, t, C:2 * C], kn[:, t, :], start=t == 0, stop=t == T - 1)
                for t in range(T):
                    m = mm(PA[:, HALF:HALF + 128], kn[:, t, 0:C], ones[:], start=t == 0, stop=t == T - 1)
                m.then_inc(S["kv_ps"], 1)
                pe.wait_ge(S["kv_sb"], b + 1)
                mm(PB[:, 0:C], kv[:, 0:C], w("rwT"), start=True, stop=True)
                mm(PB[:, HALF:HALF + 1], w("rwT"), kv[:, C:C + 1], start=True, stop=True).then_inc(S["m2_ps"], 1)
                pe.wait_ge(S["ksr_sb"], b + 1)
                for half in range(2):
                    m = mm(rows(PC, half), ksr[:], rows(q, half), start=True, stop=True)
                m.then_inc(S["kq_ps"], 1)
                pe.wait_ge(S["m2_sb"], 2 * b + 2)
                for half in range(2):
                    m = mm(rows(PA, half), m2[:], rows(q, half), start=True, stop=True)
                m.then_inc(S["m2q_ps"], 1)
                pe.wait_ge(S["attn_sb"], b + 1)
                for half in range(2):
                    conv3(PB, "c1T", attn, half).then_inc(S["c1_ps"], 1)
                pe.wait_ge(S["h1_sb"], 2 * b + 2)
                for half in range(2):
                    conv3(PC, "c2T", h1, half).then_inc(S["c2_ps"], 1)

            def position_attention(b):
                pe.wait_ge(S["x1_sb"], 2 * b + 2)
                for n, (i, ps) in enumerate(((1, PA), (2, PB), (0, PD))):
                    d = DIL[i]
                    for half in range(2):
                        for tap in range(9):
                            r0 = PADD + (tap // 3 - 1) * d + HR * half
                            c0 = PADD + (tap % 3 - 1) * d
                            m = mm(ps[0:RS, half * HALF:(half + 1) * HALF], wf[:, i, tap, :],
                                   x1[:, r0:r0 + HR, c0:c0 + W], start=tap == 0, stop=tap == 8)
                    m.then_inc(S["f_ps"], 1)
                pe.wait_ge(S["f_sb"], 3 * b + 3)
                for t in range(T):
                    if t >= 2:
                        pe.wait_ge(S["mx_sb"], T * b + t - 1)
                    for half in range(2):
                        m = mm(rows(PAB[t % 2], half), f2[:, 128 * t:128 * (t + 1)], rows(f3, half), start=True, stop=True)
                    m.then_inc(S["s_ps"], 1)
                    if t == 1:
                        for j in range(T):
                            m = nc.tensor.transpose(PC[:, j * RS:(j + 1) * RS], f1[:, 128 * j:128 * (j + 1)], ident[0:RS, 0:RS])
                        m.then_inc(S["f1T_ps"], 1)
                pe.wait_ge(S["nm_sb"], b + 1)
                for t in range(T):
                    m = mm(PD[0:1, 128 * t:128 * (t + 1)], nm[:, t:t + 1], ident, start=True, stop=True)
                m.then_inc(S["nmrow_ps"], 1)
                pe.wait_ge(S["nmrow_sb"], b + 1)
                pe.wait_ge(S["f1T_sb"], b + 1)

                def weigh(j):
                    pe.wait_ge(S["e_sb"], T * b + j + 1)
                    for half in range(2):
                        m = mm(PC[0:RS, half * HALF:(half + 1) * HALF], f1T[:, j, :], rows(E[:, j % 2, :], half),
                               start=j == 0, stop=j == T - 1)
                    m.then_inc(S["pv_ps"], 1)

                for j in range(T):
                    if j >= 2:
                        pe.wait_ge(S["e_sb"], T * b + j - 1)
                    for half in range(2):
                        m = mm(rows(PAB[j % 2], half), f3[:, 128 * j:128 * (j + 1)], rows(f2, half), start=True, stop=True)
                    m.then_inc(S["st_ps"], 1)
                    if j >= 1:
                        weigh(j - 1)
                weigh(T - 1)
                pe.wait_ge(S["U_sb"], b + 1)
                for ps, name in ((PA, "coT"), (PB, "densel")):
                    for half in range(2):
                        m = mm(rows(ps, half), w(name)[32:32 + RS, :], rows(U, half), start=True, stop=True)
                m.then_inc(S["co_ps"], 1)

            def scans(b):
                pe.wait_ge(S["stat_sb"], b + 1)
                mm(PC[:, 0:1], mean[:], mv[:, 0:1], start=True, stop=True).then_inc(S["mu_ps"], 1)
                pe.wait_ge(S["dev_sb"], b + 1)
                mm(PC[:, HALF:HALF + 1], mean[:], gs[:, 1:2], start=True, stop=True).then_inc(S["var_ps"], 1)
                pe.wait_ge(S["y0_sb"], b + 1)
                mm(PA[:, 0:NP], w("winY"), y0[:], start=True, stop=True)
                mm(PB[:, 0:NP], w("winG"), y0[:], start=True, stop=True).then_inc(S["yw_ps"], 1)
                pe.wait_ge(S["y2_sb"], b + 1)
                mm(PA[:, HALF:HALF + NP], w("wd"), y2[:], start=True, stop=True)
                mm(PB[:, HALF:HALF + NP], w("wv"), y2[:], start=True, stop=True).then_inc(S["dv_ps"], 1)
                pe.wait_ge(S["yg_sb"], 2 * b + 2)
                mm(PC[:, 0:NP], w("wout"), yg[:].rearrange("p a b -> p (a b)"), start=True, stop=True).then_inc(S["z_ps"], 1)

            def offsets(b):
                pe.wait_ge(S["x3_sb"], 2 * b + 2)
                x3f = x3[:].rearrange("p a b -> p (a b)")
                for half in range(2):
                    m = mm(rows(PA, half), w("w1T"), rows(x3f, half), start=True, stop=True)
                m.then_inc(S["w1_ps"], 1)
                pe.wait_ge(S["s4_sb"], 4 * b + 4)
                for half in range(2):
                    for q4 in range(4):
                        by, bx = 2 * (q4 // 2), 2 * (q4 % 2)
                        m = mm(PB[0:27, half * HALF:(half + 1) * HALF], w("woff")[:, q4 * 27:(q4 + 1) * 27],
                               S4[:, by + HR * half:by + HR * half + HR, bx:bx + W], start=q4 == 0, stop=q4 == 3)
                m.then_inc(S["off_ps"], 1)
                s4f = S4[:].rearrange("p a b -> p (a b)")
                banks = (PC[:, HALF:N], PD[:, 0:HALF], PD[:, HALF:N])
                for t in range(QT):
                    if t == QT - 1:
                        pe.wait_ge(S["off_sb"], b + 1)
                    m = nc.tensor.transpose(banks[t // 4][0:QP, (t % 4) * 128:(t % 4 + 1) * 128],
                                            s4f[:, QP * t:QP * (t + 1)], ident)
                    if t % 4 == 3 or t == QT - 1:
                        m.then_inc(S["tab_ps"], 1)
                for t in range(T):
                    m = nc.tensor.transpose(PC[:, t * 27:(t + 1) * 27], off[:, 128 * t:128 * (t + 1)], ident[64:91, 64:91])
                m.then_inc(S["offT_ps"], 1)

            def deformed(b):
                for t in range(T):
                    pe.wait_ge(S["sm_sb"], T * b + t + 1)
                    if t >= 2:
                        pe.wait_ge(S["sT_sb"], T * b + t - 1)
                    ps = (PC[0:96, 0:3 * 128], PD[0:96, 0:3 * 128])[t % 2]
                    for g in range(3):
                        m = nc.tensor.transpose(ps[:, g * 128:(g + 1) * 128], sm[:, t % 2, g * 96:(g + 1) * 96], ident)
                    m.then_inc(S["tr_ps"], 1)
                    if t % 4 == 3:
                        half = t // 4
                        pe.wait_ge(S["sT_sb"], T * b + t + 1)
                        for g in range(3):
                            m = mm(PB[0:CB, half * HALF:(half + 1) * HALF], w("w2T")[0:96, g * CB:(g + 1) * CB],
                                   sT[:, g, :], start=g == 0, stop=g == 2)
                        m.then_inc(S["dcn_ps"], 1)
                pe.wait_ge(S["h3_sb"], b + 1)
                for half in range(2):
                    m = mm(rows(PD, half), w("w3T")[96:128, :], rows(h3, half), start=True, stop=True)
                m.then_inc(S["w3_ps"], 1)

            def image(b, first):
                linear_attention(b)
                position_attention(b)
                if not first:
                    deformed(b - 1)
                scans(b)
                offsets(b)

            image(0, True)
            with pe.Fori(1, B) as b:
                image(b, False)
            deformed(B - 1)

        @block.scalar
        def _(act):
            a_ = nc.scalar.activation

            def linear_attention(b):
                act.wait_ge(S["q_ps"], b + 1)
                a_(q[:], PC[:], ACT.Identity, bias=vec("qb")).then_inc(S["q_sb"], 1)
                a_(qsq[:], PC[:], ACT.Square, bias=vec("qb")).then_inc(S["qsq_sb"], 1)
                for t in range(T):
                    act.wait_ge(S["kvt_sb"], 4 * b + t // 2 + 1)
                    a_(ksqj[:], kvt[:, t, 0:C], ACT.Square, accum_out=kss[:, t:t + 1]).then_inc(S["ksq_sb"], 1)
                    act.wait_ge(S["ksq_sb"], T * b + t + 1)
                a_(kss[:], kss[:], ACT.Sqrt).then_inc(S["kss_rt"], 1)
                act.wait_ge(S["nq_ps"], b + 1)
                a_(nq[:], PD[:], ACT.Sqrt).then_inc(S["nq_sb"], 1)
                act.wait_ge(S["kv_ps"], b + 1)
                a_(kv[:], PA[:, 0:C + 1], ACT.Copy).then_inc(S["kv_sb"], 1)
                act.wait_ge(S["m2_ps"], b + 1)
                a_(m2[:], PB[:, 0:C], ACT.Copy).then_inc(S["m2_sb"], 1)
                a_(rv[:], PB[:, HALF:HALF + 1], ACT.Copy).then_inc(S["m2_sb"], 1)
                act.wait_ge(S["attn_raw"], b + 1)
                a_(attn[:, 1:H + 1, 1:W + 1], num[:].rearrange("p (a b) -> p a b", b=W), ACT.Identity,
                   bias=vec("rb")).then_inc(S["attn_sb"], 1)
                for half in range(2):
                    act.wait_ge(S["c1_ps"], 2 * b + half + 1)
                    a_(h1[:, 1 + HR * half:1 + HR * half + HR, 1:W + 1], rows(PB, half).rearrange("p (a b) -> p a b", b=W),
                       ACT.Identity, bias=vec("c1b")).then_inc(S["h1_sb"], 1)

            def position_attention(b):
                for n, (i, ps, f) in enumerate(((1, PA, f2), (2, PB, f3), (0, PD, f1))):
                    act.wait_ge(S["f_ps"], 3 * b + n + 1)
                    a_(f[:, :], ps[0:RS, :], ACT.Identity, bias=fbias[0:RS, i:i + 1]).then_inc(S["f_sb"], 1)
                act.wait_ge(S["f1T_ps"], b + 1)
                a_(f1T[:].rearrange("p a b -> p (a b)"), PC[:, 0:T * RS], ACT.Copy).then_inc(S["f1T_sb"], 1)
                act.wait_ge(S["nmrow_ps"], b + 1)
                a_(f2[0:1, :], PD[0:1, :], ACT.Copy).then_inc(S["nmrow_sb"], 1)
                for j in range(T):
                    act.wait_ge(S["st_ps"], T * b + j + 1)
                    if j >= 2:
                        act.wait_ge(S["pv_ps"], T * b + j - 1)
                    a_(E[:, j % 2, :], PAB[j % 2][:], ACT.Exp).then_inc(S["e_sb"], 1)
                act.wait_ge(S["pv_ps"], T * b + T)
                a_(U, PC[0:RS, :], ACT.Copy).then_inc(S["U_sb"], 1)

            def scans(b):
                act.wait_ge(S["gnv_sb"], b + 1)
                a_(gs[:, 7:8], gs[:, 7:8], ACT.Sqrt).then_inc(S["gn_rt"], 1)
                act.wait_ge(S["yw_ps"], b + 1)
                yw = PA[:, 0:NP].rearrange("p (a b) -> p a b", b=w2)
                a_(ypad[0:INNER, 1:h2 + 1, 1:w2 + 1], yw[0:INNER], ACT.Copy).then_inc(S["ypad_sb"], 1)
                a_(ypad[INNER:128, 1:w2 + 1, 1:h2 + 1], yw[INNER:128].rearrange("p a b -> p b a"), ACT.Copy)\
                    .then_inc(S["ypad_sb"], 1)
                a_(gate[:].rearrange("p a b -> p (a b)"), PB[:, 0:NP], ACT.Sigmoid).then_inc(S["gate_sb"], 1)
                act.wait_ge(S["y1_sb"], 9 * b + 9)
                a_(es[:], y1[:].rearrange("p a b -> p (a b)"), ACT.Sigmoid).then_inc(S["es_sb"], 1)
                act.wait_ge(S["dv_ps"], b + 1)
                a_(dl[:].rearrange("p a b -> p (a b)"), PA[:, HALF:HALF + NP], ACT.Sigmoid, bias=vec("bd"))\
                    .then_inc(S["ed_sb"], 1)
                act.wait_ge(S["z_ps"], b + 1)
                z = PC[:, 0:NP].rearrange("p (a b) -> p a b", b=w2)
                a_(zp[:, :, 1:w2 + 1], z, ACT.Copy, scale=1.0 / 64).then_inc(S["zp_sb"], 1)
                a_(zp[:, :, 0:1], z[:, :, 0:1], ACT.Copy, scale=1.0 / 64).then_inc(S["zp_sb"], 1)
                a_(zp[:, :, w2 + 1:w2 + 2], z[:, :, w2 - 1:w2], ACT.Copy, scale=1.0 / 64).then_inc(S["zp_sb"], 1)

            def offsets(b):
                act.wait_ge(S["w1_ps"], b + 1)
                hp = PA[:].rearrange("p (a b) -> p a b", b=W)
                for g in range(4):
                    dy, dx = divmod(g, 2)
                    s = slice(32 * g, 32 * g + 32)
                    a_(S4[s, 1 - dy:H + 1 - dy, 1 - dx:W + 1 - dx], hp[s], ACT.Relu, scale=bns[s, 0:1],
                       bias=bnb[s, 0:1]).then_inc(S["s4_sb"], 1)
                act.wait_ge(S["off_ps"], b + 1)
                a_(off, PB[0:27, :], ACT.Identity, bias=vec("boff", 0, 27)).then_inc(S["off_sb"], 1)
                banks = (PC[0:QP, HALF:N], PD[0:QP, 0:HALF], PD[0:QP, HALF:HALF + 384])
                for n in range(3):
                    act.wait_ge(S["tab_ps"], 3 * b + n + 1)
                    if n == 0:
                        act.wait_ge(S["table_in"], 16 * b)
                    last = min(4 * n + 4, QT)
                    a_(quads[:, 4 * n:last, :].rearrange("p a b -> p (a b)"), banks[n], ACT.Copy).then_inc(S["quads_sb"], 1)
                act.wait_ge(S["offT_sb"], b + 1)
                a_(em[:], offT[:, :, 18:27], ACT.Sigmoid).then_inc(S["em_sb"], 1)

            def deformed(b):
                for t in range(T):
                    act.wait_ge(S["tr_ps"], T * b + t + 1)
                    ps = (PC[0:96, 0:3 * 128], PD[0:96, 0:3 * 128])[t % 2]
                    if t == 4:
                        act.wait_ge(S["dcn_ps"], 2 * b + 1)
                    a_(sT[:, :, 128 * (t % 4):128 * (t % 4 + 1)], ps.rearrange("p (g n) -> p g n", g=3), ACT.Copy)\
                        .then_inc(S["sT_sb"], 1)
                act.wait_ge(S["dcn_ps"], 2 * b + 2)
                a_(h3, PB[0:CB, :], ACT.Relu, scale=bns[0:CB, 1:2], bias=bnb[0:CB, 1:2]).then_inc(S["h3_sb"], 1)
                act.wait_ge(S["o_sb"], b + 1)
                act.wait_ge(S["stored"], 16 * b)
                a_(ob[:], o[:], ACT.Relu, bias=bnb[:, 2:3]).then_inc(S["ob_sb"], 1)

            def image(b, first):
                linear_attention(b)
                position_attention(b)
                if not first:
                    deformed(b - 1)
                scans(b)
                offsets(b)

            act.wait_ge(S["zeroed"], 10)
            act.wait_ge(S["bnv_sb"], 3)
            a_(bnt[:], bnt[:], ACT.Sqrt).then_inc(S["bnr_sb"], 1)
            act.wait_ge(S["init_v"], 1)
            image(0, True)
            with act.Fori(1, B) as b:
                image(b, False)
            deformed(B - 1)

        @block.vector
        def _(dve):
            v = nc.vector
            dve.wait_ge(S["w_in"], 32)
            dve.wait_ge(S["zeroed"], 10)
            pwT = w("pwT").rearrange("p (i r) -> p i r", i=3)
            dww = w("dww").rearrange("p (i t) -> p i t", i=3)
            v.tensor_tensor(wf[:], pwT.unsqueeze(2).to_broadcast([128, 3, 9, RS]),
                            dww.unsqueeze(3).to_broadcast([128, 3, 9, RS]), ALU.mult).then_inc(S["consts"], 1)
            dve.wait_ge(S["bias_mm"], 1)
            v.tensor_tensor(fbias[0:RS, :], PA[0:RS, 0:3], w("pwb")[0:RS, :], ALU.add).then_inc(S["consts"], 1)
            bns_names = ("bn1", "bn2", "bn3")
            for i, name in enumerate(bns_names):
                v.tensor_scalar(bnt[:, i:i + 1], vec(name, 3), EPS_BN, None, ALU.add).then_inc(S["bnv_sb"], 1)
            dve.wait_ge(S["bnr_sb"], 1)
            v.reciprocal(bnr[:], bnt[:]).then_inc(S["bnr_sb"], 1)
            dve.wait_ge(S["bnr_sb"], 2)
            for i, name in enumerate(bns_names):
                v.tensor_tensor(bns[:, i:i + 1], bnr[:, i:i + 1], vec(name, 0), ALU.mult).then_inc(S["consts"], 1)
                if i == 1:
                    v.tensor_tensor(bnt[:, 1:2], vec(name, 4), vec(name, 2), ALU.subtract).then_inc(S["consts"], 1)
                else:
                    v.tensor_scalar(bnt[:, i:i + 1], vec(name, 2), -1.0, None, ALU.mult).then_inc(S["consts"], 1)
                dve.wait_ge(S["consts"], 4 + 3 * i)
                v.scalar_tensor_tensor(bnb[:, i:i + 1], bnt[:, i:i + 1], bns[:, i:i + 1], vec(name, 1),
                                       ALU.mult, ALU.add).then_inc(S["consts"], 1)
            dve.wait_ge(S["consts"], 11)
            v.memset(gs[:], 0.0).then_inc(S["init_v"], 1)

            def linear_attention(b):
                for j in range(4):
                    dve.wait_ge(S["kvt_ps"], 4 * b + j + 1)
                    bank = PAB[j // 2][:, (j % 2) * HALF:(j % 2 + 1) * HALF].rearrange("p (t n) -> p t n", t=2)
                    v.tensor_tensor(kvt[:, 2 * j:2 * j + 2, :], bank,
                                    w("kvb").unsqueeze(1).to_broadcast([128, 2, 2 * C]), ALU.add).then_inc(S["kvt_sb"], 1)
                dve.wait_ge(S["kss_rt"], b + 1)
                v.reciprocal(krn[:], kss[:]).then_inc(S["krn_sb"], 1)
                dve.wait_ge(S["krn_sb"], b + 1)
                v.tensor_tensor(kn[:, :, 0:C], kvt[:, :, 0:C], krn[:].unsqueeze(2).to_broadcast([128, T, C]), ALU.mult)\
                    .then_inc(S["kn_sb"], 1)
                dve.wait_ge(S["kv_ps"], b + 1)
                v.tensor_copy(ksr[:], PA[:, HALF:HALF + 128]).then_inc(S["ksr_sb"], 1)
                dve.wait_ge(S["nq_sb"], b + 1)
                dve.wait_ge(S["kq_ps"], b + 1)
                v.scalar_tensor_tensor(den[:], nq[:], N + EPS_L0, PC[:], ALU.mult, ALU.add).then_inc(S["den_sb"], 1)
                dve.wait_ge(S["den_sb"], b + 1)
                v.reciprocal(rden[:], den[:]).then_inc(S["rden_sb"], 1)
                dve.wait_ge(S["rden_sb"], b + 1)
                dve.wait_ge(S["m2q_ps"], b + 1)
                v.scalar_tensor_tensor(den[:], nq[:], rv[:, 0:1], PA[:], ALU.mult, ALU.add).then_inc(S["num_sb"], 1)
                dve.wait_ge(S["num_sb"], b + 1)
                v.tensor_tensor(num[:], den[:], rden[:], ALU.mult).then_inc(S["attn_raw"], 1)
                for half in range(2):
                    dve.wait_ge(S["c2_ps"], 2 * b + half + 1)
                    s = slice(HR * half, HR * half + HR)
                    xh = rows(xin, half).rearrange("p (a b) -> p a b", b=W)
                    v.scalar_tensor_tensor(hx[:, s, :], rows(PC, half).rearrange("p (a b) -> p a b", b=W), vec("c2b"),
                                           xh, ALU.add, ALU.mult).then_inc(S["hx_sb"], 1)
                    dve.wait_ge(S["hx_sb"], 2 * b + half + 1)
                    v.tensor_tensor(x1[:, PADD + HR * half:PADD + HR * half + HR, PADD:PADD + W], hx[:, s, :], xh, ALU.add)\
                        .then_inc(S["x1_sb"], 1)

            def position_attention(b):
                for t in range(T):
                    dve.wait_ge(S["s_ps"], T * b + t + 1)
                    v.tensor_reduce(mx[:, t:t + 1], PAB[t % 2][:], AX_X, ALU.max).then_inc(S["mx_sb"], 1)
                dve.wait_ge(S["mx_sb"], T * b + T)
                v.tensor_scalar(nm[:], mx[:], -1.0, None, ALU.mult).then_inc(S["nm_sb"], 1)
                dve.wait_ge(S["co_ps"], b + 1)
                v.reciprocal(rden[:], PB[:]).then_inc(S["rd_sb"], 1)
                dve.wait_ge(S["rd_sb"], b + 1)
                v.tensor_tensor(den[:], PA[:], rden[:], ALU.mult).then_inc(S["av_sb"], 1)
                dve.wait_ge(S["av_sb"], b + 1)
                v.tensor_tensor(x2[:], den[:].rearrange("p (a b) -> p a b", b=W), x1[:, PADD:PADD + H, PADD:PADD + W],
                                ALU.add).then_inc(S["x2_sb"], 1)

            def scans(b):
                dve.wait_ge(S["x2_sb"], b + 1)
                x2f = x2[:].rearrange("p a b -> p (a b)")
                for half in range(2):
                    v.bn_stats(st[:, half, :], rows(x2f, half)).then_inc(S["pool_sb"], 1)
                dve.wait_ge(S["pool_sb"], 4 * b + 2)
                v.tensor_tensor(p1[:], x2[:, 0:H:2, :], x2[:, 1:H:2, :], ALU.add).then_inc(S["pool_sb"], 1)
                v.bn_aggr(mv[:], st[:].rearrange("p a b -> p (a b)")).then_inc(S["stat_sb"], 1)
                dve.wait_ge(S["pool_sb"], 4 * b + 3)
                v.tensor_tensor(p2[:], p1[:, :, 0:W:2], p1[:, :, 1:W:2], ALU.add).then_inc(S["pool_sb"], 1)
                dve.wait_ge(S["mu_ps"], b + 1)
                dve.wait_ge(S["stat_sb"], b + 1)
                v.tensor_tensor(gs[:, 0:1], mv[:, 0:1], PC[:, 0:1], ALU.subtract).then_inc(S["gn_sb"], 1)
                v.tensor_scalar(gs[:, 2:3], PC[:, 0:1], -1.0, None, ALU.mult).then_inc(S["gn_sb"], 1)
                dve.wait_ge(S["gn_sb"], 6 * b + 2)
                v.scalar_tensor_tensor(gs[:, 1:2], gs[:, 0:1], gs[:, 0:1], mv[:, 1:2], ALU.mult, ALU.add).then_inc(S["dev_sb"], 1)
                dve.wait_ge(S["var_ps"], b + 1)
                v.tensor_scalar(gs[:, 7:8], PC[:, HALF:HALF + 1], EPS_GN, None, ALU.add).then_inc(S["gnv_sb"], 1)
                dve.wait_ge(S["gn_rt"], b + 1)
                v.reciprocal(gs[:, 3:4], gs[:, 7:8]).then_inc(S["gn_sb"], 1)
                dve.wait_ge(S["gn_sb"], 6 * b + 3)
                v.tensor_tensor(gs[:, 4:5], gs[:, 3:4], vec("gnw"), ALU.mult).then_inc(S["gn_sb"], 1)
                dve.wait_ge(S["gn_sb"], 6 * b + 4)
                v.scalar_tensor_tensor(gs[:, 5:6], gs[:, 2:3], gs[:, 4:5], vec("gnb"), ALU.mult, ALU.add).then_inc(S["gn_sb"], 1)
                v.tensor_scalar(gs[:, 6:7], gs[:, 4:5], 0.25, None, ALU.mult).then_inc(S["gn_sb"], 1)
                dve.wait_ge(S["gn_sb"], 6 * b + 6)
                dve.wait_ge(S["pool_sb"], 4 * b + 4)
                v.tensor_scalar(y0[:], p2[:].rearrange("p a b -> p (a b)"), gs[:, 6:7], gs[:, 5:6], ALU.mult, ALU.add)\
                    .then_inc(S["y0_sb"], 1)
                dve.wait_ge(S["ypad_sb"], 2 * b + 2)
                for tap in range(9):
                    src = ypad[:, tap // 3:tap // 3 + h2, tap % 3:tap % 3 + w2]
                    if tap == 0:
                        v.tensor_scalar(y1[:], src, vec("dwk", 0), None, ALU.mult).then_inc(S["y1_sb"], 1)
                    else:
                        dve.wait_ge(S["y1_sb"], 9 * b + tap)
                        v.scalar_tensor_tensor(y1[:], src, vec("dwk", tap), y1[:], ALU.mult, ALU.add).then_inc(S["y1_sb"], 1)
                dve.wait_ge(S["es_sb"], b + 1)
                v.tensor_tensor(y2[:], y1[:].rearrange("p a b -> p (a b)"), es[:], ALU.mult).then_inc(S["y2_sb"], 1)
                dve.wait_ge(S["ed_sb"], b + 1)
                v.tensor_scalar(af[:, :, 1:w2], dl[:, :, 1:w2], -1.0, 1.0, ALU.mult, ALU.add).then_inc(S["scan_in"], 1)
                v.tensor_scalar(ab[:, :, 0:w2 - 1], dl[:, :, 0:w2 - 1], -1.0, 1.0, ALU.mult, ALU.add).then_inc(S["scan_in"], 1)
                v.scalar_tensor_tensor(bb[:], PB[:, HALF:HALF + NP], vec("bv"), dl[:].rearrange("p a b -> p (a b)"),
                                       ALU.add, ALU.mult).then_inc(S["scan_in"], 1)
                dve.wait_ge(S["scan_in"], 3 * b + 3)
                v.tensor_tensor_scan(sf[:], af[:].rearrange("p a b -> p (a b)"), bb[:], 0.0, ALU.mult, ALU.add)\
                    .then_inc(S["scan_sb"], 1)
                v.tensor_tensor_scan(sr[:, ::-1], ab[:].rearrange("p a b -> p (a b)")[:, ::-1], bb[:, ::-1], 0.0,
                                     ALU.mult, ALU.add).then_inc(S["scan_sb"], 1)
                dve.wait_ge(S["scan_sb"], 2 * b + 2)
                v.tensor_tensor(ss[:].rearrange("p a b -> p (a b)"), sf[:], sr[:], ALU.add).then_inc(S["ss_sb"], 1)
                dve.wait_ge(S["ss_sb"], b + 1)
                dve.wait_ge(S["gate_sb"], b + 1)
                v.tensor_tensor(yg[0:INNER], ss[0:INNER], gate[0:INNER], ALU.mult).then_inc(S["yg_sb"], 1)
                v.tensor_tensor(yg[INNER:128], ss[INNER:128].rearrange("p a b -> p b a"), gate[INNER:128], ALU.mult)\
                    .then_inc(S["yg_sb"], 1)
                dve.wait_ge(S["zp_sb"], 3 * b + 3)
                mid = zp[:, :, 1:w2 + 1]
                for k in range(2):
                    v.scalar_tensor_tensor(up[:, 1:h2 + 1, k:W:2], mid, 3.0, zp[:, :, 2 * k:2 * k + w2], ALU.mult, ALU.add)\
                        .then_inc(S["up_sb"], 1)
                dve.wait_ge(S["up_sb"], 2 * b + 2)
                v.tensor_copy(up[:, 0:1, :], up[:, 1:2, :]).then_inc(S["upe_sb"], 1)
                v.tensor_copy(up[:, h2 + 1:h2 + 2, :], up[:, h2:h2 + 1, :]).then_inc(S["upe_sb"], 1)
                dve.wait_ge(S["upe_sb"], 2 * b + 2)
                for k in range(2):
                    v.scalar_tensor_tensor(rs[:, :, k, :], up[:, 1:h2 + 1, :], 3.0, up[:, 2 * k:2 * k + h2, :],
                                           ALU.mult, ALU.add).then_inc(S["rs_sb"], 1)
                for k in range(2):
                    dve.wait_ge(S["rs_sb"], 2 * b + k + 1)
                    v.tensor_tensor(x3[:, k:H:2, :], rs[:, :, k, :], x2[:, k:H:2, :], ALU.add).then_inc(S["x3_sb"], 1)

            def offsets(b):
                dve.wait_ge(S["offT_ps"], b + 1)
                for t in range(T):
                    dve.wait_ge(gathered[t], 144 * b)
                v.tensor_copy(offT[:].rearrange("p a b -> p (a b)"), PC[:, 0:T * 27]).then_inc(S["offT_sb"], 1)
                dve.wait_ge(S["offT_sb"], b + 1)
                base = w("base").rearrange("p (t k) -> p t k", t=T)
                n = IX_STEPS * b
                v.tensor_tensor(uu[:], offT[:, :, 0:18], base, ALU.add).then_inc(S["ixs"], 1)
                dve.wait_ge(S["ixs"], n + 1)
                v.tensor_scalar(uu[:], uu[:], 0.0, float(H + 1), ALU.max, ALU.min).then_inc(S["ixs"], 1)
                dve.wait_ge(S["ixs"], n + 2)
                v.tensor_scalar(rr[:], uu[:], ROUND, None, ALU.add).then_inc(S["ixs"], 1)
                dve.wait_ge(S["ixs"], n + 3)
                v.tensor_scalar(rr[:], rr[:], ROUND, None, ALU.subtract).then_inc(S["ixs"], 1)
                dve.wait_ge(S["ixs"], n + 4)
                v.tensor_tensor(gg[:], rr[:], uu[:], ALU.is_gt).then_inc(S["ixs"], 1)
                dve.wait_ge(S["ixs"], n + 5)
                v.tensor_tensor(rr[:], rr[:], gg[:], ALU.subtract).then_inc(S["ixs"], 1)
                dve.wait_ge(S["ixs"], n + 6)
                v.tensor_scalar(u0[:], rr[:], float(H), None, ALU.min).then_inc(S["ixs"], 1)
                dve.wait_ge(S["ixs"], n + 7)
                v.scalar_tensor_tensor(ixf[:], u0[:, :, 0:18:2], float(QS), u0[:, :, 1:18:2], ALU.mult, ALU.add)\
                    .then_inc(S["ixs"], 1)
                dve.wait_ge(S["ixs"], n + 8)
                v.tensor_copy(ix[:], ixf[:].rearrange("p a b -> p (a b)")).then_inc(S["ix_sb"], 1)
                v.tensor_tensor(w1_[:], uu[:], u0[:], ALU.subtract).then_inc(S["ixs"], 1)
                dve.wait_ge(S["ixs"], n + 9)
                m = 5 * b
                v.tensor_scalar(w0_[:], w1_[:], -1.0, 1.0, ALU.mult, ALU.add).then_inc(S["wq_sb"], 1)
                dve.wait_ge(S["em_sb"], b + 1)
                dve.wait_ge(S["wq_sb"], 5 * b + 1)
                v.tensor_tensor(ay[:, 0], w0_[:, :, 0:18:2], em[:], ALU.mult).then_inc(S["wq_sb"], 1)
                v.tensor_tensor(ay[:, 1], w1_[:, :, 0:18:2], em[:], ALU.mult).then_inc(S["wq_sb"], 1)
                dve.wait_ge(S["wq_sb"], 5 * b + 3)
                for g in range(3):
                    wx = (w0_, w1_)[g % 2]
                    i = v.tensor_tensor(wq[:, :, :, g], ay[:, g // 2], wx[:, :, 1:18:2], ALU.mult)
                    if g != 1:
                        i.then_inc(S["wq_sb"], 1)

            def deformed(b):
                dve.wait_ge(S["wq_sb"], 5 * b + 5)
                dve.wait_ge(S["wq3_sb"], b + 1)
                for t in range(T):
                    dve.wait_ge(gathered[t], 144 * b + 144)
                    v.tensor_tensor(Gw[:].rearrange("p k (g c) -> p k g c", g=4),
                                    G[:, t].rearrange("p k (g c) -> p k g c", g=4),
                                    wq[:, t].unsqueeze(3).to_broadcast([128, 9, 4, CB]), ALU.mult).then_inc(S["gw_sb"], 1)
                    dve.wait_ge(S["gw_sb"], T * b + t + 1)
                    v.tensor_tensor(G2[:], Gw[:, :, 0:64], Gw[:, :, 64:128], ALU.add).then_inc(S["g2_sb"], 1)
                    dve.wait_ge(S["g2_sb"], T * b + t + 1)
                    if t >= 2:
                        dve.wait_ge(S["tr_ps"], T * b + t - 1)
                    v.tensor_tensor(sm[:, t % 2].rearrange("p (k c) -> p k c", k=9), G2[:, :, 0:32],
                                    G2[:, :, 32:64], ALU.add).then_inc(S["sm_sb"], 1)
                dve.wait_ge(S["w3_ps"], b + 1)
                v.scalar_tensor_tensor(o[:], PD[:], bns[:, 2:3], x3[:].rearrange("p a b -> p (a b)"), ALU.mult, ALU.add)\
                    .then_inc(S["o_sb"], 1)

            def image(b, first):
                linear_attention(b)
                position_attention(b)
                if not first:
                    deformed(b - 1)
                scans(b)
                offsets(b)

            image(0, True)
            with dve.Fori(1, B) as b:
                image(b, False)
            deformed(B - 1)


def _columns(i, np):
    f = np.float32

    def full(a, rows=None):
        a = np.asarray(a, f)
        a = a.reshape(a.shape[0], -1)
        z = np.zeros((128, a.shape[1]), f)
        z[:a.shape[0]] = a
        return z

    def four(a):
        return np.concatenate([a] * 4, axis=0)

    l0 = lambda n: i["L0_conv_" + n]
    l1 = lambda n: i["L1_conv_" + n]
    l2 = lambda n: i["L2_conv_" + n]
    l3 = lambda n: i["L3_conv_" + n]
    r = {}
    r["wkv"] = np.concatenate([l0("kw").T, l0("vw").T], axis=1)
    r["kvb"] = np.broadcast_to(np.concatenate([l0("kb"), l0("vb")])[None, :], (128, 2 * C))
    r["qwT"], r["rwT"] = l0("qw").T, l0("rw").T
    r["c1T"] = l0("c1w").transpose(1, 2, 3, 0).reshape(C, -1)
    r["c2T"] = l0("c2w").transpose(1, 2, 3, 0).reshape(C, -1)
    r["ident"] = np.eye(128, dtype=f)
    pw = np.zeros((C, 3, RS), f)
    pwb = np.zeros((RS, 3), f)
    pwb[0, 0] = pwb[0, 2] = 1.0
    for n in range(3):
        pw[:, n, 1:] = l1(f"c{n + 1}_pw_w")[:, :, 0, 0].T
        pwb[1:, n] = l1(f"c{n + 1}_pw_b")
    r["pwT"], r["pwb"] = full(pw), full(pwb)
    r["dww"] = np.concatenate([l1(f"c{n}_dw_w").reshape(C, 9) for n in (1, 2, 3)], axis=1)
    r["dwb"] = np.stack([l1(f"c{n}_dw_b") for n in (1, 2, 3)], axis=1)
    r["coT"] = np.roll(full(np.concatenate([l1("co_b")[None, :], l1("co_w")[:, :, 0, 0].T], axis=0)), 32, axis=0)
    densel = np.zeros((128, C), f)
    densel[32] = 1.0
    r["densel"] = densel
    win = l2("w_in").T
    r["winY"] = np.concatenate([win[:, :INNER]] * 2, axis=1)
    r["winG"] = np.concatenate([win[:, INNER:]] * 2, axis=1)
    dwk = l2("w_dw").reshape(INNER, 3, 3)
    r["dwk"] = np.concatenate([dwk.reshape(INNER, 9), dwk.transpose(0, 2, 1).reshape(INNER, 9)], axis=0)
    for n in ("wd", "wv"):
        z = np.zeros((128, 128), f)
        z[:INNER, :INNER] = l2("row_" + n).T
        z[INNER:, INNER:] = l2("col_" + n).T
        r[n] = z
    r["wout"] = np.concatenate([l2("w_out").T] * 2, axis=0)
    r["bd"] = np.concatenate([l2("row_bd"), l2("col_bd")])[:, None]
    r["bv"] = np.concatenate([l2("row_bv"), l2("col_bv")])[:, None]
    r["w1T"] = np.concatenate([l3("w1").T] * 4, axis=1)
    wo = np.zeros((4, CB, 4, 27), f)
    for g in range(4):
        for q in range(4):
            ky, kx = 2 * (q // 2) + g // 2, 2 * (q % 2) + g % 2
            if ky < 3 and kx < 3:
                wo[g, :, q, :] = l3("woff")[:, :, ky, kx].T
    r["woff"] = wo.reshape(128, 4 * 27)
    w2 = l3("w2").reshape(CB, CB, 3, 3).transpose(2, 3, 1, 0).reshape(3, 96, CB)
    r["w2T"] = full(w2.transpose(1, 0, 2))
    r["w3T"] = np.roll(full(l3("w3").T), 96, axis=0)
    p = np.arange(128)
    base = np.zeros((128, T, 9, 2), f)
    for t in range(T):
        for k in range(9):
            base[:, t, k, 0] = 4 * t + p // W + k // 3
            base[:, t, k, 1] = p % W + k % 3
    r["base"] = full(base)
    for n in ("qb", "rb", "c1b", "c2b"):
        r[n] = l0(n)[:, None]
    r["gnw"], r["gnb"] = l2("gn_w")[:, None], l2("gn_b")[:, None]
    r["boff"] = full(l3("boff")[:, None])
    for n in (1, 2, 3):
        c = [l3(f"bn{n}_{s}") for s in "gbmv"] + ([l3("dcn_b")] if n == 2 else [])
        a = np.stack(c, axis=1)
        r[f"bn{n}"] = four(a) if a.shape[0] == CB else a
    return np.ascontiguousarray(np.concatenate([np.asarray(r[n], f).reshape(128, k) for n, k in FIELDS], axis=1))


def kernel(**inputs):
    import numpy as np
    import concourse.bacc as bacc
    from concourse.bass_utils import run_bass_kernel_spmd as run

    nc = bacc.Bacc("TRN2", target_bir_lowering=False, num_devices=1)
    ins = {k: np.asarray(a) for k, a in inputs.items()}
    x = np.ascontiguousarray(ins["x"].reshape(B, C, N))
    weights = _columns(ins, np)
    dx = nc.dram_tensor("in_x", x.shape, F32, kind="ExternalInput").ap()
    dw = nc.dram_tensor("in_weights", weights.shape, F32, kind="ExternalInput").ap()
    table = nc.dram_tensor("quad_table", (QT * QP, 128), F32, kind="Internal").ap()
    do = nc.dram_tensor("out_x", (B, C, N), F32, kind="ExternalOutput").ap()
    build(nc, dx, dw, table, do)
    r = run(nc, [{"in_x": x, "in_weights": weights}], core_ids=[0])
    return r.results[0]["out_x"].reshape(B, C, H, W)
```

```python
from contextlib import ExitStack

import concourse.bass as bass
from concourse import mybir

F32 = mybir.dt.float32
F32R = mybir.dt.float32r
U32 = mybir.dt.uint32
ALU = mybir.AluOpType
ACT = mybir.ActivationFunctionType
AX_X = mybir.AxisListType.X

B, C, H, W = 8, 128, 32, 32
N = H * W
HALF = N // 2
HR = H // 2
T = N // 128
R = C // 8
DIL = (1, 3, 5)
PADD = max(DIL)
CB = 32
NT = 9
QS = W + 2
QT = 11
QP = (H + 1) * QS // QT
INNER = 64
h2, w2 = H // 2, W // 2
NP = h2 * w2
EPS_L0, EPS_GN, EPS_BN = 1e-6, 1e-5, 1e-5
ROUND = float(2 ** 23)

FIELDS = [("wkv", 2 * C), ("kvb", 2 * C), ("qwT", C), ("rwT", C), ("ident", C),
          ("pwT", 3 * R), ("pwS", 3 * 96), ("dww", 27), ("dwb", 3), ("pwb", 3), ("sel", 96), ("coT", C), ("densel", C),
          ("winY", C), ("winG", C), ("dwk", 9), ("wd", C), ("wv", C), ("wout", C),
          ("w1T", C), ("woff", 4 * 27), ("w2T", 3 * CB), ("w3T", C), ("base", T * 18),
          ("qb", 1), ("rb", 1), ("c1b", 1), ("c2b", 1), ("gnw", 1), ("gnb", 1), ("bd", 1), ("bv", 1), ("boff", 1),
          ("bn1", 4), ("bn2", 5), ("bn3", 4)]
AT = {}
_n = 0
for _name, _len in FIELDS:
    AT[_name] = (_n, _len)
    _n += _len
WCOLS = _n

ORDER = [
    ("taps", 2, 0, 2), ("keys", 1, 0, 1), ("taps", 2, 2, 1), ("queries", 1, 0, 1), ("tapsum", 2, 0, 3),
    ("norms", 1, 0, 1), ("maxima", 2, 0, 2), ("keyvalue", 1, 0, 1), ("maxima", 2, 2, 4), ("fold", 1, 0, 1),
    ("maxima", 2, 6, 2), ("maxrow", 2, 0, 1), ("denominator", 1, 0, 1), ("weigh", 2, 0, 3), ("numerator", 1, 0, 1),
    ("weigh", 2, 3, 3), ("split_x", 0, 0, 1), ("weigh", 2, 6, 2), ("conv1", 1, 0, 1), ("attend", 2, 0, 1),
    ("conv1", 1, 1, 8), ("sample", 3, 0, 1), ("conv1", 1, 9, 3), ("sample", 3, 1, 1), ("conv1", 1, 12, 1),
    ("sample", 3, 2, 1), ("conv1", 1, 13, 3), ("mean", 2, 0, 1), ("variance", 2, 0, 1), ("conv1", 1, 16, 2),
    ("project", 2, 0, 1), ("conv2", 1, 0, 7), ("deltas", 2, 0, 1), ("conv2", 1, 7, 2), ("scan", 2, 0, 1),
    ("sample", 3, 3, 2), ("resize", 2, 0, 1), ("hidden", 2, 0, 1), ("conv2", 1, 9, 6), ("sample", 3, 5, 2),
    ("conv2", 1, 15, 2), ("sample", 3, 7, 1), ("conv2", 1, 17, 1), ("residual", 1, 0, 1), ("deform", 3, 0, 1),
    ("offset", 2, 0, 1), ("quads", 2, 0, 1), ("indices", 2, 0, 1)]
LAST_LAG = 3
PARTS = 9


def build(nc, x, weights, convs, table, out):
    with ExitStack() as ctx:
        def sb(name, shape, dt=F32):
            return ctx.enter_context(nc.sbuf_tensor(name, shape, dt))

        def sem(name):
            return ctx.enter_context(nc.semaphore(name))

        wt = sb("wt", [128, WCOLS])

        def w(name):
            a, n = AT[name]
            return wt[:, a:a + n]

        def vec(name, i=0, p=128):
            a, n = AT[name]
            return wt[0:p, a + i:a + i + 1]

        PA = ctx.enter_context(nc.psum_tensor("PA", [128, N], F32))
        PB = ctx.enter_context(nc.psum_tensor("PB", [128, N], F32))
        PC = ctx.enter_context(nc.psum_tensor("PC", [128, N], F32))
        PD = ctx.enter_context(nc.psum_tensor("PD", [128, N], F32))
        PAB = (PA, PB)

        wkv = sb("wkv", [128, 2, 2 * C], F32R)
        qw = sb("qw", [128, 2, C], F32R)
        c1 = sb("c1", [128, 2, 9 * C], F32R)
        c2 = sb("c2", [128, 2, 9 * C], F32R)
        identr = sb("identr", [128, 128], F32R)
        wf = sb("wf", [128, 3, 3, 3, 2 * R], F32R)
        ones = sb("ones", [128, 128])
        mean = sb("mean", [128, 128])
        fbias = sb("fbias", [96, 3])
        bns = sb("bns", [128, 3])
        bnb = sb("bnb", [128, 3])
        bnt = sb("bnt", [128, 3])
        bnr = sb("bnr", [128, 3])
        xq = sb("xq", [128, 2, N], F32R)
        kvt = sb("kvt", [128, T, 1 + 2 * C])
        ksqj = sb("ksqj", [128, C])
        kss = sb("kss", [128, T])
        krn = sb("krn", [128, T])
        kv = sb("kv", [128, C + 1])
        ksc = sb("ksc", [128, 1])
        ks = sb("ks", [128, 2, 128], F32R)
        m2 = sb("m2", [128, 2, C], F32R)
        rv = sb("rv", [128, 1])
        nq = sb("nq", [128, N])
        xres = nq
        den = sb("den", [128, N])
        qsq = den
        xin = den
        ob = den
        attn = sb("attn", [128, 2, H + 2, W + 2], F32R)
        x1 = sb("x1", [128, H, W])
        x1p = sb("x1p", [128, 2, H, W + 2 * PADD], F32R)
        Y = sb("Y", [96, 3, H, W])
        f2 = sb("f2", [96, N], F32R)
        f3 = sb("f3", [96, N], F32R)
        rowbuf = sb("rowbuf", [128, N])
        f1, off, h3 = rowbuf[0:32], rowbuf[64:91], rowbuf[96:128]
        f1T = sb("f1T", [128, T, 32])
        mx = sb("mx", [128, T])
        nm = sb("nm", [128, T, 65], F32R)
        work = sb("work", [128, 4 * N])
        E = work[:, 0:2 * N].rearrange("p (a n) -> p a n", a=2)
        U, rden = work[:, 2 * N:3 * N], work[:, 3 * N:4 * N]
        x2 = sb("x2", [128, H, W])
        place = [0]

        def temp(cols):
            a = place[0]
            place[0] += cols
            return work[:, a:a + cols]

        def image(ap, width):
            return ap.rearrange("p (a b) -> p a b", b=width)

        p1 = image(temp(h2 * W), W)
        p2, y0, y1, y2, es, gate, dl, bb, sf, sr, ss, yg = (temp(NP) for _ in range(12))
        st = sb("st", [128, 2, 6])
        mv = sb("mv", [128, 2])
        gs = sb("gs", [128, 8])
        ypad = sb("ypad", [128, h2 + 2, w2 + 2])
        af = sb("af", [128, h2, w2])
        ab = sb("ab", [128, h2, w2])
        zp = sb("zp", [128, h2, w2 + 2])
        up = sb("up", [128, h2 + 2, W])
        x3 = sb("x3", [128, H, W])
        res = sb("res", [128, N])
        S4 = sb("S4", [128, H + 2, W + 2])
        offT = sb("offT", [128, T, 27])
        quads = work[0:QP, 0:QT * 128].rearrange("p (t c) -> p t c", t=QT)
        uu = sb("uu", [128, T, 18])
        rr = sb("rr", [128, T, 18])
        gg = sb("gg", [128, T, 18])
        u0 = sb("u0", [128, T, 18])
        wt1 = sb("wt1", [128, T, 18])
        wt0 = sb("wt0", [128, T, 18])
        ixf = sb("ixf", [128, T, 9])
        ix = sb("ix", [128, T * 9], U32)
        em = sb("em", [128, T, 9])
        ay = sb("ay", [128, 2, T, 9])
        wq = sb("wq", [128, T, 9, 4])
        G = sb("G", [128, T, 9, 128])
        sm = sb("sm", [128, 2, 9 * CB])
        sT = sb("sT", [96, 3, HALF])
        TAPS = ((1, PA), (2, PB), (0, PA))
        TAPSUM = ((96, PC), (96, PB), (32, PA))
        QBANKS = (PA[:, 0:HALF], PA[:, HALF:N], PC[:, 0:HALF])
        PS_DCN = (PB[0:CB, HALF:N], PB[0:CB, 0:HALF])
        cstage = G[:].rearrange("p t k c -> p (t k c)")[:, 0:18 * C]
        wstage = image(work[:, 0:27 * R], R)

        S = {}
        for n in ("w_in c_in x_in xres_in zeroed consts bias_ps bnv_sb bnr_sb wh_sb wl_sb init_v init_a "
                  "xh_sb xl_sb kvt_ps kvt_sb ksq_sb kss_rt krn_sb kn_sb q_ps qh_sb ql_sb qsq_sb nq_ps nq_sb "
                  "kv_ps kv_sb ksc_sb ksh_sb ksl_sb m2_ps m2h_sb m2l_sb rv_sb kq_ps den_sb rec_sb m2q_ps num_sb attn_raw "
                  "ah_sb al_sb c1_ps hh_sb hl_sb c2_ps hx_sb x1_sb x1h_sb x1l_sb "
                  "tap_ps Y_sb f_ps fh_sb fl_sb f1T_ps f1T_sb s_ps mx_sb nmh_sb nml_sb nmrow_ps nmrow_sb st_ps e_sb "
                  "pv_ps U_sb co_ps rd_sb av_sb x2_sb stats_sb p1_sb p2_sb stat_sb mu_ps dm_sb dev_sb var_ps gnv_sb gn_rt "
                  "gn_sb y0_sb yw_ps ypad_sb gate_sb y1_sb es_sb y2_sb dv_ps dl_sb scan_in scan_sb ss_sb yg_sb z_ps "
                  "zp_sb up_sb upe_sb rs_sb x3_sb w1_ps s4_sb off_ps off_sb offT_ps offT_sb tab_ps quads_sb table_in "
                  "ixs em_sb ix_sb wq_sb wq3_sb res_sb gw_sb g2_sb sm_sb tr_ps sT_sb dcn_ps h3_sb w3_ps o_sb ob_sb stored").split():
            S[n] = sem("s_" + n)
        gathered = [sem(f"s_gathered{t}") for t in range(T)]

        def rows(ap, half):
            return ap[:, half * HALF:(half + 1) * HALF]

        def wait(eng, name, value):
            if not (isinstance(value, int) and value <= 0):
                eng.wait_ge(S[name], value)

        def upto(count):
            return min(count, B) if isinstance(count, int) else count

        def run(eng, stages):
            def iteration(i):
                for name, lag, first, count in ORDER:
                    b = i - lag
                    if name in stages and not (isinstance(b, int) and not 0 <= b < B):
                        for part in range(first, first + count):
                            stages[name](b, part)

            for i in range(LAST_LAG + 1):
                iteration(i)
            with eng.Fori(LAST_LAG + 1, B) as i:
                iteration(i)
            for i in range(B, B + LAST_LAG):
                iteration(i)

        block = ctx.enter_context(nc.Block())

        @block.sync
        def _(sp):
            sp.dma_start(wt[:], weights).then_inc(S["w_in"], 16)
            for i in range(B + LAST_LAG):
                if i < B:
                    if i:
                        sp.wait_ge(S["attn_raw"], i)
                    sp.dma_start(xin[:], x[i]).then_inc(S["x_in"], 16)
                if i == 0:
                    sp.dma_start(cstage, convs).then_inc(S["c_in"], 16)
                b = i - 1
                if 0 <= b < B:
                    sp.wait_ge(S["al_sb"], b + 1)
                    sp.dma_start(xres[:], x[b]).then_inc(S["xres_in"], 16)
                b = i - 3
                if 0 <= b < B:
                    sp.wait_ge(S["ob_sb"], b + 1)
                    sp.dma_start(out[b], ob[:]).then_inc(S["stored"], 16)
                b = i - 2
                if 0 <= b < B:
                    sp.wait_ge(S["quads_sb"], 3 * b + 3)
                    if b:
                        for t in range(T):
                            sp.wait_ge(gathered[t], 144 * b)
                    sp.dma_start(table.rearrange("(t p) c -> p t c", p=QP), quads).then_inc(S["table_in"], 16)
            sp.wait_ge(S["stored"], 16 * B)

        @block.gpsimd
        def _(pool):
            for buf in (attn, x1p, nm):
                nc.gpsimd.memset(buf[:].bitcast(F32), 0.0).then_inc(S["zeroed"], 1)
            for buf in (Y, ypad, S4, af, ab):
                nc.gpsimd.memset(buf[:], 0.0).then_inc(S["zeroed"], 1)
            nc.gpsimd.memset(ones[:], 1.0).then_inc(S["zeroed"], 1)
            nc.gpsimd.memset(mean[:], 1.0 / C).then_inc(S["zeroed"], 1)
            nc.gpsimd.memset(kvt[:], 1.0).then_inc(S["zeroed"], 1)

            def indices(b, _):
                wait(pool, "table_in", 16 * b + 16)
                wait(pool, "ix_sb", b + 1)
                wait(pool, "gw_sb", T * b)
                wait(pool, "wq_sb", 5 * b + 5)
                nc.gpsimd.tensor_tensor(wq[:, :, :, 3], ay[:, 1], wt1[:, :, 1:18:2], ALU.mult).then_inc(S["wq3_sb"], 1)
                for t in range(T):
                    for k in range(NT):
                        pool.indirect_dma_start(G[:, t, k, :], None, table, bass.IndirectOffsetOnAxis(
                            ap=ix[:, NT * t + k:NT * t + k + 1], axis=0)).then_inc(gathered[t], 16)

            run(pool, {"indices": indices})

        @block.tensor
        def _(pe):
            mm = nc.tensor.matmul
            ident = w("ident")

            def product(out, lhsT, rhs, start=True, stop=True):
                for n, (i, j) in enumerate(((0, 0), (0, 1), (1, 0))):
                    m = mm(out, lhsT(i), rhs(j), start=start and n == 0, stop=stop and n == 2)
                return m

            pe.wait_ge(S["w_in"], 16)
            for i in range(3):
                m = mm(PA[0:96, i:i + 1], w("pwS")[:, i * 96:(i + 1) * 96], w("dwb")[:, i:i + 1], start=True, stop=True)
            m.then_inc(S["bias_ps"], 1)
            pe.wait_ge(S["zeroed"], 11)
            pe.wait_ge(S["init_v"], 1)
            pe.wait_ge(S["init_a"], 1)

            def keys(b, _):
                wait(pe, "xh_sb", b + 1)
                wait(pe, "xl_sb", b + 1)
                wait(pe, "x1_sb", 2 * b)
                for j in range(4):
                    if j >= 2:
                        wait(pe, "kvt_sb", 4 * b + j - 1)
                    for t in (2 * j, 2 * j + 1):
                        m = product(PD[:, (j % 2) * HALF + (t % 2) * 256:(j % 2) * HALF + (t % 2 + 1) * 256],
                                    lambda i: xq[:, i, 128 * t:128 * (t + 1)], lambda i: wkv[:, i, :])
                    m.then_inc(S["kvt_ps"], 1)

            def queries(b, _):
                wait(pe, "kvt_sb", 4 * b + 4)
                for half in range(2):
                    m = product(rows(PD, half), lambda i: qw[:, i, :], lambda i: rows(xq[:, i, :], half))
                m.then_inc(S["q_ps"], 1)

            def norms(b, _):
                wait(pe, "qsq_sb", b + 1)
                wait(pe, "ql_sb", b + 1)
                for half in range(2):
                    m = mm(rows(PD, half), ones[:], rows(qsq, half), start=True, stop=True)
                m.then_inc(S["nq_ps"], 1)

            def keyvalue(b, _):
                wait(pe, "kn_sb", b + 1)
                wait(pe, "nq_sb", b + 1)
                for t in range(T):
                    mm(PD[:, 0:C + 1], kvt[:, t, 1 + C:], kvt[:, t, 0:1 + C], start=t == 0, stop=t == T - 1)
                for t in range(T):
                    m = mm(PD[:, HALF:HALF + 1], kvt[:, t, 1:1 + C], ones[:, 0:1], start=t == 0, stop=t == T - 1)
                m.then_inc(S["kv_ps"], 1)

            def fold(b, _):
                wait(pe, "kv_sb", b + 1)
                wait(pe, "ksc_sb", b + 1)
                mm(PD[:, 0:C], kv[:, 1:1 + C], w("rwT"), start=True, stop=True)
                mm(PD[:, HALF:HALF + 1], w("rwT"), kv[:, 0:1], start=True, stop=True).then_inc(S["m2_ps"], 1)

            def denominator(b, _):
                wait(pe, "ksl_sb", b + 1)
                wait(pe, "m2l_sb", b + 1)
                wait(pe, "rv_sb", b + 1)
                for half in range(2):
                    m = product(rows(PD, half), lambda i: ks[:, i, :], lambda i: rows(xq[:, i, :], half))
                m.then_inc(S["kq_ps"], 1)

            def numerator(b, _):
                wait(pe, "den_sb", b + 1)
                for half in range(2):
                    m = product(rows(PD, half), lambda i: m2[:, i, :], lambda i: rows(xq[:, i, :], half))
                m.then_inc(S["m2q_ps"], 1)

            def dense(cw, part):
                half, tap = divmod(part, PARTS)
                dy, dx = divmod(tap, 3)
                return product(rows(PD, half), lambda i: cw[:, i, tap * C:(tap + 1) * C],
                               lambda i: attn[:, i, dy + HR * half:dy + HR * half + HR, dx:dx + W],
                               start=tap == 0, stop=tap == PARTS - 1)

            def conv1(b, part):
                if part == 0:
                    wait(pe, "ah_sb", b + 1)
                    wait(pe, "al_sb", b + 1)
                m = dense(c1, part)
                if part % PARTS == PARTS - 1:
                    m.then_inc(S["c1_ps"], 1)

            def conv2(b, part):
                if part == 0:
                    wait(pe, "hh_sb", 2 * b + 2)
                    wait(pe, "hl_sb", 2 * b + 2)
                m = dense(c2, part)
                if part % PARTS == PARTS - 1:
                    m.then_inc(S["c2_ps"], 1)

            def taps(b, n):
                i, ps = TAPS[n]
                wait(pe, "x1h_sb", b + 1)
                wait(pe, "x1l_sb", b + 1)
                if n == 0:
                    wait(pe, "quads_sb", 3 * b)
                    wait(pe, "offT_sb", b)
                    wait(pe, "o_sb", b - 1)
                if n == 2:
                    wait(pe, "Y_sb", 9 * b + 3)
                for half in range(2):
                    for dx in range(3):
                        c0 = PADD + (dx - 1) * DIL[i]
                        for part in range(2):
                            m = mm(ps[0:96, half * HALF:(half + 1) * HALF], wf[:, i, dx].rearrange("p y r -> p (y r)"),
                                   x1p[:, part, HR * half:HR * half + HR, c0:c0 + W],
                                   start=dx == 0 and part == 0, stop=dx == 2 and part == 1)
                m.then_inc(S["tap_ps"], 1)

            def tapsum(b, n):
                i, _ = TAPS[n]
                m_out, ps = TAPSUM[n]
                wait(pe, "Y_sb", 9 * b + 3 * n + 3)
                for half in range(2):
                    m = mm(ps[0:m_out, half * HALF:(half + 1) * HALF], w("sel")[0:96, 0:m_out],
                           Y[:, i, HR * half:HR * half + HR, :], start=True, stop=True)
                m.then_inc(S["f_ps"], 1)

            def maxima(b, t):
                if t == 0:
                    wait(pe, "fh_sb", 3 * b + 3)
                    wait(pe, "fl_sb", 2 * b + 2)
                if t >= 2:
                    wait(pe, "mx_sb", T * b + t - 1)
                for half in range(2):
                    m = mm(rows(PAB[t % 2], half), f2[:, 128 * t:128 * (t + 1)], rows(f3, half), start=True, stop=True)
                m.then_inc(S["s_ps"], 1)
                if t == 1:
                    for j in range(T):
                        m = nc.tensor.transpose(PC[:, j * 32:(j + 1) * 32], f1[:, 128 * j:128 * (j + 1)], ident[0:32, 0:32])
                    m.then_inc(S["f1T_ps"], 1)

            def maxrow(b, _):
                wait(pe, "nml_sb", b + 1)
                wait(pe, "f1T_sb", b + 1)
                for t in range(T):
                    m = mm(PC[0:65, 128 * t:128 * (t + 1)], nm[:, t, :], identr[:], start=True, stop=True)
                m.then_inc(S["nmrow_ps"], 1)

            def weigh(b, j):
                def values(j):
                    wait(pe, "e_sb", T * b + j + 1)
                    for half in range(2):
                        m = mm(PC[32 * (j % 4):32 * (j % 4) + 32, half * HALF:(half + 1) * HALF], f1T[:, j, :],
                               rows(E[:, j % 2, :], half), start=j < 4, stop=j >= 4)
                    m.then_inc(S["pv_ps"], 1)

                if j == 0:
                    wait(pe, "nmrow_sb", 2 * b + 2)
                if j >= 2:
                    wait(pe, "e_sb", T * b + j - 1)
                for half in range(2):
                    m = mm(rows(PAB[j % 2], half), f3[:, 128 * j:128 * (j + 1)], rows(f2, half), start=True, stop=True)
                m.then_inc(S["st_ps"], 1)
                if j >= 1:
                    values(j - 1)
                if j == T - 1:
                    values(j)

            def attend(b, _):
                wait(pe, "U_sb", b + 1)
                for ps, name in ((PA, "coT"), (PB, "densel")):
                    for half in range(2):
                        m = mm(rows(ps, half), w(name), rows(U, half), start=True, stop=True)
                m.then_inc(S["co_ps"], 1)

            def mean_(b, _):
                wait(pe, "stat_sb", b + 1)
                mm(PC[:, 0:1], mean[:], mv[:, 0:1], start=True, stop=True).then_inc(S["mu_ps"], 1)

            def variance(b, _):
                wait(pe, "dev_sb", b + 1)
                mm(PC[:, HALF:HALF + 1], mean[:], gs[:, 1:2], start=True, stop=True).then_inc(S["var_ps"], 1)

            def project(b, _):
                wait(pe, "y0_sb", b + 1)
                mm(PA[:, 0:NP], w("winY"), y0, start=True, stop=True)
                mm(PA[:, HALF:HALF + NP], w("winG"), y0, start=True, stop=True).then_inc(S["yw_ps"], 1)

            def deltas(b, _):
                wait(pe, "y2_sb", b + 1)
                wait(pe, "gate_sb", b + 1)
                mm(PA[:, 0:NP], w("wd"), y2, start=True, stop=True)
                mm(PA[:, HALF:HALF + NP], w("wv"), y2, start=True, stop=True).then_inc(S["dv_ps"], 1)

            def scan(b, _):
                wait(pe, "yg_sb", 2 * b + 2)
                mm(PC[:, 0:NP], w("wout"), yg, start=True, stop=True).then_inc(S["z_ps"], 1)

            def hidden(b, _):
                wait(pe, "x3_sb", 2 * b + 2)
                x3f = x3[:].rearrange("p a b -> p (a b)")
                for half in range(2):
                    m = mm(rows(PA, half), w("w1T"), rows(x3f, half), start=True, stop=True)
                m.then_inc(S["w1_ps"], 1)

            def offset(b, _):
                wait(pe, "s4_sb", 4 * b + 4)
                for half in range(2):
                    for q4 in range(4):
                        by, bx = 2 * (q4 // 2), 2 * (q4 % 2)
                        m = mm(PC[0:27, half * HALF:(half + 1) * HALF], w("woff")[:, q4 * 27:(q4 + 1) * 27],
                               S4[:, by + HR * half:by + HR * half + HR, bx:bx + W], start=q4 == 0, stop=q4 == 3)
                m.then_inc(S["off_ps"], 1)

            def quads_(b, _):
                s4f = S4[:].rearrange("p a b -> p (a b)")
                for t in range(QT):
                    if t == 8:
                        wait(pe, "off_sb", b + 1)
                    m = nc.tensor.transpose(QBANKS[t // 4][0:QP, (t % 4) * 128:(t % 4 + 1) * 128],
                                            s4f[:, QP * t:QP * (t + 1)], ident)
                    if t % 4 == 3 or t == QT - 1:
                        m.then_inc(S["tab_ps"], 1)
                for t in range(T):
                    m = nc.tensor.transpose(PC[:, HALF + t * 27:HALF + (t + 1) * 27], off[:, 128 * t:128 * (t + 1)],
                                            ident[64:91, 64:91])
                m.then_inc(S["offT_ps"], 1)

            def sample(b, t):
                if t == 0:
                    wait(pe, "rd_sb", upto(b + 2))
                wait(pe, "sm_sb", T * b + t + 1)
                if t >= 2:
                    wait(pe, "sT_sb", T * b + t - 1)
                if t == 5:
                    wait(pe, "h3_sb", 2 * b + 1)
                ps = PB[0:96, (t % 2) * HALF:(t % 2) * HALF + 384]
                for g in range(3):
                    m = nc.tensor.transpose(ps[:, g * 128:(g + 1) * 128], sm[:, t % 2, g * 96:(g + 1) * 96], ident)
                m.then_inc(S["tr_ps"], 1)

            def deform(b, _):
                wait(pe, "h3_sb", 2 * b + 2)
                for half in range(2):
                    m = mm(rows(PB, half), w("w3T")[96:128, :], rows(h3, half), start=True, stop=True)
                m.then_inc(S["w3_ps"], 1)

            def sample_and_mix(b, t):
                sample(b, t)
                if t % 4 == 3:
                    half = t // 4
                    wait(pe, "sT_sb", T * b + t + 1)
                    for g in range(3):
                        m = mm(PS_DCN[half], w("w2T")[0:96, g * CB:(g + 1) * CB], sT[:, g, :], start=g == 0, stop=g == 2)
                    m.then_inc(S["dcn_ps"], 1)

            run(pe, {"taps": taps, "keys": keys, "queries": queries, "tapsum": tapsum, "norms": norms,
                     "keyvalue": keyvalue, "maxima": maxima, "fold": fold, "denominator": denominator,
                     "maxrow": maxrow, "weigh": weigh, "numerator": numerator, "attend": attend, "conv1": conv1,
                     "conv2": conv2, "mean": mean_, "variance": variance, "project": project, "deltas": deltas,
                     "scan": scan, "hidden": hidden, "offset": offset, "quads": quads_, "sample": sample_and_mix,
                     "deform": deform})

        @block.scalar
        def _(act):
            a_ = nc.scalar.activation

            act.wait_ge(S["w_in"], 16)
            for dst, src in ((wkv[:, 0, :], w("wkv")), (qw[:, 0, :], w("qwT")), (identr[:], w("ident"))):
                m = a_(dst, src, ACT.Copy)
                m.then_inc(S["wh_sb"], 1)
            act.wait_ge(S["c_in"], 16)
            for n, cw in enumerate((c1, c2)):
                a_(cw[:, 0, :], cstage[:, n * 9 * C:(n + 1) * 9 * C], ACT.Copy).then_inc(S["wh_sb"], 1)
            act.wait_ge(S["bnv_sb"], 3)
            a_(bnt[:], bnt[:], ACT.Sqrt).then_inc(S["bnr_sb"], 1)
            act.wait_ge(S["wh_sb"], 5)
            act.wait_ge(S["init_v"], 1)
            act.wait_ge(S["zeroed"], 11)
            a_(ksqj[:, 0:1], ones[:, 0:1], ACT.Copy).then_inc(S["init_a"], 1)

            def split_x(b, _):
                wait(act, "x_in", 16 * b + 16)
                wait(act, "m2q_ps", b)
                a_(xq[:, 0, :], xin[:], ACT.Copy).then_inc(S["xh_sb"], 1)

            def keys(b, _):
                for t in range(T):
                    wait(act, "kvt_sb", 4 * b + t // 2 + 1)
                    a_(ksqj[:], kvt[:, t, 1:1 + C], ACT.Square, accum_out=kss[:, t:t + 1]).then_inc(S["ksq_sb"], 1)
                    act.wait_ge(S["ksq_sb"], T * b + t + 1)

            def queries(b, _):
                wait(act, "q_ps", b + 1)
                a_(xq[:, 0, :], PD[:], ACT.Identity, bias=vec("qb")).then_inc(S["qh_sb"], 1)
                wait(act, "stored", 16 * (b - 2))
                a_(qsq[:], PD[:], ACT.Square, bias=vec("qb")).then_inc(S["qsq_sb"], 1)

            def norms(b, _):
                wait(act, "ksq_sb", T * b + T)
                a_(kss[:], kss[:], ACT.Sqrt).then_inc(S["kss_rt"], 1)
                wait(act, "nq_ps", b + 1)
                a_(nq[:], PD[:], ACT.Sqrt).then_inc(S["nq_sb"], 1)

            def keyvalue(b, _):
                wait(act, "kv_ps", b + 1)
                a_(kv[:], PD[:, 0:C + 1], ACT.Copy).then_inc(S["kv_sb"], 1)

            def fold(b, _):
                wait(act, "m2_ps", b + 1)
                a_(m2[:, 0, :], PD[:, 0:C], ACT.Copy).then_inc(S["m2h_sb"], 1)
                a_(rv[:], PD[:, HALF:HALF + 1], ACT.Copy).then_inc(S["rv_sb"], 1)

            def numerator(b, _):
                wait(act, "attn_raw", b + 1)
                a_(attn[:, 0, 1:H + 1, 1:W + 1], image(nq[:], W), ACT.Identity, bias=vec("rb")).then_inc(S["ah_sb"], 1)

            def conv1(b, part):
                if part == 2 * PARTS - 1:
                    wait(act, "c1_ps", 2 * b + 2)
                    for half in range(2):
                        a_(attn[:, 0, 1 + HR * half:1 + HR * half + HR, 1:W + 1], image(rows(PD, half), W),
                           ACT.Identity, bias=vec("c1b")).then_inc(S["hh_sb"], 1)

            def residual(b, _):
                wait(act, "x1_sb", 2 * b + 2)
                wait(act, "tap_ps", 3 * b)
                a_(x1p[:, 0, :, PADD:PADD + W], x1[:], ACT.Copy).then_inc(S["x1h_sb"], 1)

            def taps(b, n):
                i, ps = TAPS[n]
                d = DIL[i]
                wait(act, "tap_ps", 3 * b + n + 1)
                wait(act, "f_ps", 3 * b)
                for dy in range(3):
                    s = slice(32 * dy, 32 * dy + 32)
                    to = slice(max(0, (1 - dy) * d), H + min(0, (1 - dy) * d))
                    fr = slice(max(0, (dy - 1) * d), H + min(0, (dy - 1) * d))
                    a_(Y[s, i, to, :], image(ps[s, :], W)[:, fr, :], ACT.Copy).then_inc(S["Y_sb"], 1)

            def tapsum(b, n):
                i, _ = TAPS[n]
                m_out, ps = TAPSUM[n]
                dst = (f2[:, :], f3[:, :], f1)[n]
                wait(act, "f_ps", 3 * b + n + 1)
                a_(dst, ps[0:m_out, :], ACT.Identity, bias=fbias[0:m_out, i:i + 1]).then_inc(S["fh_sb"], 1)

            def maxima(b, t):
                if t == 1:
                    wait(act, "f1T_ps", b + 1)
                    a_(f1T[:].rearrange("p a b -> p (a b)"), PC[:, 0:T * 32], ACT.Copy).then_inc(S["f1T_sb"], 1)

            def maxrow(b, _):
                wait(act, "nmrow_ps", b + 1)
                for p in (0, 64):
                    a_(f2[p:p + 1, :], PC[p:p + 1, :], ACT.Copy).then_inc(S["nmrow_sb"], 1)

            def weigh(b, j):
                if j == 0:
                    wait(act, "table_in", 16 * b)
                wait(act, "st_ps", T * b + j + 1)
                if j >= 2:
                    wait(act, "pv_ps", T * b + j - 1)
                a_(E[:, j % 2, :], PAB[j % 2][:], ACT.Exp).then_inc(S["e_sb"], 1)

            def attend(b, _):
                wait(act, "pv_ps", T * b + T)
                a_(U, PC[:], ACT.Copy).then_inc(S["U_sb"], 1)

            def variance(b, _):
                wait(act, "gnv_sb", b + 1)
                a_(gs[:, 7:8], gs[:, 7:8], ACT.Sqrt).then_inc(S["gn_rt"], 1)

            def project(b, _):
                wait(act, "yw_ps", b + 1)
                yw = image(PA[:, 0:NP], w2)
                a_(ypad[0:INNER, 1:h2 + 1, 1:w2 + 1], yw[0:INNER], ACT.Copy).then_inc(S["ypad_sb"], 1)
                a_(ypad[INNER:128, 1:w2 + 1, 1:h2 + 1], yw[INNER:128].rearrange("p a b -> p b a"), ACT.Copy)\
                    .then_inc(S["ypad_sb"], 1)
                a_(gate, PA[:, HALF:HALF + NP], ACT.Sigmoid).then_inc(S["gate_sb"], 1)

            def deltas(b, _):
                wait(act, "y1_sb", 9 * b + 9)
                a_(es, y1, ACT.Sigmoid).then_inc(S["es_sb"], 1)
                wait(act, "dv_ps", b + 1)
                a_(dl, PA[:, 0:NP], ACT.Sigmoid, bias=vec("bd")).then_inc(S["dl_sb"], 1)

            def scan(b, _):
                wait(act, "z_ps", b + 1)
                z = image(PC[:, 0:NP], w2)
                for dst, src in ((slice(1, w2 + 1), slice(0, w2)), (slice(0, 1), slice(0, 1)),
                                 (slice(w2 + 1, w2 + 2), slice(w2 - 1, w2))):
                    a_(zp[:, :, dst], z[:, :, src], ACT.Copy, scale=1.0 / 64).then_inc(S["zp_sb"], 1)

            def hidden(b, _):
                wait(act, "w1_ps", b + 1)
                for g in range(4):
                    dy, dx = divmod(g, 2)
                    s = slice(32 * g, 32 * g + 32)
                    a_(S4[s, 1 - dy:H + 1 - dy, 1 - dx:W + 1 - dx], image(PA[s, :], W), ACT.Relu, scale=bns[s, 0:1],
                       bias=bnb[s, 0:1]).then_inc(S["s4_sb"], 1)

            def offset(b, _):
                wait(act, "off_ps", b + 1)
                a_(off, PC[0:27, :], ACT.Identity, bias=vec("boff", 0, 27)).then_inc(S["off_sb"], 1)

            def quads_(b, _):
                for n in range(3):
                    wait(act, "tab_ps", 3 * b + n + 1)
                    first, last = 4 * n, min(4 * n + 4, QT)
                    a_(quads[:, first:last, :].rearrange("p a b -> p (a b)"), QBANKS[n][0:QP, 0:(last - first) * 128],
                       ACT.Copy).then_inc(S["quads_sb"], 1)

            def indices(b, _):
                wait(act, "offT_sb", b + 1)
                a_(em[:], offT[:, :, 18:27], ACT.Sigmoid).then_inc(S["em_sb"], 1)
                wait(act, "o_sb", b)
                a_(res[:], x3[:].rearrange("p a b -> p (a b)"), ACT.Copy).then_inc(S["res_sb"], 1)

            def sample(b, t):
                wait(act, "tr_ps", T * b + t + 1)
                if t in (0, 4):
                    wait(act, "dcn_ps", 2 * b + t // 4)
                ps = PB[0:96, (t % 2) * HALF:(t % 2) * HALF + 384]
                a_(sT[:, :, 128 * (t % 4):128 * (t % 4 + 1)], ps.rearrange("p (g n) -> p g n", g=3), ACT.Copy)\
                    .then_inc(S["sT_sb"], 1)
                if t % 4 == 3:
                    half = t // 4
                    wait(act, "dcn_ps", 2 * b + half + 1)
                    a_(rows(h3, half), PS_DCN[half], ACT.Relu, scale=bns[0:CB, 1:2], bias=bnb[0:CB, 1:2])\
                        .then_inc(S["h3_sb"], 1)

            def deform(b, _):
                wait(act, "o_sb", b + 1)
                a_(ob[:], ob[:], ACT.Relu, bias=bnb[:, 2:3]).then_inc(S["ob_sb"], 1)

            run(act, {"split_x": split_x, "keys": keys, "queries": queries, "norms": norms, "keyvalue": keyvalue,
                      "fold": fold, "numerator": numerator, "conv1": conv1, "residual": residual, "taps": taps,
                      "tapsum": tapsum, "maxima": maxima, "maxrow": maxrow, "weigh": weigh, "attend": attend,
                      "variance": variance, "project": project, "deltas": deltas, "scan": scan, "hidden": hidden,
                      "offset": offset, "quads": quads_, "indices": indices, "sample": sample, "deform": deform})

        @block.vector
        def _(dve):
            v = nc.vector

            def low(out, value, high):
                return v.tensor_tensor(out, value, high.bitcast(F32), ALU.subtract)

            dve.wait_ge(S["w_in"], 16)
            bn_names = ("bn1", "bn2", "bn3")
            for i, name in enumerate(bn_names):
                v.tensor_scalar(bnt[:, i:i + 1], vec(name, 3), EPS_BN, None, ALU.add).then_inc(S["bnv_sb"], 1)
            pwT = w("pwT").rearrange("p (i r) -> p i r", i=3)
            dww = w("dww").rearrange("p (i t) -> p i t", i=3)
            for i in range(3):
                v.tensor_tensor(wstage[:, 9 * i:9 * i + 9, :], pwT[:, i:i + 1, :].to_broadcast([128, 9, R]),
                                dww[:, i, :].unsqueeze(2).to_broadcast([128, 9, R]), ALU.mult).then_inc(S["consts"], 1)
            dve.wait_ge(S["consts"], 3)
            for i in range(3):
                src = wstage[:, 9 * i:9 * i + 9, :].rearrange("p (y x) r -> p x y r", y=3)
                v.tensor_copy(wf[:, i, :, :, 0:R], src).then_inc(S["consts"], 1)
            dve.wait_ge(S["consts"], 6)
            for i in range(3):
                src = wstage[:, 9 * i:9 * i + 9, :].rearrange("p (y x) r -> p x y r", y=3)
                low(wf[:, i, :, :, R:2 * R], src, wf[:, i, :, :, 0:R]).then_inc(S["consts"], 1)
            dve.wait_ge(S["bias_ps"], 1)
            v.tensor_tensor(fbias[:], PA[0:96, 0:3], w("pwb")[0:96, :], ALU.add).then_inc(S["consts"], 1)
            dve.wait_ge(S["bnr_sb"], 1)
            v.reciprocal(bnr[:], bnt[:]).then_inc(S["bnr_sb"], 1)
            dve.wait_ge(S["bnr_sb"], 2)
            for i, name in enumerate(bn_names):
                v.tensor_tensor(bns[:, i:i + 1], bnr[:, i:i + 1], vec(name, 0), ALU.mult).then_inc(S["consts"], 1)
                if i == 1:
                    v.tensor_tensor(bnt[:, 1:2], vec(name, 4), vec(name, 2), ALU.subtract).then_inc(S["consts"], 1)
                else:
                    v.tensor_scalar(bnt[:, i:i + 1], vec(name, 2), -1.0, None, ALU.mult).then_inc(S["consts"], 1)
                dve.wait_ge(S["consts"], 12 + 3 * i)
                v.scalar_tensor_tensor(bnb[:, i:i + 1], bnt[:, i:i + 1], bns[:, i:i + 1], vec(name, 1),
                                       ALU.mult, ALU.add).then_inc(S["consts"], 1)
            dve.wait_ge(S["wh_sb"], 5)
            low(wkv[:, 1, :], w("wkv"), wkv[:, 0, :]).then_inc(S["wl_sb"], 1)
            low(qw[:, 1, :], w("qwT"), qw[:, 0, :]).then_inc(S["wl_sb"], 1)
            for n, cw in enumerate((c1, c2)):
                low(cw[:, 1, :], cstage[:, n * 9 * C:(n + 1) * 9 * C], cw[:, 0, :]).then_inc(S["wl_sb"], 1)
            dve.wait_ge(S["wl_sb"], 4)
            dve.wait_ge(S["consts"], 19)
            dve.wait_ge(S["zeroed"], 11)
            v.memset(gs[:], 0.0).then_inc(S["init_v"], 1)

            def split_x(b, _):
                wait(dve, "xh_sb", b + 1)
                low(xq[:, 1, :], xin[:], xq[:, 0, :]).then_inc(S["xl_sb"], 1)

            def keys(b, _):
                wait(dve, "kv_ps", b)
                for j in range(4):
                    wait(dve, "kvt_ps", 4 * b + j + 1)
                    bank = rows(PD, j % 2).rearrange("p (t n) -> p t n", t=2)
                    v.tensor_tensor(kvt[:, 2 * j:2 * j + 2, 1:], bank, w("kvb").unsqueeze(1).to_broadcast([128, 2, 2 * C]),
                                    ALU.add).then_inc(S["kvt_sb"], 1)

            def queries(b, _):
                wait(dve, "qh_sb", b + 1)
                wait(dve, "qsq_sb", b + 1)
                v.scalar_tensor_tensor(xq[:, 1, :], PD[:], vec("qb"), xq[:, 0, :].bitcast(F32), ALU.add, ALU.subtract)\
                    .then_inc(S["ql_sb"], 1)

            def norms(b, _):
                wait(dve, "kss_rt", b + 1)
                v.reciprocal(krn[:], kss[:]).then_inc(S["krn_sb"], 1)
                wait(dve, "krn_sb", b + 1)
                v.tensor_tensor(kvt[:, :, 1:1 + C], kvt[:, :, 1:1 + C], krn[:].unsqueeze(2).to_broadcast([128, T, C]), ALU.mult)\
                    .then_inc(S["kn_sb"], 1)

            def keyvalue(b, _):
                wait(dve, "kv_ps", b + 1)
                v.tensor_copy(ksc[:], PD[:, HALF:HALF + 1]).then_inc(S["ksc_sb"], 1)
                wait(dve, "ksc_sb", b + 1)
                v.tensor_scalar(ks[:, 0, :], ones[:], ksc[:, 0:1], None, ALU.mult).then_inc(S["ksh_sb"], 1)
                wait(dve, "ksh_sb", b + 1)
                v.scalar_tensor_tensor(ks[:, 1, :], ones[:], ksc[:, 0:1], ks[:, 0, :].bitcast(F32), ALU.mult, ALU.subtract)\
                    .then_inc(S["ksl_sb"], 1)

            def fold(b, _):
                wait(dve, "m2h_sb", b + 1)
                low(m2[:, 1, :], PD[:, 0:C], m2[:, 0, :]).then_inc(S["m2l_sb"], 1)

            def denominator(b, _):
                wait(dve, "nq_sb", b + 1)
                wait(dve, "kq_ps", b + 1)
                v.scalar_tensor_tensor(den[:], nq[:], N + EPS_L0, PD[:], ALU.mult, ALU.add).then_inc(S["den_sb"], 1)
                wait(dve, "den_sb", b + 1)
                v.reciprocal(den[:], den[:]).then_inc(S["rec_sb"], 1)

            def numerator(b, _):
                wait(dve, "m2q_ps", b + 1)
                v.scalar_tensor_tensor(nq[:], nq[:], rv[:, 0:1], PD[:], ALU.mult, ALU.add).then_inc(S["num_sb"], 1)
                wait(dve, "num_sb", b + 1)
                v.tensor_tensor(nq[:], nq[:], den[:], ALU.mult).then_inc(S["attn_raw"], 1)
                wait(dve, "ah_sb", b + 1)
                v.scalar_tensor_tensor(attn[:, 1, 1:H + 1, 1:W + 1], image(nq[:], W), vec("rb"),
                                       attn[:, 0, 1:H + 1, 1:W + 1].bitcast(F32), ALU.add, ALU.subtract).then_inc(S["al_sb"], 1)

            def conv1(b, part):
                if part == 2 * PARTS - 1:
                    for half in range(2):
                        s = slice(1 + HR * half, 1 + HR * half + HR)
                        wait(dve, "hh_sb", 2 * b + half + 1)
                        v.scalar_tensor_tensor(attn[:, 1, s, 1:W + 1], image(rows(PD, half), W), vec("c1b"),
                                               attn[:, 0, s, 1:W + 1].bitcast(F32), ALU.add, ALU.subtract)\
                            .then_inc(S["hl_sb"], 1)

            def conv2(b, part):
                if part % PARTS == PARTS - 1:
                    half = part // PARTS
                    s = slice(HR * half, HR * half + HR)
                    xh = image(rows(xres, half), W)
                    if half == 0:
                        wait(dve, "xres_in", 16 * b + 16)
                        wait(dve, "x2_sb", b)
                        wait(dve, "x1h_sb", b)
                    wait(dve, "c2_ps", 2 * b + half + 1)
                    v.scalar_tensor_tensor(x1[:, s, :], image(rows(PD, half), W), vec("c2b"), xh, ALU.add, ALU.mult)\
                        .then_inc(S["hx_sb"], 1)
                    wait(dve, "hx_sb", 2 * b + half + 1)
                    v.tensor_tensor(x1[:, s, :], x1[:, s, :], xh, ALU.add).then_inc(S["x1_sb"], 1)

            def residual(b, _):
                wait(dve, "x1h_sb", b + 1)
                low(x1p[:, 1, :, PADD:PADD + W], x1[:], x1p[:, 0, :, PADD:PADD + W]).then_inc(S["x1l_sb"], 1)

            def tapsum(b, n):
                if n == 2:
                    return
                i, _ = TAPS[n]
                m_out, ps = TAPSUM[n]
                f, s = ((f2, slice(64, 96)), (f3, slice(32, 64)))[n]
                wait(dve, "fh_sb", 3 * b + n + 1)
                v.scalar_tensor_tensor(f[s, :], ps[s, :], fbias[s, i:i + 1], f[s, :].bitcast(F32), ALU.add, ALU.subtract)\
                    .then_inc(S["fl_sb"], 1)

            def maxima(b, t):
                wait(dve, "s_ps", T * b + t + 1)
                v.tensor_reduce(mx[:, t:t + 1], PAB[t % 2][:], AX_X, ALU.max).then_inc(S["mx_sb"], 1)
                if t == T - 1:
                    wait(dve, "mx_sb", T * b + T)
                    v.tensor_scalar(nm[:, :, 0], mx[:], -1.0, None, ALU.mult).then_inc(S["nmh_sb"], 1)
                    wait(dve, "nmh_sb", b + 1)
                    v.scalar_tensor_tensor(nm[:, :, 64], mx[:], -1.0, nm[:, :, 0].bitcast(F32), ALU.mult, ALU.subtract)\
                        .then_inc(S["nml_sb"], 1)

            def attend(b, _):
                wait(dve, "co_ps", b + 1)
                v.reciprocal(rden, PB[:]).then_inc(S["rd_sb"], 1)
                wait(dve, "rd_sb", b + 1)
                v.tensor_tensor(rden, PA[:], rden, ALU.mult).then_inc(S["av_sb"], 1)
                wait(dve, "av_sb", b + 1)
                v.tensor_tensor(x2[:], image(rden, W), x1[:], ALU.add).then_inc(S["x2_sb"], 1)

            def mean_(b, _):
                wait(dve, "x2_sb", b + 1)
                x2f = x2[:].rearrange("p a b -> p (a b)")
                for half in range(2):
                    v.bn_stats(st[:, half, :], rows(x2f, half)).then_inc(S["stats_sb"], 1)
                wait(dve, "stats_sb", 2 * b + 2)
                v.tensor_tensor(p1, x2[:, 0:H:2, :], x2[:, 1:H:2, :], ALU.add).then_inc(S["p1_sb"], 1)
                v.bn_aggr(mv[:], st[:].rearrange("p a b -> p (a b)")).then_inc(S["stat_sb"], 1)
                wait(dve, "p1_sb", b + 1)
                v.tensor_tensor(image(p2, w2), p1[:, :, 0:W:2], p1[:, :, 1:W:2], ALU.add).then_inc(S["p2_sb"], 1)
                wait(dve, "mu_ps", b + 1)
                wait(dve, "stat_sb", b + 1)
                v.tensor_tensor(gs[:, 0:1], mv[:, 0:1], PC[:, 0:1], ALU.subtract).then_inc(S["dm_sb"], 1)
                v.tensor_scalar(gs[:, 2:3], PC[:, 0:1], -1.0, None, ALU.mult).then_inc(S["dm_sb"], 1)
                wait(dve, "dm_sb", 2 * b + 2)
                v.scalar_tensor_tensor(gs[:, 1:2], gs[:, 0:1], gs[:, 0:1], mv[:, 1:2], ALU.mult, ALU.add).then_inc(S["dev_sb"], 1)

            def variance(b, _):
                n = 4 * b
                wait(dve, "var_ps", b + 1)
                v.tensor_scalar(gs[:, 7:8], PC[:, HALF:HALF + 1], EPS_GN, None, ALU.add).then_inc(S["gnv_sb"], 1)
                wait(dve, "gn_rt", b + 1)
                v.reciprocal(gs[:, 3:4], gs[:, 7:8]).then_inc(S["gn_sb"], 1)
                wait(dve, "gn_sb", n + 1)
                v.tensor_tensor(gs[:, 4:5], gs[:, 3:4], vec("gnw"), ALU.mult).then_inc(S["gn_sb"], 1)
                wait(dve, "gn_sb", n + 2)
                v.scalar_tensor_tensor(gs[:, 5:6], gs[:, 2:3], gs[:, 4:5], vec("gnb"), ALU.mult, ALU.add).then_inc(S["gn_sb"], 1)
                v.tensor_scalar(gs[:, 6:7], gs[:, 4:5], 0.25, None, ALU.mult).then_inc(S["gn_sb"], 1)
                wait(dve, "gn_sb", n + 4)
                wait(dve, "p2_sb", b + 1)
                v.tensor_scalar(y0, p2, gs[:, 6:7], gs[:, 5:6], ALU.mult, ALU.add).then_inc(S["y0_sb"], 1)

            def project(b, _):
                wait(dve, "ypad_sb", 2 * b + 2)
                for tap in range(9):
                    src = ypad[:, tap // 3:tap // 3 + h2, tap % 3:tap % 3 + w2]
                    if tap == 0:
                        v.tensor_scalar(image(y1, w2), src, vec("dwk", 0), None, ALU.mult).then_inc(S["y1_sb"], 1)
                    else:
                        wait(dve, "y1_sb", 9 * b + tap)
                        v.scalar_tensor_tensor(image(y1, w2), src, vec("dwk", tap), image(y1, w2), ALU.mult, ALU.add)\
                            .then_inc(S["y1_sb"], 1)

            def deltas(b, _):
                wait(dve, "es_sb", b + 1)
                v.tensor_tensor(y2, y1, es, ALU.mult).then_inc(S["y2_sb"], 1)
                wait(dve, "dl_sb", b + 1)
                d = image(dl, w2)
                v.tensor_scalar(af[:, :, 1:w2], d[:, :, 1:w2], -1.0, 1.0, ALU.mult, ALU.add).then_inc(S["scan_in"], 1)
                v.tensor_scalar(ab[:, :, 0:w2 - 1], d[:, :, 0:w2 - 1], -1.0, 1.0, ALU.mult, ALU.add).then_inc(S["scan_in"], 1)
                v.scalar_tensor_tensor(bb, PA[:, HALF:HALF + NP], vec("bv"), dl, ALU.add, ALU.mult).then_inc(S["scan_in"], 1)
                wait(dve, "scan_in", 3 * b + 3)
                v.tensor_tensor_scan(sf, af[:].rearrange("p a b -> p (a b)"), bb, 0.0, ALU.mult, ALU.add)\
                    .then_inc(S["scan_sb"], 1)
                v.tensor_tensor_scan(sr[:, ::-1], ab[:].rearrange("p a b -> p (a b)")[:, ::-1], bb[:, ::-1], 0.0,
                                     ALU.mult, ALU.add).then_inc(S["scan_sb"], 1)
                wait(dve, "scan_sb", 2 * b + 2)
                v.tensor_tensor(ss, sf, sr, ALU.add).then_inc(S["ss_sb"], 1)
                wait(dve, "ss_sb", b + 1)
                wait(dve, "gate_sb", b + 1)
                v.tensor_tensor(yg[0:INNER], ss[0:INNER], gate[0:INNER], ALU.mult).then_inc(S["yg_sb"], 1)
                v.tensor_tensor(image(yg[INNER:128], w2), image(ss[INNER:128], h2).rearrange("p a b -> p b a"),
                                image(gate[INNER:128], w2), ALU.mult).then_inc(S["yg_sb"], 1)

            def resize(b, _):
                wait(dve, "zp_sb", 3 * b + 3)
                mid = zp[:, :, 1:w2 + 1]
                for k in range(2):
                    v.scalar_tensor_tensor(up[:, 1:h2 + 1, k:W:2], mid, 3.0, zp[:, :, 2 * k:2 * k + w2], ALU.mult, ALU.add)\
                        .then_inc(S["up_sb"], 1)
                wait(dve, "up_sb", 2 * b + 2)
                v.tensor_copy(up[:, 0:1, :], up[:, 1:2, :]).then_inc(S["upe_sb"], 1)
                v.tensor_copy(up[:, h2 + 1:h2 + 2, :], up[:, h2:h2 + 1, :]).then_inc(S["upe_sb"], 1)
                wait(dve, "upe_sb", 2 * b + 2)
                wait(dve, "res_sb", b)
                for k in range(2):
                    v.scalar_tensor_tensor(x3[:, k:H:2, :], up[:, 1:h2 + 1, :], 3.0, up[:, 2 * k:2 * k + h2, :],
                                           ALU.mult, ALU.add).then_inc(S["rs_sb"], 1)
                for k in range(2):
                    wait(dve, "rs_sb", 2 * b + k + 1)
                    v.tensor_tensor(x3[:, k:H:2, :], x3[:, k:H:2, :], x2[:, k:H:2, :], ALU.add).then_inc(S["x3_sb"], 1)

            def indices(b, _):
                wait(dve, "offT_ps", b + 1)
                if not (isinstance(b, int) and b == 0):
                    for t in range(T):
                        dve.wait_ge(gathered[t], 144 * b)
                v.tensor_copy(offT[:].rearrange("p a b -> p (a b)"), PC[:, HALF:HALF + T * 27]).then_inc(S["offT_sb"], 1)
                wait(dve, "offT_sb", b + 1)
                base = w("base").rearrange("p (t k) -> p t k", t=T)
                n = 9 * b
                v.tensor_tensor(uu[:], offT[:, :, 0:18], base, ALU.add).then_inc(S["ixs"], 1)
                wait(dve, "ixs", n + 1)
                v.tensor_scalar(uu[:], uu[:], 0.0, float(H + 1), ALU.max, ALU.min).then_inc(S["ixs"], 1)
                wait(dve, "ixs", n + 2)
                v.tensor_scalar(rr[:], uu[:], ROUND, None, ALU.add).then_inc(S["ixs"], 1)
                wait(dve, "ixs", n + 3)
                v.tensor_scalar(rr[:], rr[:], ROUND, None, ALU.subtract).then_inc(S["ixs"], 1)
                wait(dve, "ixs", n + 4)
                v.tensor_tensor(gg[:], rr[:], uu[:], ALU.is_gt).then_inc(S["ixs"], 1)
                wait(dve, "ixs", n + 5)
                v.tensor_tensor(rr[:], rr[:], gg[:], ALU.subtract).then_inc(S["ixs"], 1)
                wait(dve, "ixs", n + 6)
                v.tensor_scalar(u0[:], rr[:], float(H), None, ALU.min).then_inc(S["ixs"], 1)
                wait(dve, "ixs", n + 7)
                v.scalar_tensor_tensor(ixf[:], u0[:, :, 0:18:2], float(QS), u0[:, :, 1:18:2], ALU.mult, ALU.add)\
                    .then_inc(S["ixs"], 1)
                wait(dve, "ixs", n + 8)
                v.tensor_copy(ix[:], ixf[:].rearrange("p a b -> p (a b)")).then_inc(S["ix_sb"], 1)
                v.tensor_tensor(wt1[:], uu[:], u0[:], ALU.subtract).then_inc(S["ixs"], 1)
                wait(dve, "ixs", n + 9)
                m = 5 * b
                v.tensor_scalar(wt0[:], wt1[:], -1.0, 1.0, ALU.mult, ALU.add).then_inc(S["wq_sb"], 1)
                wait(dve, "em_sb", b + 1)
                wait(dve, "wq_sb", m + 1)
                v.tensor_tensor(ay[:, 0], wt0[:, :, 0:18:2], em[:], ALU.mult).then_inc(S["wq_sb"], 1)
                v.tensor_tensor(ay[:, 1], wt1[:, :, 0:18:2], em[:], ALU.mult).then_inc(S["wq_sb"], 1)
                wait(dve, "wq_sb", m + 3)
                for g in range(3):
                    wx = (wt0, wt1)[g % 2]
                    i = v.tensor_tensor(wq[:, :, :, g], ay[:, g // 2], wx[:, :, 1:18:2], ALU.mult)
                    if g:
                        i.then_inc(S["wq_sb"], 1)

            def sample(b, t):
                if t == 0:
                    wait(dve, "wq_sb", 5 * b + 5)
                    wait(dve, "wq3_sb", b + 1)
                dve.wait_ge(gathered[t], 144 * b + 144)
                Gt = G[:, t].rearrange("p k (g c) -> p k g c", g=4)
                v.tensor_tensor(Gt, Gt, wq[:, t].unsqueeze(3).to_broadcast([128, 9, 4, CB]), ALU.mult).then_inc(S["gw_sb"], 1)
                wait(dve, "gw_sb", T * b + t + 1)
                v.tensor_tensor(G[:, t, :, 0:64], G[:, t, :, 0:64], G[:, t, :, 64:128], ALU.add).then_inc(S["g2_sb"], 1)
                wait(dve, "g2_sb", T * b + t + 1)
                if t >= 2:
                    wait(dve, "tr_ps", T * b + t - 1)
                v.tensor_tensor(sm[:, t % 2].rearrange("p (k c) -> p k c", k=9), G[:, t, :, 0:32], G[:, t, :, 32:64],
                                ALU.add).then_inc(S["sm_sb"], 1)

            def deform(b, _):
                wait(dve, "w3_ps", b + 1)
                wait(dve, "xl_sb", upto(b + LAST_LAG + 1))
                wait(dve, "stored", 16 * b)
                v.scalar_tensor_tensor(ob[:], PB[:], bns[:, 2:3], res[:], ALU.mult, ALU.add).then_inc(S["o_sb"], 1)

            run(dve, {"split_x": split_x, "keys": keys, "queries": queries, "norms": norms, "keyvalue": keyvalue,
                      "fold": fold, "denominator": denominator, "numerator": numerator, "conv1": conv1, "conv2": conv2,
                      "residual": residual, "tapsum": tapsum, "maxima": maxima, "attend": attend, "mean": mean_,
                      "variance": variance, "project": project, "deltas": deltas, "resize": resize,
                      "indices": indices, "sample": sample, "deform": deform})


def _columns(i, np):
    f = np.float32

    def full(a, rows=None):
        a = np.asarray(a, f)
        a = a.reshape(a.shape[0], -1)
        z = np.zeros((128, a.shape[1]), f)
        z[:a.shape[0]] = a
        return z

    def four(a):
        return np.concatenate([a] * 4, axis=0)

    l0 = lambda n: i["L0_conv_" + n]
    l1 = lambda n: i["L1_conv_" + n]
    l2 = lambda n: i["L2_conv_" + n]
    l3 = lambda n: i["L3_conv_" + n]
    r = {}
    r["wkv"] = np.concatenate([l0("kw").T, l0("vw").T], axis=1)
    r["kvb"] = np.broadcast_to(np.concatenate([l0("kb"), l0("vb")])[None, :], (128, 2 * C))
    r["qwT"], r["rwT"] = l0("qw").T, l0("rw").T
    r["ident"] = np.eye(128, dtype=f)
    pw = np.zeros((C, 3, 3, 32), f)
    pwb = np.zeros((3, 32, 3), f)
    pwb[:, 0, 0] = pwb[:, 0, 2] = 1.0
    for n in range(3):
        pw[:, n, :, 1:1 + R] = l1(f"c{n + 1}_pw_w")[:, :, 0, 0].T[:, None, :]
        pwb[:, 1:1 + R, n] = l1(f"c{n + 1}_pw_b")[None, :]
    r["pwS"], r["pwb"] = pw.reshape(C, -1), full(pwb.reshape(96, 3))
    r["pwT"] = np.ascontiguousarray(pw[:, :, 0, 1:1 + R]).reshape(C, -1)
    sel = np.zeros((3, 2, R, 3, 32), f)
    for c in range(R):
        sel[:, :, c, :, 1 + c] = 1.0
    r["sel"] = full(sel.reshape(96, 96))
    r["dww"] = np.concatenate([l1(f"c{n}_dw_w").reshape(C, 9) for n in (1, 2, 3)], axis=1)
    r["dwb"] = np.stack([l1(f"c{n}_dw_b") for n in (1, 2, 3)], axis=1)
    co = np.zeros((4, 32, C), f)
    co[:, 0] = l1("co_b")
    co[:, 1:1 + R] = l1("co_w")[:, :, 0, 0].T
    densel = np.zeros((4, 32, C), f)
    densel[:, 0] = 1.0
    r["coT"], r["densel"] = co.reshape(128, C), densel.reshape(128, C)
    win = l2("w_in").T
    r["winY"] = np.concatenate([win[:, :INNER]] * 2, axis=1)
    r["winG"] = np.concatenate([win[:, INNER:]] * 2, axis=1)
    dwk = l2("w_dw").reshape(INNER, 3, 3)
    r["dwk"] = np.concatenate([dwk.reshape(INNER, 9), dwk.transpose(0, 2, 1).reshape(INNER, 9)], axis=0)
    for n in ("wd", "wv"):
        z = np.zeros((128, 128), f)
        z[:INNER, :INNER] = l2("row_" + n).T
        z[INNER:, INNER:] = l2("col_" + n).T
        r[n] = z
    r["wout"] = np.concatenate([l2("w_out").T] * 2, axis=0)
    r["bd"] = np.concatenate([l2("row_bd"), l2("col_bd")])[:, None]
    r["bv"] = np.concatenate([l2("row_bv"), l2("col_bv")])[:, None]
    r["w1T"] = np.concatenate([l3("w1").T] * 4, axis=1)
    wo = np.zeros((4, CB, 4, 27), f)
    for g in range(4):
        for q in range(4):
            ky, kx = 2 * (q // 2) + g // 2, 2 * (q % 2) + g % 2
            if ky < 3 and kx < 3:
                wo[g, :, q, :] = l3("woff")[:, :, ky, kx].T
    r["woff"] = wo.reshape(128, 4 * 27)
    w2 = l3("w2").reshape(CB, CB, 3, 3).transpose(2, 3, 1, 0).reshape(3, 96, CB)
    r["w2T"] = full(w2.transpose(1, 0, 2))
    r["w3T"] = np.roll(full(l3("w3").T), 96, axis=0)
    p = np.arange(128)
    base = np.zeros((128, T, 9, 2), f)
    for t in range(T):
        for k in range(9):
            base[:, t, k, 0] = 4 * t + p // W + k // 3
            base[:, t, k, 1] = p % W + k % 3
    r["base"] = full(base)
    for n in ("qb", "rb", "c1b", "c2b"):
        r[n] = l0(n)[:, None]
    r["gnw"], r["gnb"] = l2("gn_w")[:, None], l2("gn_b")[:, None]
    r["boff"] = full(l3("boff")[:, None])
    for n in (1, 2, 3):
        c = [l3(f"bn{n}_{s}") for s in "gbmv"] + ([l3("dcn_b")] if n == 2 else [])
        a = np.stack(c, axis=1)
        r[f"bn{n}"] = four(a) if a.shape[0] == CB else a
    return np.ascontiguousarray(np.concatenate([np.asarray(r[n], f).reshape(128, k) for n, k in FIELDS], axis=1))


def kernel(**inputs):
    import numpy as np
    import concourse.bacc as bacc
    from concourse.bass_utils import run_bass_kernel_spmd as run

    nc = bacc.Bacc("TRN2", target_bir_lowering=False, num_devices=1)
    ins = {k: np.asarray(a) for k, a in inputs.items()}
    x = np.ascontiguousarray(ins["x"].reshape(B, C, N))
    weights = _columns(ins, np)
    dx = nc.dram_tensor("in_x", x.shape, F32, kind="ExternalInput").ap()
    dw = nc.dram_tensor("in_weights", weights.shape, F32, kind="ExternalInput").ap()
    convs = np.ascontiguousarray(np.concatenate(
        [ins[f"L0_conv_{n}"].transpose(1, 2, 3, 0).reshape(C, -1) for n in ("c1w", "c2w")], axis=1))
    dc = nc.dram_tensor("in_convs", convs.shape, F32, kind="ExternalInput").ap()
    table = nc.dram_tensor("quad_table", (QT * QP, 128), F32, kind="Internal").ap()
    do = nc.dram_tensor("out_x", (B, C, N), F32, kind="ExternalOutput").ap()
    build(nc, dx, dw, dc, table, do)
    r = run(nc, [{"in_x": x, "in_weights": weights, "in_convs": convs}], core_ids=[0])
    return r.results[0]["out_x"].reshape(B, C, H, W)
```

```python
from contextlib import ExitStack

import concourse.bass as bass
from concourse import mybir

F32 = mybir.dt.float32
F32R = mybir.dt.float32r
U32 = mybir.dt.uint32
ALU = mybir.AluOpType
ACT = mybir.ActivationFunctionType
AX_X = mybir.AxisListType.X

B, C, H, W = 8, 128, 32, 32
N = H * W
HALF = N // 2
HR = H // 2
T = N // 128
R = C // 8
DIL = (1, 3, 5)
PADD = max(DIL)
CB = 32
NT = 9
QS = W + 2
QT = 11
QP = (H + 1) * QS // QT
INNER = 64
h2, w2 = H // 2, W // 2
NP = h2 * w2
EPS_L0, EPS_GN, EPS_BN = 1e-6, 1e-5, 1e-5
ROUND = float(2 ** 23)

FIELDS = [("kvqb", 3 * C), ("qw", C), ("rwT", C), ("ident", C),
          ("pwT", 3 * R), ("pwS", 3 * 96), ("dww", 27), ("dwb", 3), ("pwb", 3), ("sel", 96), ("coT", C), ("gsum", 32),
          ("winY", C), ("winG", C), ("dwk", 9), ("wd", C), ("wv", C), ("wout", C),
          ("w1T", C), ("woff", 4 * 27), ("w2T", 3 * CB), ("w3T", C), ("base", T * 18),
          ("qb", 1), ("rb", 1), ("c1b", 1), ("c2b", 1), ("gnw", 1), ("gnb", 1), ("bd", 1), ("bv", 1), ("boff", 1),
          ("bn1", 4), ("bn2", 5), ("bn3", 4)]
AT = {}
_n = 0
for _name, _len in FIELDS:
    AT[_name] = (_n, _len)
    _n += _len
WCOLS = _n

ORDER = [
    ("conv1", 1, 14, 1), ("weigh", 2, 3, 1), ("quads", 3, 1, 1), ("conv1", 1, 15, 1), ("weigh", 2, 4, 1),
    ("conv1", 1, 16, 1), ("quads", 3, 2, 1), ("sample", 4, 3, 1), ("indices", 3, 0, 1), ("conv1", 1, 17, 1),
    ("weigh", 2, 5, 1), ("mix", 4, 0, 1), ("conv2", 1, 0, 1), ("weigh", 2, 6, 1), ("index", 3, 0, 1),
    ("conv2", 1, 1, 1), ("sample", 4, 4, 1), ("weigh", 2, 7, 1), ("sample", 4, 5, 1), ("conv2", 1, 2, 3),
    ("split_x", 0, 0, 1), ("attend", 2, 0, 1), ("conv2", 1, 5, 2), ("attend", 2, 1, 1), ("conv2", 1, 7, 1),
    ("sample", 4, 6, 1), ("attend", 2, 2, 1), ("conv2", 1, 8, 8), ("sample", 4, 7, 1), ("conv2", 1, 16, 1),
    ("mean", 2, 0, 1), ("conv2", 1, 17, 1), ("residual", 1, 0, 1), ("mix", 4, 1, 1), ("keys", 0, 0, 4),
    ("deform", 4, 0, 1), ("keys", 0, 4, 4), ("variance", 2, 0, 1), ("norms", 0, 0, 1), ("taps", 1, 0, 2),
    ("deform", 4, 1, 1), ("keyvalue", 0, 0, 1), ("corners", 3, 0, 1), ("tapsum", 1, 0, 1), ("fold", 0, 0, 1),
    ("tapsum", 1, 1, 1), ("fold", 0, 1, 1), ("project", 2, 0, 1), ("taps", 1, 2, 1), ("numerator", 0, 0, 2),
    ("deltas", 2, 0, 1), ("numerator", 0, 2, 1), ("tapsum", 1, 2, 1), ("scan", 2, 0, 1), ("turn", 0, 0, 1),
    ("carry", 3, 0, 1), ("turn", 0, 1, 1), ("maxima", 1, 0, 2), ("conv1", 0, 0, 2), ("resize", 2, 0, 1),
    ("conv1", 0, 2, 2), ("maxima", 1, 2, 2), ("conv1", 0, 4, 3), ("hidden", 2, 0, 1), ("conv1", 0, 7, 1),
    ("maxima", 1, 4, 2), ("conv1", 0, 8, 2), ("maxima", 1, 6, 2), ("hidden", 2, 1, 1), ("conv1", 0, 10, 3),
    ("maxrow", 1, 0, 1), ("offset", 2, 0, 1), ("conv1", 0, 13, 1), ("weigh", 1, 0, 1), ("sample", 3, 0, 1),
    ("offset", 2, 1, 1), ("sample", 3, 1, 1), ("weigh", 1, 1, 2), ("quads", 2, 0, 1), ("sample", 3, 2, 1)]
LAST_LAG = 4
PARTS = 9
MC = C + 2
PHASES = ((0, 1, 2), (3, 4, 5), (6, 7))


def build(nc, x, weights, convs, table, out):
    with ExitStack() as ctx:
        def sb(name, shape, dt=F32):
            return ctx.enter_context(nc.sbuf_tensor(name, shape, dt))

        def sem(name):
            return ctx.enter_context(nc.semaphore(name))

        wt = sb("wt", [128, WCOLS])

        def w(name):
            a, n = AT[name]
            return wt[:, a:a + n]

        def vec(name, i=0, p=128):
            a, n = AT[name]
            return wt[0:p, a + i:a + i + 1]

        PA = ctx.enter_context(nc.psum_tensor("PA", [128, N], F32))
        PC = ctx.enter_context(nc.psum_tensor("PC", [128, N], F32))
        PD = ctx.enter_context(nc.psum_tensor("PD", [128, N], F32))
        PT = ctx.enter_context(nc.psum_tensor("PT", [128, HALF], F32))
        PS = ctx.enter_context(nc.psum_tensor("PS", [128, HALF], F32))

        wkvq = sb("wkvq", [128, 2, 3 * C], F32R)
        c1 = sb("c1", [128, 2, 9 * C], F32R)
        c2 = sb("c2", [128, 2, 9 * C], F32R)
        identr = sb("identr", [128, 128], F32R)
        wf = sb("wf", [128, 3, 3, 3, 2 * R], F32R)
        ones = sb("ones", [128, 128])
        mean = sb("mean", [128, 128])
        fbias = sb("fbias", [96, 3])
        c2b1 = sb("c2b1", [128, 1])
        bns = sb("bns", [128, 3])
        bnb = sb("bnb", [128, 3])
        bnt = sb("bnt", [128, 3])
        bnr = sb("bnr", [128, 3])
        xin = sb("xin", [128, N])
        xs = sb("xs", [128, 2, N], F32R)
        kvt = sb("kvt", [128, T, 1 + 2 * C])
        num = kvt[:, :, 0:MC]
        qs = sb("qs", [128, 2, C])
        sqj = sb("sqj", [128, C])
        nss = sb("nss", [128, 2, T])
        ktot = sb("ktot", [128, C])
        krn = sb("krn", [128, T])
        rden = sb("rden", [128, T])
        kv = sb("kv", [128, C + 1])
        vsr = sb("vsr", [128, C])
        qbr = sb("qbr", [128, C])
        m2 = sb("m2", [128, MC])
        m3 = sb("m3", [128, 2, MC], F32R)
        rvr = sb("rvr", [128, C])
        mb = sb("mb", [128, MC])
        xres = sb("xres", [128, N])
        attn = sb("attn", [128, 2, H + 2, W + 2], F32R)
        x1 = sb("x1", [128, H, W])
        x1p = sb("x1p", [128, 2, H, W + 2 * PADD], F32R)
        Y = sb("Y", [128, 3, H, W])
        Yf = Y[:].rearrange("p n a b -> p n (a b)")
        f1, h3, off = Yf[96:128, 0], Yf[96:128, 1], Yf[96:123, 2]
        mixed = f1
        f2 = sb("f2", [96, N], F32R)
        f3 = sb("f3", [96, N], F32R)
        f1T = sb("f1T", [128, T, 32])
        mxh = sb("mxh", [128, T, 2])
        mx = sb("mx", [128, T])
        nm = sb("nm", [128, T, 65], F32R)
        E = sb("E", [128, 2, N])
        U = E[:, 0, :]
        mrd = sb("mrd", [128, T])
        mixT = sb("mixT", [128, T, 32])
        x2 = sb("x2", [128, H, W])
        work = sb("work", [128, h2 * W + 12 * NP])
        place = [0]

        def temp(cols):
            a = place[0]
            place[0] += cols
            return work[:, a:a + cols]

        def image(ap, width):
            return ap.rearrange("p (a b) -> p a b", b=width)

        p1 = image(temp(h2 * W), W)
        p2, y0, y1, y2, es, gate, dl, bb, sf, sr, ss, yg = (temp(NP) for _ in range(12))
        st = sb("st", [128, 2, 6])
        mv = sb("mv", [128, 2])
        gs = sb("gs", [128, 8])
        ypad = sb("ypad", [128, h2 + 2, w2 + 2])
        af = sb("af", [128, h2, w2])
        ab = sb("ab", [128, h2, w2])
        up = image(work[:, 0:(h2 + 2) * W], W)
        zp = image(work[:, h2 * W + NP:h2 * W + NP + h2 * (w2 + 2)], w2 + 2)
        x3 = sb("x3", [128, H, W])
        res = sb("res", [128, N])
        S4 = sb("S4", [128, H + 2, W + 2])
        offT = sb("offT", [128, T, 27])
        quads = work[0:QP, 0:QT * 128].rearrange("p (t c) -> p t c", t=QT)
        uu = sb("uu", [128, T, 18])
        rr = sb("rr", [128, T, 18])
        gg = sb("gg", [128, T, 18])
        u0 = sb("u0", [128, T, 18])
        wt1 = sb("wt1", [128, T, 18])
        wt0 = sb("wt0", [128, T, 18])
        ixf = sb("ixf", [128, T, 9])
        ix = sb("ix", [128, T * 9], U32)
        em = sb("em", [128, T, 9])
        ay = sb("ay", [128, 2, T, 9])
        wq = sb("wq", [128, T, 9, 4])
        G = sb("G", [128, T, 9, 128])
        sm = sb("sm", [128, 2, 9 * CB])
        sT = sb("sT", [96, 3, HALF])
        TAPS = ((1, PA), (2, PC), (0, PA))
        TAPSUM = ((96, PA), (96, PC), (32, PC))
        cstage = G[:].rearrange("p t k c -> p (t k c)")[:, 0:21 * C]
        wstage = image(work[:, 0:27 * R], R)

        S = {}
        for n in ("w_in p_in c_in x_in xres_in zeroed consts bias_ps bnv_sb bnr_sb wh_sb wl_sb init_v init_a "
                  "xh_sb xl_sb kvt_ps kvt_sb qs_sb ksq_sb qsq_sb nss_rt krn_sb kn_sb ktot_sb kv_ps kv_sb ksum_sb vsr_sb m2_ps m2_sb rvr_sb "
                  "m3_ps m3h_sb m3l_sb mb_sb num_ps num_sb den_sb rec_sb add_sb attn_raw turn_ps "
                  "ah_sb al_sb c1_ps hh_sb hl_sb c2_ps x1_sb x1h_sb x1l_sb "
                  "tap_ps Y_sb f_ps fh_sb fl_sb f1T_ps f1T_sb s_ps mxh_sb mx_sb nmh_sb nml_sb nmrow_ps nmrow_sb nmlow_sb st_ps e_sb "
                  "pv_ps U_sb us_ps mrd_sb mixT_sb mix_ps mixed_sb co_ps x2_sb stats_sb p1_sb p2_sb stat_sb mu_ps dm_sb dev_sb "
                  "var_ps gnv_sb gn_rt gn_sb y0_sb yw_ps ypad_sb gate_sb y1_sb es_sb y2_sb dv_ps dl_sb scan_in scan_sb ss_sb yg_sb "
                  "z_ps zp_sb up_sb upe_sb rs_sb x3_sb w1_ps s4_sb off_ps off_sb offT_ps offT_sb tab_ps quads_sb table_in "
                  "ixs wt1_sb corner_sb em_sb ix_sb wq_sb wq3_sb res_sb gw_sb g2_sb sm_sb tr_ps sT_sb dcn_ps h3_sb w3_ps o_sb ob_sb stored").split():
            S[n] = sem("s_" + n)
        gathered = [sem(f"s_gathered{t}") for t in range(T)]

        def rows(ap, half):
            return ap[:, half * HALF:(half + 1) * HALF]

        def wait(eng, name, value):
            if not (isinstance(value, int) and value <= 0):
                eng.wait_ge(S[name], value)

        def upto(count):
            return min(count, B) if isinstance(count, int) else count

        def run(eng, stages):
            def iteration(i):
                for name, lag, first, count in ORDER:
                    b = i - lag
                    if name in stages and not (isinstance(b, int) and not 0 <= b < B):
                        for part in range(first, first + count):
                            stages[name](b, part)

            for i in range(LAST_LAG + 1):
                iteration(i)
            with eng.Fori(LAST_LAG + 1, B) as i:
                iteration(i)
            for i in range(B, B + LAST_LAG):
                iteration(i)

        block = ctx.enter_context(nc.Block())

        @block.sync
        def _(sp):
            sp.dma_start(xin[:], x[0]).then_inc(S["x_in"], 16)
            sp.dma_start(wt[:], weights).then_inc(S["w_in"], 16)
            sp.dma_start(cstage[:, 18 * C:], convs[:, 18 * C:]).then_inc(S["p_in"], 16)
            sp.dma_start(cstage[:, 0:18 * C], convs[:, 0:18 * C]).then_inc(S["c_in"], 16)
            for i in range(B + LAST_LAG):
                if 0 < i < B:
                    sp.wait_ge(S["xl_sb"], i)
                    sp.dma_start(xin[:], x[i]).then_inc(S["x_in"], 16)
                b = i - 1
                if 0 <= b < B:
                    if b:
                        sp.wait_ge(S["x1_sb"], 2 * b)
                    sp.dma_start(xres[:], x[b]).then_inc(S["xres_in"], 16)
                b = i - 3
                if 0 <= b < B:
                    sp.wait_ge(S["quads_sb"], 3 * b + 3)
                    if b:
                        for t in range(T):
                            sp.wait_ge(gathered[t], 144 * b)
                    sp.dma_start(table.rearrange("(t p) c -> p t c", p=QP), quads).then_inc(S["table_in"], 16)
                b = i - 4
                if 0 <= b < B:
                    sp.wait_ge(S["ob_sb"], b + 1)
                    sp.dma_start(out[b], res[:]).then_inc(S["stored"], 16)
            sp.wait_ge(S["stored"], 16 * B)

        @block.gpsimd
        def _(pool):
            for buf in (attn, x1p, nm):
                nc.gpsimd.memset(buf[:].bitcast(F32), 0.0).then_inc(S["zeroed"], 1)
            for buf in (Y, ypad, S4, af, ab, m2):
                nc.gpsimd.memset(buf[:], 0.0).then_inc(S["zeroed"], 1)
            nc.gpsimd.memset(ones[:], 1.0).then_inc(S["zeroed"], 1)
            nc.gpsimd.memset(mean[:], 1.0 / C).then_inc(S["zeroed"], 1)
            nc.gpsimd.memset(kvt[:], 1.0).then_inc(S["zeroed"], 1)

            def indices(b, _):
                wait(pool, "table_in", 16 * b + 16)
                wait(pool, "ix_sb", b + 1)
                wait(pool, "wq_sb", 3 * b + 3)
                for t in range(T):
                    wait(pool, "sm_sb", T * (b - 1) + t + 1)
                    nc.gpsimd.tensor_tensor(wq[:, t, :, 3], ay[:, 1, t], wt1[:, t, 1:18:2], ALU.mult).then_inc(S["wq3_sb"], 1)
                    for k in range(NT):
                        pool.indirect_dma_start(G[:, t, k, :], None, table, bass.IndirectOffsetOnAxis(
                            ap=ix[:, NT * t + k:NT * t + k + 1], axis=0)).then_inc(gathered[t], 16)

            run(pool, {"indices": indices})

        @block.tensor
        def _(pe):
            mm = nc.tensor.matmul
            ident = w("ident")

            def product(out, lhsT, rhs, start=True, stop=True):
                for n, (i, j) in enumerate(((0, 0), (0, 1), (1, 0))):
                    m = mm(out, lhsT(i), rhs(j), start=start and n == 0, stop=stop and n == 2)
                return m

            pe.wait_ge(S["w_in"], 16)
            for i in range(3):
                m = mm(PA[0:96, i:i + 1], w("pwS")[:, i * 96:(i + 1) * 96], w("dwb")[:, i:i + 1], start=True, stop=True)
            m.then_inc(S["bias_ps"], 1)
            pe.wait_ge(S["zeroed"], 12)
            pe.wait_ge(S["init_v"], 1)
            pe.wait_ge(S["init_a"], 1)

            def keys(b, t):
                if t == 0:
                    wait(pe, "xh_sb", b + 1)
                    wait(pe, "xl_sb", b + 1)
                    wait(pe, "x1_sb", 2 * b)
                else:
                    wait(pe, "kvt_sb", T * b + t - 1)
                    wait(pe, "qs_sb", T * b + t - 1)
                product(PD[:, (t % 2) * HALF:(t % 2) * HALF + 3 * C], lambda i: xs[:, i, 128 * t:128 * (t + 1)],
                        lambda i: wkvq[:, i, :]).then_inc(S["kvt_ps"], 1)

            def keyvalue(b, _):
                wait(pe, "kn_sb", b + 1)
                for t in range(T):
                    mm(PD[:, 0:C + 1], kvt[:, t, 1 + C:], kvt[:, t, 0:1 + C], start=t == 0, stop=t == T - 1)
                wait(pe, "ktot_sb", b + 1)
                mm(PD[:, HALF:HALF + 1], ktot[:], ones[:, 0:1], start=True, stop=True).then_inc(S["kv_ps"], 1)

            def fold(b, part):
                if part == 0:
                    wait(pe, "kv_sb", b + 1)
                    wait(pe, "ksum_sb", b + 1)
                    mm(PD[:, 0:C], kv[:, 1:1 + C], w("rwT"), start=True, stop=True).then_inc(S["m2_ps"], 1)
                    wait(pe, "vsr_sb", b + 1)
                    mm(PD[:, HALF:HALF + C], vsr[:], w("rwT"), start=True, stop=True).then_inc(S["m2_ps"], 1)
                else:
                    wait(pe, "m2_sb", b + 1)
                    wait(pe, "rvr_sb", b + 1)
                    mm(PD[:, 0:MC], w("qw"), m2[:], start=True, stop=True).then_inc(S["m3_ps"], 1)
                    mm(PD[:, HALF:HALF + MC], qbr[:], m2[:], start=True, stop=True).then_inc(S["m3_ps"], 1)

            def numerator(b, part):
                if part == 0:
                    wait(pe, "m3l_sb", b + 1)
                    wait(pe, "mb_sb", b + 1)
                if part == 2:
                    wait(pe, "num_sb", 3 * b + 1)
                for n, t in enumerate(PHASES[part]):
                    c0 = (part % 2) * HALF + n * MC
                    m = product(PD[:, c0:c0 + MC], lambda i: xs[:, i, 128 * t:128 * (t + 1)], lambda i: m3[:, i, :])
                m.then_inc(S["num_ps"], 1)

            def turn(b, half):
                wait(pe, "attn_raw", 2 * b + half + 1)
                for n in range(4):
                    m = nc.tensor.transpose(rows(PD, half)[:, n * 128:(n + 1) * 128], num[:, 4 * half + n, 0:C], ident)
                m.then_inc(S["turn_ps"], 1)

            def dense(cw, part):
                half, tap = divmod(part, PARTS)
                dy, dx = divmod(tap, 3)
                return product(rows(PD, half), lambda i: cw[:, i, tap * C:(tap + 1) * C],
                               lambda i: attn[:, i, dy + HR * half:dy + HR * half + HR, dx:dx + W],
                               start=tap == 0, stop=tap == PARTS - 1)

            def conv1(b, part):
                if part == 0:
                    if isinstance(b, int) and b == 0:
                        pe.wait_ge(S["wl_sb"], 3)
                    wait(pe, "ah_sb", 2 * b + 2)
                    wait(pe, "al_sb", 2 * b + 2)
                m = dense(c1, part)
                if part % PARTS == PARTS - 1:
                    m.then_inc(S["c1_ps"], 1)

            def conv2(b, part):
                if part == 0:
                    wait(pe, "hh_sb", 2 * b + 2)
                    wait(pe, "hl_sb", 2 * b + 2)
                m = dense(c2, part)
                if part % PARTS == PARTS - 1:
                    m.then_inc(S["c2_ps"], 1)

            def taps(b, n):
                i, ps = TAPS[n]
                wait(pe, "x1h_sb", b + 1)
                wait(pe, "x1l_sb", b + 1)
                if n == 0:
                    wait(pe, "x2_sb", 2 * b)
                if n == 2:
                    wait(pe, "fh_sb", 3 * b + 1)
                    wait(pe, "fl_sb", 2 * b + 1)
                for half in range(2):
                    for dx in range(3):
                        c0 = PADD + (dx - 1) * DIL[i]
                        for part in range(2):
                            m = mm(ps[0:96, half * HALF:(half + 1) * HALF], wf[:, i, dx].rearrange("p y r -> p (y r)"),
                                   x1p[:, part, HR * half:HR * half + HR, c0:c0 + W],
                                   start=dx == 0 and part == 0, stop=dx == 2 and part == 1)
                m.then_inc(S["tap_ps"], 1)

            def tapsum(b, n):
                i, _ = TAPS[n]
                m_out, ps = TAPSUM[n]
                wait(pe, "Y_sb", 9 * b + 3 * n + 3)
                if n == 2:
                    wait(pe, "fh_sb", 3 * b + 2)
                    wait(pe, "fl_sb", 2 * b + 2)
                for half in range(2):
                    m = mm(ps[0:m_out, half * HALF:(half + 1) * HALF], w("sel")[0:96, 0:m_out],
                           Y[0:96, i, HR * half:HR * half + HR, :], start=True, stop=True)
                m.then_inc(S["f_ps"], 1)

            def maxima(b, t):
                if t == 0:
                    wait(pe, "fh_sb", 3 * b + 3)
                    wait(pe, "fl_sb", 2 * b + 2)
                for half in range(2):
                    if t >= 2:
                        wait(pe, "mxh_sb", 2 * (T * b + t) + half - 3)
                    mm(rows((PA, PC)[t % 2], half), f2[:, 128 * t:128 * (t + 1)], rows(f3, half), start=True, stop=True).then_inc(S["s_ps"], 1)

            def maxrow(b, _):
                wait(pe, "nml_sb", b + 1)
                for t in range(T):
                    m = mm(PC[0:65, 128 * t:128 * (t + 1)], nm[:, t, :], identr[:], start=True, stop=True)
                m.then_inc(S["nmrow_ps"], 1)
                for j in range(T):
                    m = nc.tensor.transpose(PA[:, j * 32:(j + 1) * 32], f1[:, 128 * j:128 * (j + 1)], ident[96:128, 96:128])
                m.then_inc(S["f1T_ps"], 1)

            def weigh(b, j):
                def values(j):
                    for half in range(2):
                        wait(pe, "e_sb", 2 * (T * b + j) + half + 1)
                        m = mm(PC[32 * (j % 4):32 * (j % 4) + 32, half * HALF:(half + 1) * HALF], f1T[:, j, :],
                               rows(E[:, j % 2, :], half), start=j < 4, stop=j >= 4)
                    m.then_inc(S["pv_ps"], 1)

                if j == 0:
                    wait(pe, "nmrow_sb", b + 1)
                    wait(pe, "nmlow_sb", b + 1)
                    wait(pe, "f1T_sb", b + 1)
                for half in range(2):
                    if j >= 1:
                        wait(pe, "e_sb", 2 * (T * b + j) + half - 1)
                    mm(rows(PA, half), f3[:, 128 * j:128 * (j + 1)], rows(f2, half), start=True, stop=True).then_inc(S["st_ps"], 1)
                if j >= 1:
                    values(j - 1)
                if j == T - 1:
                    values(j)

            def attend(b, part):
                if part == 0:
                    wait(pe, "U_sb", b + 1)
                    for t in range(T):
                        m = mm(PA[:, t * 32:(t + 1) * 32], U[:, 128 * t:128 * (t + 1)], w("gsum"), start=True, stop=True)
                    m.then_inc(S["us_ps"], 1)
                if part == 1:
                    wait(pe, "mixT_sb", b + 1)
                    for t in range(T):
                        m = nc.tensor.transpose(PC[0:32, 128 * t:128 * (t + 1)], mixT[:, t, :], ident)
                        if t % 4 == 3:
                            m.then_inc(S["mix_ps"], 1)
                if part == 2:
                    for half in range(2):
                        wait(pe, "mixed_sb", 2 * b + half + 1)
                        mm(rows(PA, half), w("coT")[96:128, :], rows(mixed, half), start=True, stop=True).then_inc(S["co_ps"], 1)

            def mean_(b, _):
                wait(pe, "stat_sb", b + 1)
                mm(PT[:, 0:1], mean[:], mv[:, 0:1], start=True, stop=True).then_inc(S["mu_ps"], 1)

            def variance(b, _):
                wait(pe, "dev_sb", b + 1)
                mm(PT[:, 1:2], mean[:], gs[:, 1:2], start=True, stop=True).then_inc(S["var_ps"], 1)

            def project(b, _):
                wait(pe, "y0_sb", b + 1)
                mm(PT[:, 0:NP], w("winY"), y0, start=True, stop=True)
                mm(PT[:, NP:2 * NP], w("winG"), y0, start=True, stop=True).then_inc(S["yw_ps"], 1)

            def deltas(b, _):
                wait(pe, "y2_sb", b + 1)
                wait(pe, "gate_sb", b + 1)
                mm(PT[:, 0:NP], w("wd"), y2, start=True, stop=True)
                mm(PT[:, NP:2 * NP], w("wv"), y2, start=True, stop=True).then_inc(S["dv_ps"], 1)

            def scan(b, _):
                wait(pe, "yg_sb", 2 * b + 2)
                mm(PT[:, 0:NP], w("wout"), yg, start=True, stop=True).then_inc(S["z_ps"], 1)

            def hidden(b, half):
                wait(pe, "x3_sb", 2 * b + 2)
                if half:
                    wait(pe, "s4_sb", 8 * b + 4)
                mm(PT[:], w("w1T"), rows(x3[:].rearrange("p a b -> p (a b)"), half), start=True, stop=True).then_inc(S["w1_ps"], 1)

            def offset(b, half):
                wait(pe, "s4_sb", 8 * b + 8)
                if half:
                    wait(pe, "off_sb", 2 * b + 1)
                for q4 in range(4):
                    by, bx = 2 * (q4 // 2), 2 * (q4 % 2)
                    m = mm(PT[0:27, :], w("woff")[:, q4 * 27:(q4 + 1) * 27],
                           S4[:, by + HR * half:by + HR * half + HR, bx:bx + W], start=q4 == 0, stop=q4 == 3)
                m.then_inc(S["off_ps"], 1)

            def quads_(b, n):
                if n == 0:
                    wait(pe, "off_sb", 2 * b + 2)
                    for t in range(T):
                        src, dst = off[:, 128 * t:128 * (t + 1)], PT[:, t * 27:(t + 1) * 27]
                        if t == 0:
                            m = mm(dst, src, ident[96:123, 96:123], start=True, stop=True)
                        else:
                            m = nc.tensor.transpose(dst, src, ident[96:123, 96:123])
                    m.then_inc(S["offT_ps"], 1)
                    wait(pe, "offT_sb", b + 1)
                else:
                    wait(pe, "quads_sb", 3 * b + n)
                s4f = S4[:].rearrange("p a b -> p (a b)")
                for t in range(4 * n, min(4 * n + 4, QT)):
                    m = nc.tensor.transpose(PT[0:QP, (t % 4) * 128:(t % 4 + 1) * 128], s4f[:, QP * t:QP * (t + 1)], ident)
                m.then_inc(S["tab_ps"], 1)

            def sample(b, t):
                if t == 0:
                    wait(pe, "o_sb", 2 * b)
                else:
                    wait(pe, "sT_sb", T * b + t)
                if t == 4:
                    wait(pe, "h3_sb", 2 * b + 1)
                wait(pe, "sm_sb", T * b + t + 1)
                for g in range(3):
                    m = nc.tensor.transpose(PS[0:96, g * 128:(g + 1) * 128], sm[:, t % 2, g * 96:(g + 1) * 96], ident)
                m.then_inc(S["tr_ps"], 1)

            def mix(b, half):
                wait(pe, "sT_sb", T * b + 4 * half + 4)
                for g in range(3):
                    m = mm(PS[0:CB, :], w("w2T")[0:96, g * CB:(g + 1) * CB], sT[:, g, :], start=g == 0, stop=g == 2)
                m.then_inc(S["dcn_ps"], 1)

            def deform(b, half):
                wait(pe, "h3_sb", 2 * b + 2)
                if half:
                    wait(pe, "o_sb", 2 * b + 1)
                mm(PS[:], w("w3T")[96:128, :], rows(h3, half), start=True, stop=True).then_inc(S["w3_ps"], 1)

            run(pe, {"taps": taps, "keys": keys, "tapsum": tapsum, "keyvalue": keyvalue, "maxima": maxima, "fold": fold,
                     "maxrow": maxrow, "weigh": weigh, "numerator": numerator, "turn": turn, "attend": attend,
                     "conv1": conv1, "conv2": conv2, "mean": mean_, "variance": variance, "project": project,
                     "deltas": deltas, "scan": scan, "hidden": hidden, "offset": offset, "quads": quads_,
                     "sample": sample, "mix": mix, "deform": deform})

        @block.scalar
        def _(act):
            a_ = nc.scalar.activation

            act.wait_ge(S["w_in"], 16)
            a_(identr[:], w("ident"), ACT.Copy).then_inc(S["wh_sb"], 1)
            act.wait_ge(S["bnv_sb"], 3)
            a_(bnt[:], bnt[:], ACT.Sqrt).then_inc(S["bnr_sb"], 1)
            act.wait_ge(S["p_in"], 16)
            a_(wkvq[:, 0, :], cstage[:, 18 * C:21 * C], ACT.Copy).then_inc(S["wh_sb"], 1)
            act.wait_ge(S["wh_sb"], 2)
            act.wait_ge(S["init_v"], 1)
            act.wait_ge(S["zeroed"], 12)
            a_(sqj[:, 0:1], ones[:, 0:1], ACT.Copy).then_inc(S["init_a"], 1)

            def split_x(b, _):
                wait(act, "x_in", 16 * b + 16)
                wait(act, "num_ps", 3 * b)
                a_(xs[:, 0, :], xin[:], ACT.Copy).then_inc(S["xh_sb"], 1)

            def keys(b, t):
                wait(act, "kvt_sb", T * b + t + 1)
                if t:
                    act.wait_ge(S["ksq_sb"], T * b + t)
                a_(sqj[:], kvt[:, t, 1:1 + C], ACT.Square, accum_out=nss[:, 0, t:t + 1]).then_inc(S["ksq_sb"], 1)
                wait(act, "qs_sb", T * b + t + 1)
                a_(qs[:, t % 2, :], qs[:, t % 2, :], ACT.Square, accum_out=nss[:, 1, t:t + 1]).then_inc(S["qsq_sb"], 1)

            def norms(b, _):
                wait(act, "ksq_sb", T * b + T)
                wait(act, "qsq_sb", T * b + T)
                nf = nss[:].rearrange("p a t -> p (a t)")
                a_(nf, nf, ACT.Sqrt).then_inc(S["nss_rt"], 1)
                if isinstance(b, int) and b == 0:
                    act.wait_ge(S["c_in"], 16)
                    for n, cw in enumerate((c1, c2)):
                        a_(cw[:, 0, :], cstage[:, n * 9 * C:(n + 1) * 9 * C], ACT.Copy).then_inc(S["wh_sb"], 1)

            def keyvalue(b, _):
                wait(act, "kv_ps", b + 1)
                a_(kv[:], PD[:, 0:C + 1], ACT.Copy).then_inc(S["kv_sb"], 1)

            def fold(b, part):
                if part == 0:
                    wait(act, "m2_ps", 2 * b + 1)
                    a_(m2[:, 0:C], PD[:, 0:C], ACT.Copy).then_inc(S["m2_sb"], 1)
                    wait(act, "m2_ps", 2 * b + 2)
                    a_(rvr[:], PD[:, HALF:HALF + C], ACT.Copy).then_inc(S["rvr_sb"], 1)
                else:
                    wait(act, "m3_ps", 2 * b + 1)
                    a_(m3[:, 0, :], PD[:, 0:MC], ACT.Copy).then_inc(S["m3h_sb"], 1)
                    wait(act, "m3_ps", 2 * b + 2)
                    a_(mb[:], PD[:, HALF:HALF + MC], ACT.Copy).then_inc(S["mb_sb"], 1)

            def turn(b, half):
                wait(act, "turn_ps", 2 * b + half + 1)
                a_(attn[:, 0, 1 + HR * half:1 + HR * half + HR, 1:W + 1], image(rows(PD, half), W), ACT.Identity,
                   bias=vec("rb")).then_inc(S["ah_sb"], 1)

            def conv1(b, part):
                if part == 2 * PARTS - 1:
                    wait(act, "c1_ps", 2 * b + 2)
                    for half in range(2):
                        a_(attn[:, 0, 1 + HR * half:1 + HR * half + HR, 1:W + 1], image(rows(PD, half), W),
                           ACT.Identity, bias=vec("c1b")).then_inc(S["hh_sb"], 1)

            def residual(b, _):
                wait(act, "x1_sb", 2 * b + 2)
                wait(act, "tap_ps", 3 * b)
                a_(x1p[:, 0, :, PADD:PADD + W], x1[:], ACT.Copy).then_inc(S["x1h_sb"], 1)

            def taps(b, n):
                i, ps = TAPS[n]
                d = DIL[i]
                wait(act, "tap_ps", 3 * b + n + 1)
                wait(act, "f_ps", 3 * b)
                for dy in range(3):
                    s = slice(32 * dy, 32 * dy + 32)
                    to = slice(max(0, (1 - dy) * d), H + min(0, (1 - dy) * d))
                    fr = slice(max(0, (dy - 1) * d), H + min(0, (dy - 1) * d))
                    a_(Y[s, i, to, :], image(ps[s, :], W)[:, fr, :], ACT.Copy).then_inc(S["Y_sb"], 1)

            def tapsum(b, n):
                i, _ = TAPS[n]
                m_out, ps = TAPSUM[n]
                dst = (f2[:, :], f3[:, :], f1)[n]
                wait(act, "f_ps", 3 * b + n + 1)
                a_(dst, ps[0:m_out, :], ACT.Identity, bias=fbias[0:m_out, i:i + 1]).then_inc(S["fh_sb"], 1)

            def maxrow(b, _):
                wait(act, "nmrow_ps", b + 1)
                a_(f2[0:1, :], PC[0:1, :], ACT.Copy).then_inc(S["nmrow_sb"], 1)
                wait(act, "f1T_ps", b + 1)
                a_(f1T[:].rearrange("p a b -> p (a b)"), PA[:, 0:T * 32], ACT.Copy).then_inc(S["f1T_sb"], 1)

            def weigh(b, j):
                if j >= 2:
                    wait(act, "pv_ps", T * b + j - 1)
                for half in range(2):
                    wait(act, "st_ps", 2 * (T * b + j) + half + 1)
                    a_(rows(E[:, j % 2, :], half), rows(PA, half), ACT.Exp).then_inc(S["e_sb"], 1)

            def attend(b, part):
                if part == 0:
                    wait(act, "pv_ps", T * b + T)
                    a_(U, PC[:], ACT.Copy).then_inc(S["U_sb"], 1)
                if part == 1:
                    for half in range(2):
                        wait(act, "mix_ps", 2 * b + half + 1)
                        a_(rows(mixed, half), PC[0:32, half * HALF:(half + 1) * HALF], ACT.Copy).then_inc(S["mixed_sb"], 1)

            def variance(b, _):
                wait(act, "gnv_sb", b + 1)
                a_(gs[:, 7:8], gs[:, 7:8], ACT.Sqrt).then_inc(S["gn_rt"], 1)

            def project(b, _):
                wait(act, "yw_ps", b + 1)
                yw = image(PT[:, 0:NP], w2)
                a_(ypad[0:INNER, 1:h2 + 1, 1:w2 + 1], yw[0:INNER], ACT.Copy).then_inc(S["ypad_sb"], 1)
                a_(ypad[INNER:128, 1:w2 + 1, 1:h2 + 1], yw[INNER:128].rearrange("p a b -> p b a"), ACT.Copy)\
                    .then_inc(S["ypad_sb"], 1)
                a_(gate, PT[:, NP:2 * NP], ACT.Sigmoid).then_inc(S["gate_sb"], 1)

            def deltas(b, _):
                wait(act, "y1_sb", 9 * b + 9)
                a_(es, y1, ACT.Sigmoid).then_inc(S["es_sb"], 1)
                wait(act, "dv_ps", b + 1)
                a_(dl, PT[:, 0:NP], ACT.Sigmoid, bias=vec("bd")).then_inc(S["dl_sb"], 1)

            def scan(b, _):
                wait(act, "z_ps", b + 1)
                z = image(PT[:, 0:NP], w2)
                for dst, src in ((slice(1, w2 + 1), slice(0, w2)), (slice(0, 1), slice(0, 1)),
                                 (slice(w2 + 1, w2 + 2), slice(w2 - 1, w2))):
                    a_(zp[:, :, dst], z[:, :, src], ACT.Copy, scale=1.0 / 64).then_inc(S["zp_sb"], 1)

            def hidden(b, half):
                wait(act, "w1_ps", 2 * b + half + 1)
                for g in range(4):
                    dy, dx = divmod(g, 2)
                    s = slice(32 * g, 32 * g + 32)
                    y = 1 - dy + HR * half
                    a_(S4[s, y:y + HR, 1 - dx:W + 1 - dx], image(PT[s, :], W), ACT.Relu, scale=bns[s, 0:1],
                       bias=bnb[s, 0:1]).then_inc(S["s4_sb"], 1)

            def offset(b, half):
                wait(act, "off_ps", 2 * b + half + 1)
                a_(rows(off, half), PT[0:27, :], ACT.Identity, bias=vec("boff", 0, 27)).then_inc(S["off_sb"], 1)

            def quads_(b, n):
                wait(act, "tab_ps", 3 * b + n + 1)
                first, last = 4 * n, min(4 * n + 4, QT)
                a_(quads[:, first:last, :].rearrange("p a b -> p (a b)"), PT[0:QP, 0:(last - first) * 128],
                   ACT.Copy).then_inc(S["quads_sb"], 1)

            def indices(b, _):
                wait(act, "offT_sb", b + 1)
                a_(em[:], offT[:, :, 18:27], ACT.Sigmoid).then_inc(S["em_sb"], 1)

            def carry(b, _):
                wait(act, "x3_sb", 2 * b + 2)
                wait(act, "stored", 16 * b)
                a_(res[:], x3[:].rearrange("p a b -> p (a b)"), ACT.Copy).then_inc(S["res_sb"], 1)

            def sample(b, t):
                wait(act, "tr_ps", T * b + t + 1)
                if t in (0, 4):
                    wait(act, "dcn_ps", 2 * b + t // 4)
                a_(sT[:, :, 128 * (t % 4):128 * (t % 4 + 1)], PS[0:96, 0:384].rearrange("p (g n) -> p g n", g=3), ACT.Copy)\
                    .then_inc(S["sT_sb"], 1)

            def mix(b, half):
                wait(act, "dcn_ps", 2 * b + half + 1)
                a_(rows(h3, half), PS[0:CB, :], ACT.Relu, scale=bns[0:CB, 1:2], bias=bnb[0:CB, 1:2]).then_inc(S["h3_sb"], 1)

            def deform(b, half):
                if half:
                    wait(act, "o_sb", 2 * b + 2)
                    a_(res[:], res[:], ACT.Relu, bias=bnb[:, 2:3]).then_inc(S["ob_sb"], 1)

            run(act, {"split_x": split_x, "keys": keys, "norms": norms, "keyvalue": keyvalue, "fold": fold, "turn": turn,
                      "conv1": conv1, "residual": residual, "taps": taps, "tapsum": tapsum,
                      "maxrow": maxrow, "weigh": weigh, "attend": attend, "variance": variance, "project": project,
                      "deltas": deltas, "scan": scan, "hidden": hidden, "offset": offset, "quads": quads_,
                      "indices": indices, "carry": carry, "sample": sample, "mix": mix, "deform": deform})

        @block.vector
        def _(dve):
            v = nc.vector

            def low(out, value, high):
                return v.tensor_tensor(out, value, high.bitcast(F32), ALU.subtract)

            dve.wait_ge(S["w_in"], 16)
            bn_names = ("bn1", "bn2", "bn3")
            for i, name in enumerate(bn_names):
                v.tensor_scalar(bnt[:, i:i + 1], vec(name, 3), EPS_BN, None, ALU.add).then_inc(S["bnv_sb"], 1)
            pwT = w("pwT").rearrange("p (i r) -> p i r", i=3)
            dww = w("dww").rearrange("p (i t) -> p i t", i=3)
            for i in range(3):
                v.tensor_tensor(wstage[:, 9 * i:9 * i + 9, :], pwT[:, i:i + 1, :].to_broadcast([128, 9, R]),
                                dww[:, i, :].unsqueeze(2).to_broadcast([128, 9, R]), ALU.mult).then_inc(S["consts"], 1)
            dve.wait_ge(S["consts"], 3)
            for i in range(3):
                src = wstage[:, 9 * i:9 * i + 9, :].rearrange("p (y x) r -> p x y r", y=3)
                v.tensor_copy(wf[:, i, :, :, 0:R], src).then_inc(S["consts"], 1)
            dve.wait_ge(S["consts"], 6)
            for i in range(3):
                src = wstage[:, 9 * i:9 * i + 9, :].rearrange("p (y x) r -> p x y r", y=3)
                low(wf[:, i, :, :, R:2 * R], src, wf[:, i, :, :, 0:R]).then_inc(S["consts"], 1)
            dve.wait_ge(S["bias_ps"], 1)
            v.tensor_tensor(fbias[:], PA[0:96, 0:3], w("pwb")[0:96, :], ALU.add).then_inc(S["consts"], 1)
            dve.wait_ge(S["bnr_sb"], 1)
            v.reciprocal(bnr[:], bnt[:]).then_inc(S["bnr_sb"], 1)
            dve.wait_ge(S["bnr_sb"], 2)
            for i, name in enumerate(bn_names):
                v.tensor_tensor(bns[:, i:i + 1], bnr[:, i:i + 1], vec(name, 0), ALU.mult).then_inc(S["consts"], 1)
                if i == 1:
                    v.tensor_tensor(bnt[:, 1:2], vec(name, 4), vec(name, 2), ALU.subtract).then_inc(S["consts"], 1)
                else:
                    v.tensor_scalar(bnt[:, i:i + 1], vec(name, 2), -1.0, None, ALU.mult).then_inc(S["consts"], 1)
                dve.wait_ge(S["consts"], 12 + 3 * i)
                v.scalar_tensor_tensor(bnb[:, i:i + 1], bnt[:, i:i + 1], bns[:, i:i + 1], vec(name, 1),
                                       ALU.mult, ALU.add).then_inc(S["consts"], 1)
            v.tensor_scalar(c2b1[:], vec("c2b"), 1.0, None, ALU.add).then_inc(S["consts"], 1)
            v.tensor_scalar(qbr[:], w("ident"), 0.0, vec("qb"), ALU.mult, ALU.add).then_inc(S["consts"], 1)
            dve.wait_ge(S["wh_sb"], 2)
            low(wkvq[:, 1, :], cstage[:, 18 * C:21 * C], wkvq[:, 0, :]).then_inc(S["wl_sb"], 1)
            dve.wait_ge(S["wl_sb"], 1)
            dve.wait_ge(S["consts"], 21)
            dve.wait_ge(S["zeroed"], 12)
            v.memset(gs[:], 0.0).then_inc(S["init_v"], 1)

            def split_x(b, _):
                wait(dve, "xh_sb", b + 1)
                low(xs[:, 1, :], xin[:], xs[:, 0, :]).then_inc(S["xl_sb"], 1)

            def keys(b, t):
                if t == 0:
                    wait(dve, "turn_ps", 2 * b)
                wait(dve, "kvt_ps", T * b + t + 1)
                ps = PD[:, (t % 2) * HALF:(t % 2) * HALF + 3 * C]
                v.tensor_tensor(kvt[:, t, 1:], ps[:, 0:2 * C], w("kvqb")[:, 0:2 * C], ALU.add).then_inc(S["kvt_sb"], 1)
                wait(dve, "qsq_sb", T * b + t - 1)
                v.tensor_tensor(qs[:, t % 2, :], ps[:, 2 * C:3 * C], w("kvqb")[:, 2 * C:3 * C], ALU.add).then_inc(S["qs_sb"], 1)

            def norms(b, _):
                v.memset(kvt[:, :, 0:1], 1.0).then_inc(S["krn_sb"], 1)
                wait(dve, "nss_rt", b + 1)
                v.reciprocal(krn[:], nss[:, 0, :]).then_inc(S["krn_sb"], 1)
                wait(dve, "krn_sb", 2 * b + 2)
                v.tensor_tensor(kvt[:, :, 1:1 + C], kvt[:, :, 1:1 + C], krn[:].unsqueeze(2).to_broadcast([128, T, C]), ALU.mult)\
                    .then_inc(S["kn_sb"], 1)

            def keyvalue(b, _):
                if isinstance(b, int) and b == 0:
                    for n, cw in enumerate((c1, c2)):
                        dve.wait_ge(S["wh_sb"], 3 + n)
                        low(cw[:, 1, :], cstage[:, n * 9 * C:(n + 1) * 9 * C], cw[:, 0, :]).then_inc(S["wl_sb"], 1)
                wait(dve, "kn_sb", b + 1)
                v.tensor_reduce(ktot[:], kvt[:, :, 1:1 + C].rearrange("p t k -> p k t"), AX_X, ALU.add).then_inc(S["ktot_sb"], 1)
                wait(dve, "kv_ps", b + 1)
                v.tensor_copy(m2[:, C:C + 1], PD[:, HALF:HALF + 1]).then_inc(S["ksum_sb"], 1)
                wait(dve, "kv_sb", b + 1)
                v.tensor_scalar(vsr[:], ones[:], kv[:, 0:1], None, ALU.mult).then_inc(S["vsr_sb"], 1)

            def fold(b, part):
                if part == 1:
                    wait(dve, "m3h_sb", b + 1)
                    low(m3[:, 1, :], PD[:, 0:MC], m3[:, 0, :]).then_inc(S["m3l_sb"], 1)

            def numerator(b, part):
                wait(dve, "num_ps", 3 * b + part + 1)
                if part == 0:
                    wait(dve, "mb_sb", b + 1)
                tiles = PHASES[part]
                c0 = (part % 2) * HALF
                v.tensor_tensor(num[:, tiles[0]:tiles[-1] + 1, :],
                                PD[:, c0:c0 + len(tiles) * MC].rearrange("p (t n) -> p t n", n=MC),
                                mb[:].unsqueeze(1).to_broadcast([128, len(tiles), MC]), ALU.add).then_inc(S["num_sb"], 1)
                if part == 2:
                    wait(dve, "num_sb", 3 * b + 3)
                    v.scalar_tensor_tensor(rden[:], nss[:, 1, :], N + EPS_L0, num[:, :, C], ALU.mult, ALU.add)\
                        .then_inc(S["den_sb"], 1)
                    wait(dve, "den_sb", b + 1)
                    v.reciprocal(rden[:], rden[:]).then_inc(S["rec_sb"], 1)

            def turn(b, half):
                tiles = slice(4 * half, 4 * half + 4)
                for t in range(4 * half, 4 * half + 4):
                    v.scalar_tensor_tensor(num[:, t, 0:C], rvr[:], nss[:, 1, t:t + 1], num[:, t, 0:C], ALU.mult, ALU.add)\
                        .then_inc(S["add_sb"], 1)
                wait(dve, "rec_sb", b + 1)
                wait(dve, "add_sb", T * b + 4 * half + 4)
                v.tensor_tensor(num[:, tiles, 0:C], num[:, tiles, 0:C], rden[:, tiles].unsqueeze(2).to_broadcast([128, 4, C]),
                                ALU.mult).then_inc(S["attn_raw"], 1)
                wait(dve, "ah_sb", 2 * b + half + 1)
                s = slice(1 + HR * half, 1 + HR * half + HR)
                v.scalar_tensor_tensor(attn[:, 1, s, 1:W + 1], image(rows(PD, half), W), vec("rb"),
                                       attn[:, 0, s, 1:W + 1].bitcast(F32), ALU.add, ALU.subtract).then_inc(S["al_sb"], 1)

            def conv1(b, part):
                if part == 2 * PARTS - 1:
                    for half in range(2):
                        s = slice(1 + HR * half, 1 + HR * half + HR)
                        wait(dve, "hh_sb", 2 * b + half + 1)
                        v.scalar_tensor_tensor(attn[:, 1, s, 1:W + 1], image(rows(PD, half), W), vec("c1b"),
                                               attn[:, 0, s, 1:W + 1].bitcast(F32), ALU.add, ALU.subtract)\
                            .then_inc(S["hl_sb"], 1)

            def conv2(b, part):
                if part % PARTS == PARTS - 1:
                    half = part // PARTS
                    s = slice(HR * half, HR * half + HR)
                    xh = image(rows(xres, half), W)
                    if half == 0:
                        wait(dve, "xres_in", 16 * b + 16)
                        wait(dve, "x2_sb", 2 * b)
                        wait(dve, "x1h_sb", b)
                    wait(dve, "c2_ps", 2 * b + half + 1)
                    v.scalar_tensor_tensor(x1[:, s, :], image(rows(PD, half), W), c2b1[:, 0:1], xh, ALU.add, ALU.mult)\
                        .then_inc(S["x1_sb"], 1)

            def residual(b, _):
                wait(dve, "x1h_sb", b + 1)
                low(x1p[:, 1, :, PADD:PADD + W], x1[:], x1p[:, 0, :, PADD:PADD + W]).then_inc(S["x1l_sb"], 1)

            def tapsum(b, n):
                if n == 2:
                    return
                i, _ = TAPS[n]
                m_out, ps = TAPSUM[n]
                f, s = ((f2, slice(64, 96)), (f3, slice(32, 64)))[n]
                wait(dve, "fh_sb", 3 * b + n + 1)
                v.scalar_tensor_tensor(f[s, :], ps[s, :], fbias[s, i:i + 1], f[s, :].bitcast(F32), ALU.add, ALU.subtract)\
                    .then_inc(S["fl_sb"], 1)

            def maxima(b, t):
                for half in range(2):
                    wait(dve, "s_ps", 2 * (T * b + t) + half + 1)
                    v.tensor_reduce(mxh[:, t, half:half + 1], rows((PA, PC)[t % 2], half), AX_X, ALU.max).then_inc(S["mxh_sb"], 1)
                if t == T - 1:
                    wait(dve, "mxh_sb", 2 * T * (b + 1))
                    v.tensor_tensor(mx[:], mxh[:, :, 0], mxh[:, :, 1], ALU.max).then_inc(S["mx_sb"], 1)
                    wait(dve, "mx_sb", b + 1)
                    v.tensor_scalar(nm[:, :, 0], mx[:], -1.0, None, ALU.mult).then_inc(S["nmh_sb"], 1)
                    wait(dve, "nmh_sb", b + 1)
                    v.scalar_tensor_tensor(nm[:, :, 64], mx[:], -1.0, nm[:, :, 0].bitcast(F32), ALU.mult, ALU.subtract)\
                        .then_inc(S["nml_sb"], 1)

            def maxrow(b, _):
                wait(dve, "nmrow_ps", b + 1)
                v.tensor_copy(f2[64:65, :], PC[64:65, :]).then_inc(S["nmlow_sb"], 1)

            def attend(b, part):
                if part == 0:
                    wait(dve, "us_ps", b + 1)
                    us = PA[:, 0:T * 32].rearrange("p (t n) -> p t n", n=32)
                    v.reciprocal(mrd[:], us[:, :, 0]).then_inc(S["mrd_sb"], 1)
                    wait(dve, "mrd_sb", b + 1)
                    v.tensor_tensor(mixT[:], us, mrd[:].unsqueeze(2).to_broadcast([128, T, 32]), ALU.mult).then_inc(S["mixT_sb"], 1)
                if part == 2:
                    for half in range(2):
                        s = slice(HR * half, HR * half + HR)
                        wait(dve, "co_ps", 2 * b + half + 1)
                        v.tensor_tensor(x2[:, s, :], image(rows(PA, half), W), x1[:, s, :], ALU.add).then_inc(S["x2_sb"], 1)

            def mean_(b, _):
                wait(dve, "x2_sb", 2 * b + 2)
                wait(dve, "table_in", 16 * b)
                x2f = x2[:].rearrange("p a b -> p (a b)")
                for half in range(2):
                    v.bn_stats(st[:, half, :], rows(x2f, half)).then_inc(S["stats_sb"], 1)
                wait(dve, "stats_sb", 2 * b + 2)
                v.tensor_tensor(p1, x2[:, 0:H:2, :], x2[:, 1:H:2, :], ALU.add).then_inc(S["p1_sb"], 1)
                v.bn_aggr(mv[:], st[:].rearrange("p a b -> p (a b)")).then_inc(S["stat_sb"], 1)
                wait(dve, "p1_sb", b + 1)
                v.tensor_tensor(image(p2, w2), p1[:, :, 0:W:2], p1[:, :, 1:W:2], ALU.add).then_inc(S["p2_sb"], 1)
                wait(dve, "mu_ps", b + 1)
                wait(dve, "stat_sb", b + 1)
                v.tensor_tensor(gs[:, 0:1], mv[:, 0:1], PT[:, 0:1], ALU.subtract).then_inc(S["dm_sb"], 1)
                v.tensor_scalar(gs[:, 2:3], PT[:, 0:1], -1.0, None, ALU.mult).then_inc(S["dm_sb"], 1)
                wait(dve, "dm_sb", 2 * b + 2)
                v.scalar_tensor_tensor(gs[:, 1:2], gs[:, 0:1], gs[:, 0:1], mv[:, 1:2], ALU.mult, ALU.add).then_inc(S["dev_sb"], 1)

            def variance(b, _):
                n = 4 * b
                wait(dve, "var_ps", b + 1)
                v.tensor_scalar(gs[:, 7:8], PT[:, 1:2], EPS_GN, None, ALU.add).then_inc(S["gnv_sb"], 1)
                wait(dve, "gn_rt", b + 1)
                v.reciprocal(gs[:, 3:4], gs[:, 7:8]).then_inc(S["gn_sb"], 1)
                wait(dve, "gn_sb", n + 1)
                v.tensor_tensor(gs[:, 4:5], gs[:, 3:4], vec("gnw"), ALU.mult).then_inc(S["gn_sb"], 1)
                wait(dve, "gn_sb", n + 2)
                v.scalar_tensor_tensor(gs[:, 5:6], gs[:, 2:3], gs[:, 4:5], vec("gnb"), ALU.mult, ALU.add).then_inc(S["gn_sb"], 1)
                v.tensor_scalar(gs[:, 6:7], gs[:, 4:5], 0.25, None, ALU.mult).then_inc(S["gn_sb"], 1)
                wait(dve, "gn_sb", n + 4)
                wait(dve, "p2_sb", b + 1)
                v.tensor_scalar(y0, p2, gs[:, 6:7], gs[:, 5:6], ALU.mult, ALU.add).then_inc(S["y0_sb"], 1)

            def project(b, _):
                wait(dve, "ypad_sb", 2 * b + 2)
                for tap in range(9):
                    src = ypad[:, tap // 3:tap // 3 + h2, tap % 3:tap % 3 + w2]
                    if tap == 0:
                        v.tensor_scalar(image(y1, w2), src, vec("dwk", 0), None, ALU.mult).then_inc(S["y1_sb"], 1)
                    else:
                        wait(dve, "y1_sb", 9 * b + tap)
                        v.scalar_tensor_tensor(image(y1, w2), src, vec("dwk", tap), image(y1, w2), ALU.mult, ALU.add)\
                            .then_inc(S["y1_sb"], 1)

            def deltas(b, _):
                wait(dve, "es_sb", b + 1)
                v.tensor_tensor(y2, y1, es, ALU.mult).then_inc(S["y2_sb"], 1)
                wait(dve, "dl_sb", b + 1)
                d = image(dl, w2)
                v.tensor_scalar(af[:, :, 1:w2], d[:, :, 1:w2], -1.0, 1.0, ALU.mult, ALU.add).then_inc(S["scan_in"], 1)
                v.tensor_scalar(ab[:, :, 0:w2 - 1], d[:, :, 0:w2 - 1], -1.0, 1.0, ALU.mult, ALU.add).then_inc(S["scan_in"], 1)
                v.scalar_tensor_tensor(bb, PT[:, NP:2 * NP], vec("bv"), dl, ALU.add, ALU.mult).then_inc(S["scan_in"], 1)
                wait(dve, "scan_in", 3 * b + 3)
                v.tensor_tensor_scan(sf, af[:].rearrange("p a b -> p (a b)"), bb, 0.0, ALU.mult, ALU.add)\
                    .then_inc(S["scan_sb"], 1)
                v.tensor_tensor_scan(sr[:, ::-1], ab[:].rearrange("p a b -> p (a b)")[:, ::-1], bb[:, ::-1], 0.0,
                                     ALU.mult, ALU.add).then_inc(S["scan_sb"], 1)
                wait(dve, "scan_sb", 2 * b + 2)
                v.tensor_tensor(ss, sf, sr, ALU.add).then_inc(S["ss_sb"], 1)
                wait(dve, "ss_sb", b + 1)
                wait(dve, "gate_sb", b + 1)
                v.tensor_tensor(yg[0:INNER], ss[0:INNER], gate[0:INNER], ALU.mult).then_inc(S["yg_sb"], 1)
                v.tensor_tensor(image(yg[INNER:128], w2), image(ss[INNER:128], h2).rearrange("p a b -> p b a"),
                                image(gate[INNER:128], w2), ALU.mult).then_inc(S["yg_sb"], 1)

            def resize(b, _):
                wait(dve, "zp_sb", 3 * b + 3)
                mid = zp[:, :, 1:w2 + 1]
                for k in range(2):
                    v.scalar_tensor_tensor(up[:, 1:h2 + 1, k:W:2], mid, 3.0, zp[:, :, 2 * k:2 * k + w2], ALU.mult, ALU.add)\
                        .then_inc(S["up_sb"], 1)
                wait(dve, "up_sb", 2 * b + 2)
                v.tensor_copy(up[:, 0:1, :], up[:, 1:2, :]).then_inc(S["upe_sb"], 1)
                v.tensor_copy(up[:, h2 + 1:h2 + 2, :], up[:, h2:h2 + 1, :]).then_inc(S["upe_sb"], 1)
                wait(dve, "upe_sb", 2 * b + 2)
                wait(dve, "res_sb", b)
                for k in range(2):
                    v.scalar_tensor_tensor(x3[:, k:H:2, :], up[:, 1:h2 + 1, :], 3.0, up[:, 2 * k:2 * k + h2, :],
                                           ALU.mult, ALU.add).then_inc(S["rs_sb"], 1)
                for k in range(2):
                    wait(dve, "rs_sb", 2 * b + k + 1)
                    v.tensor_tensor(x3[:, k:H:2, :], x3[:, k:H:2, :], x2[:, k:H:2, :], ALU.add).then_inc(S["x3_sb"], 1)

            def indices(b, _):
                wait(dve, "offT_ps", b + 1)
                wait(dve, "wq3_sb", T * b)
                v.tensor_copy(offT[:].rearrange("p a b -> p (a b)"), PT[:, 0:T * 27]).then_inc(S["offT_sb"], 1)
                wait(dve, "offT_sb", b + 1)
                base = w("base").rearrange("p (t k) -> p t k", t=T)
                n = 8 * b
                v.tensor_tensor(uu[:], offT[:, :, 0:18], base, ALU.add).then_inc(S["ixs"], 1)
                wait(dve, "ixs", n + 1)
                v.tensor_scalar(uu[:], uu[:], 0.0, float(H + 1), ALU.max, ALU.min).then_inc(S["ixs"], 1)
                wait(dve, "ixs", n + 2)
                v.tensor_scalar(rr[:], uu[:], ROUND, None, ALU.add).then_inc(S["ixs"], 1)
                wait(dve, "ixs", n + 3)
                v.tensor_scalar(rr[:], rr[:], ROUND, None, ALU.subtract).then_inc(S["ixs"], 1)
                wait(dve, "ixs", n + 4)
                v.tensor_tensor(gg[:], rr[:], uu[:], ALU.is_gt).then_inc(S["ixs"], 1)
                wait(dve, "ixs", n + 5)
                v.tensor_tensor(rr[:], rr[:], gg[:], ALU.subtract).then_inc(S["ixs"], 1)
                wait(dve, "ixs", n + 6)
                v.tensor_scalar(u0[:], rr[:], float(H), None, ALU.min).then_inc(S["ixs"], 1)
                wait(dve, "ixs", n + 7)
                v.scalar_tensor_tensor(ixf[:], u0[:, :, 0:18:2], float(QS), u0[:, :, 1:18:2], ALU.mult, ALU.add)\
                    .then_inc(S["ixs"], 1)
                v.tensor_tensor(wt1[:], uu[:], u0[:], ALU.subtract).then_inc(S["wt1_sb"], 1)
                wait(dve, "wt1_sb", b + 1)
                m = 3 * b
                v.tensor_scalar(wt0[:], wt1[:], -1.0, 1.0, ALU.mult, ALU.add).then_inc(S["wq_sb"], 1)
                wait(dve, "em_sb", b + 1)
                wait(dve, "wq_sb", m + 1)
                v.tensor_tensor(ay[:, 0], wt0[:, :, 0:18:2], em[:], ALU.mult).then_inc(S["wq_sb"], 1)
                v.tensor_tensor(ay[:, 1], wt1[:, :, 0:18:2], em[:], ALU.mult).then_inc(S["wq_sb"], 1)

            def index(b, _):
                wait(dve, "ixs", 8 * b + 8)
                if not (isinstance(b, int) and b == 0):
                    for t in range(T):
                        dve.wait_ge(gathered[t], 144 * b)
                v.tensor_copy(ix[:], ixf[:].rearrange("p a b -> p (a b)")).then_inc(S["ix_sb"], 1)

            def corners(b, _):
                wait(dve, "wq_sb", 3 * b + 3)
                for g in range(3):
                    wx = (wt0, wt1)[g % 2]
                    v.tensor_tensor(wq[:, :, :, g], ay[:, g // 2], wx[:, :, 1:18:2], ALU.mult).then_inc(S["corner_sb"], 1)

            def sample(b, t):
                if t == 0:
                    wait(dve, "corner_sb", 3 * b + 3)
                wait(dve, "wq3_sb", T * b + t + 1)
                dve.wait_ge(gathered[t], 144 * b + 144)
                Gt = G[:, t].rearrange("p k (g c) -> p k g c", g=4)
                v.tensor_tensor(Gt, Gt, wq[:, t].unsqueeze(3).to_broadcast([128, 9, 4, CB]), ALU.mult).then_inc(S["gw_sb"], 1)
                wait(dve, "gw_sb", T * b + t + 1)
                v.tensor_tensor(G[:, t, :, 0:64], G[:, t, :, 0:64], G[:, t, :, 64:128], ALU.add).then_inc(S["g2_sb"], 1)
                wait(dve, "g2_sb", T * b + t + 1)
                if t >= 2:
                    wait(dve, "tr_ps", T * b + t - 1)
                v.tensor_tensor(sm[:, t % 2].rearrange("p (k c) -> p k c", k=9), G[:, t, :, 0:32], G[:, t, :, 32:64],
                                ALU.add).then_inc(S["sm_sb"], 1)

            def deform(b, half):
                wait(dve, "res_sb", b + 1)
                wait(dve, "w3_ps", 2 * b + half + 1)
                v.scalar_tensor_tensor(rows(res, half), PS[:], bns[:, 2:3], rows(res, half), ALU.mult, ALU.add)\
                    .then_inc(S["o_sb"], 1)

            run(dve, {"split_x": split_x, "keys": keys, "norms": norms, "keyvalue": keyvalue, "fold": fold,
                      "numerator": numerator, "turn": turn, "conv1": conv1, "conv2": conv2, "residual": residual,
                      "tapsum": tapsum, "maxima": maxima, "maxrow": maxrow, "attend": attend, "mean": mean_, "variance": variance,
                      "project": project, "deltas": deltas, "resize": resize, "indices": indices, "index": index,
                      "corners": corners, "sample": sample, "deform": deform})


def _columns(i, np):
    f = np.float32

    def full(a, rows=None):
        a = np.asarray(a, f)
        a = a.reshape(a.shape[0], -1)
        z = np.zeros((128, a.shape[1]), f)
        z[:a.shape[0]] = a
        return z

    def four(a):
        return np.concatenate([a] * 4, axis=0)

    l0 = lambda n: i["L0_conv_" + n]
    l1 = lambda n: i["L1_conv_" + n]
    l2 = lambda n: i["L2_conv_" + n]
    l3 = lambda n: i["L3_conv_" + n]
    r = {}
    r["kvqb"] = np.broadcast_to(np.concatenate([l0("kb"), l0("vb"), l0("qb")])[None, :], (128, 3 * C))
    r["qw"], r["rwT"] = l0("qw"), l0("rw").T
    r["ident"] = np.eye(128, dtype=f)
    pw = np.zeros((C, 3, 3, 32), f)
    pwb = np.zeros((3, 32, 3), f)
    pwb[:, 0, 0] = pwb[:, 0, 2] = 1.0
    for n in range(3):
        pw[:, n, :, 1:1 + R] = l1(f"c{n + 1}_pw_w")[:, :, 0, 0].T[:, None, :]
        pwb[:, 1:1 + R, n] = l1(f"c{n + 1}_pw_b")[None, :]
    r["pwS"], r["pwb"] = pw.reshape(C, -1), full(pwb.reshape(96, 3))
    r["pwT"] = np.ascontiguousarray(pw[:, :, 0, 1:1 + R]).reshape(C, -1)
    sel = np.zeros((3, 2, R, 3, 32), f)
    for c in range(R):
        sel[:, :, c, :, 1 + c] = 1.0
    r["sel"] = full(sel.reshape(96, 96))
    r["dww"] = np.concatenate([l1(f"c{n}_dw_w").reshape(C, 9) for n in (1, 2, 3)], axis=1)
    r["dwb"] = np.stack([l1(f"c{n}_dw_b") for n in (1, 2, 3)], axis=1)
    co = np.zeros((4, 32, C), f)
    co[:, 0] = l1("co_b")
    co[:, 1:1 + R] = l1("co_w")[:, :, 0, 0].T
    r["coT"], r["gsum"] = co.reshape(128, C), np.concatenate([np.eye(32, dtype=f)] * 4, axis=0)
    win = l2("w_in").T
    r["winY"] = np.concatenate([win[:, :INNER]] * 2, axis=1)
    r["winG"] = np.concatenate([win[:, INNER:]] * 2, axis=1)
    dwk = l2("w_dw").reshape(INNER, 3, 3)
    r["dwk"] = np.concatenate([dwk.reshape(INNER, 9), dwk.transpose(0, 2, 1).reshape(INNER, 9)], axis=0)
    for n in ("wd", "wv"):
        z = np.zeros((128, 128), f)
        z[:INNER, :INNER] = l2("row_" + n).T
        z[INNER:, INNER:] = l2("col_" + n).T
        r[n] = z
    r["wout"] = np.concatenate([l2("w_out").T] * 2, axis=0)
    r["bd"] = np.concatenate([l2("row_bd"), l2("col_bd")])[:, None]
    r["bv"] = np.concatenate([l2("row_bv"), l2("col_bv")])[:, None]
    r["w1T"] = np.concatenate([l3("w1").T] * 4, axis=1)
    wo = np.zeros((4, CB, 4, 27), f)
    for g in range(4):
        for q in range(4):
            ky, kx = 2 * (q // 2) + g // 2, 2 * (q % 2) + g % 2
            if ky < 3 and kx < 3:
                wo[g, :, q, :] = l3("woff")[:, :, ky, kx].T
    r["woff"] = wo.reshape(128, 4 * 27)
    w2 = l3("w2").reshape(CB, CB, 3, 3).transpose(2, 3, 1, 0).reshape(3, 96, CB)
    r["w2T"] = full(w2.transpose(1, 0, 2))
    r["w3T"] = np.roll(full(l3("w3").T), 96, axis=0)
    p = np.arange(128)
    base = np.zeros((128, T, 9, 2), f)
    for t in range(T):
        for k in range(9):
            base[:, t, k, 0] = 4 * t + p // W + k // 3
            base[:, t, k, 1] = p % W + k % 3
    r["base"] = full(base)
    for n in ("qb", "rb", "c1b", "c2b"):
        r[n] = l0(n)[:, None]
    r["gnw"], r["gnb"] = l2("gn_w")[:, None], l2("gn_b")[:, None]
    r["boff"] = full(l3("boff")[:, None])
    for n in (1, 2, 3):
        c = [l3(f"bn{n}_{s}") for s in "gbmv"] + ([l3("dcn_b")] if n == 2 else [])
        a = np.stack(c, axis=1)
        r[f"bn{n}"] = four(a) if a.shape[0] == CB else a
    return np.ascontiguousarray(np.concatenate([np.asarray(r[n], f).reshape(128, k) for n, k in FIELDS], axis=1))


def kernel(**inputs):
    import numpy as np
    import concourse.bacc as bacc
    from concourse.bass_utils import run_bass_kernel_spmd as run

    nc = bacc.Bacc("TRN2", target_bir_lowering=False, num_devices=1)
    ins = {k: np.asarray(a) for k, a in inputs.items()}
    x = np.ascontiguousarray(ins["x"].reshape(B, C, N))
    weights = _columns(ins, np)
    dx = nc.dram_tensor("in_x", x.shape, F32, kind="ExternalInput").ap()
    dw = nc.dram_tensor("in_weights", weights.shape, F32, kind="ExternalInput").ap()
    convs = np.ascontiguousarray(np.concatenate(
        [ins[f"L0_conv_{n}"].transpose(1, 2, 3, 0).reshape(C, -1) for n in ("c1w", "c2w")]
        + [ins[f"L0_conv_{n}"].T for n in ("kw", "vw", "qw")], axis=1))
    dc = nc.dram_tensor("in_convs", convs.shape, F32, kind="ExternalInput").ap()
    table = nc.dram_tensor("quad_table", (QT * QP, 128), F32, kind="Internal").ap()
    do = nc.dram_tensor("out_x", (B, C, N), F32, kind="ExternalOutput").ap()
    build(nc, dx, dw, dc, table, do)
    r = run(nc, [{"in_x": x, "in_weights": weights, "in_convs": convs}], core_ids=[0])
    return r.results[0]["out_x"].reshape(B, C, H, W)
```
